# Optimizing a Trainium2 kernel written in Bass

```python
import numpy as np
import jax
import jax.numpy as jnp

def _softmax(x, axis=-1):
    return jax.nn.softmax(x, axis=axis)

def _gelu(x):
    return jax.nn.gelu(x, approximate=True)

def _silu(x):
    return jax.nn.silu(x)

def _sigmoid(x):
    return jax.nn.sigmoid(x)

def _layernorm(x, axis=-1, eps=1e-05):
    m = jnp.mean(x, axis=axis, keepdims=True)
    v = jnp.var(x, axis=axis, keepdims=True)
    return (x - m) / jnp.sqrt(v + eps)

def _scatter_add(tgt, idx, src, axis=0):
    return tgt.at[idx].add(src)

def _segment_sum(src, seg, n):
    return jax.ops.segment_sum(src, seg, n)
kernel_name = 'mk_decoder_postln_d1_seqx_r4_21fa3b'

def setup_inputs(seed: int=0):
    np.random.seed(seed)
    _w = jnp.asarray

    def _rec_inputs():
        import jax
        import jax.numpy as jnp
        _rk = jax.random.key(seed)
        x = -0.0005207 + 1.001 * jax.random.normal(jax.random.fold_in(_rk, 1), (4, 512, 256), jnp.float32)
        _lenS = 512 - jax.random.randint(jax.random.fold_in(_rk, 7), (4,), 0, max(1, 512 // 4) + 1, jnp.int32)
        _lenS2 = 1024 - jax.random.randint(jax.random.fold_in(_rk, 8), (4,), 0, max(1, 1024 // 4) + 1, jnp.int32)
        _ctx_1024P = jax.random.normal(jax.random.fold_in(_rk, 11), (4, 16, 256), jnp.float32)
        _ctx_1024c = jax.random.dirichlet(jax.random.fold_in(_rk, 511), 0.3 * jnp.ones((16,), jnp.float32), (4, 1024))
        _ctx_1024t = jnp.einsum('bsk,bkd->bsd', _ctx_1024c, _ctx_1024P)
        _ctx_1024t = _ctx_1024t * jax.lax.rsqrt(jnp.mean(jnp.square(_ctx_1024t)) + 1e-12) * 0.953939
        ctx_1024 = -1.52775e-05 + 0.999936 * (_ctx_1024t + 0.3 * jax.random.normal(jax.random.fold_in(_rk, 611), (4, 1024, 256), jnp.float32))
        return (x, ctx_1024)
    x, ctx_1024 = _rec_inputs()

    def _L0_attn_setup():
        import jax, jax.numpy as jnp
        import numpy as np
        DIM = 256
        DIM_HEAD = 64
        HEADS = DIM // DIM_HEAD
        B, N = (2, 512)
        LN_EPS = 1e-05
        RMS_EPS = 1e-08

        def _rmsnorm(x, gamma):
            d = x.shape[-1]
            norm = jnp.linalg.norm(x, axis=-1, keepdims=True) * d ** (-0.5)
            return x / jnp.maximum(norm, RMS_EPS) * gamma

        def _layernorm(x, gamma, beta):
            mu = jnp.mean(x, axis=-1, keepdims=True)
            var = jnp.var(x, axis=-1, keepdims=True)
            return (x - mu) * jax.lax.rsqrt(var + LN_EPS) * gamma + beta
        key = jax.random.key(seed)
        ks = jax.random.split(key, 8)
        s = DIM ** (-0.5)
        return {'x': jax.random.normal(ks[0], (B, N, DIM), dtype=jnp.float32), 'ln_gamma': jnp.ones((DIM,), jnp.float32), 'ln_beta': jnp.zeros((DIM,), jnp.float32), 'q_gamma': jnp.ones((DIM_HEAD,), jnp.float32), 'k_gamma': jnp.ones((DIM_HEAD,), jnp.float32), 'w_q': jax.random.normal(ks[1], (DIM, DIM), jnp.float32) * s, 'w_k': jax.random.normal(ks[2], (DIM, DIM), jnp.float32) * s, 'w_v': jax.random.normal(ks[3], (DIM, DIM), jnp.float32) * s, 'w_o': jax.random.normal(ks[4], (DIM, DIM), jnp.float32) * s, 'b_o': jnp.zeros((DIM,), jnp.float32)}
    _L0_attn_all = _L0_attn_setup()
    _L0_attn_in = {k: v for k, v in _L0_attn_all.items() if k in ('ln_gamma', 'ln_beta', 'q_gamma', 'k_gamma', 'w_q', 'w_k', 'w_v', 'w_o', 'b_o')}
    del _L0_attn_all

    def _L0_xattn_setup():
        import jax, jax.numpy as jnp
        import numpy as np
        DIM = 256
        HEADS = 16
        DHEAD = 64
        INNER = HEADS * DHEAD
        EPS = 1e-05

        def layer_norm(x, g, b):
            mu = jnp.mean(x, axis=-1, keepdims=True)
            var = jnp.mean(jnp.square(x - mu), axis=-1, keepdims=True)
            return (x - mu) * jax.lax.rsqrt(var + EPS) * g + b

        def apply_rope(x, cos, sin):
            d2 = x.shape[-1] // 2
            x1, x2 = (x[..., :d2], x[..., d2:])
            return jnp.concatenate([x1 * cos - x2 * sin, x2 * cos + x1 * sin], axis=-1)
        key = jax.random.key(seed)
        ks = jax.random.split(key, 10)
        B, N, S = (8, 64, 1024)
        latents = jax.random.normal(ks[0], (B, N, DIM), dtype=jnp.float32)
        context = jax.random.normal(ks[1], (B, S, DIM), dtype=jnp.float32)
        cos = jax.random.uniform(ks[2], (S, DHEAD // 2), dtype=jnp.float32)
        sin = jax.random.uniform(ks[3], (S, DHEAD // 2), dtype=jnp.float32)
        init = lambda k, shp, fan_in: jax.random.normal(k, shp, dtype=jnp.float32) / np.sqrt(fan_in)
        return {'latents': latents, 'context': context, 'cos': cos, 'sin': sin, 'ln_lat_g': jnp.ones((DIM,), jnp.float32), 'ln_lat_b': jnp.zeros((DIM,), jnp.float32), 'ln_ctx_g': jnp.ones((DIM,), jnp.float32), 'ln_ctx_b': jnp.zeros((DIM,), jnp.float32), 'Wq': init(ks[4], (DIM, INNER), DIM), 'Wkv': init(ks[5], (DIM, 2 * INNER), DIM), 'Wo': init(ks[6], (INNER, DIM), INNER), 'bo': jnp.zeros((DIM,), jnp.float32)}
    _L0_xattn_all = _L0_xattn_setup()
    _L0_xattn_in = {k: v for k, v in _L0_xattn_all.items() if k in ('cos', 'sin', 'ln_lat_g', 'ln_lat_b', 'ln_ctx_g', 'ln_ctx_b', 'Wq', 'Wkv', 'Wo', 'bo')}
    del _L0_xattn_all

    def _L0_ffn_setup():
        import jax, jax.numpy as jnp
        import numpy as np
        EMB = 256
        HEADS = 16
        SEQ = 512
        LATENT = 128
        N_EXP = 8
        TOP_K = 2
        EXP_DIM = 512
        BATCH = 2
        EPS = 1e-06

        def _rmsnorm(x, g):
            return x * jax.lax.rsqrt(jnp.mean(x * x, axis=-1, keepdims=True) + EPS) * g

        def _mla(h, Wq, Wdkv, Wuk, Wuv, Wo):
            B, S, D = h.shape
            hd = D // HEADS
            q = (h @ Wq).reshape(B, S, HEADS, hd)
            c = h @ Wdkv
            k = (c @ Wuk).reshape(B, S, HEADS, hd)
            v = (c @ Wuv).reshape(B, S, HEADS, hd)
            scores = jnp.einsum('bqhd,bkhd->bhqk', q, k) / jnp.sqrt(jnp.asarray(hd, h.dtype))
            causal = jnp.tril(jnp.ones((S, S), bool))
            scores = jnp.where(causal, scores, jnp.asarray(-1000000000.0, h.dtype))
            a = jax.nn.softmax(scores, axis=-1)
            out = jnp.einsum('bhqk,bkhd->bqhd', a, v).reshape(B, S, D)
            return out @ Wo

        def _moe(h, gate_w, w1, w2):
            B, S, D = h.shape
            t = h.reshape(B * S, D)
            logits = t @ gate_w
            top_v, top_i = jax.lax.top_k(logits, TOP_K)
            gates = jax.nn.softmax(top_v, axis=-1)
            T = t.shape[0]
            combine = jnp.zeros((T, N_EXP), t.dtype).at[jnp.arange(T)[:, None], top_i].add(gates)
            hid = jax.nn.silu(jnp.einsum('td,edh->teh', t, w1))
            ye = jnp.einsum('teh,ehd->ted', hid, w2)
            out = jnp.einsum('te,ted->td', combine, ye)
            return out.reshape(B, S, D)
        key = jax.random.key(seed)
        ks = jax.random.split(key, 12)
        s = 0.02
        return {'x': jax.random.normal(ks[0], (BATCH, SEQ, EMB), jnp.float32), 'g1': jnp.ones((EMB,), jnp.float32), 'Wq': jax.random.normal(ks[1], (EMB, EMB), jnp.float32) * s, 'Wdkv': jax.random.normal(ks[2], (EMB, LATENT), jnp.float32) * s, 'Wuk': jax.random.normal(ks[3], (LATENT, EMB), jnp.float32) * s, 'Wuv': jax.random.normal(ks[4], (LATENT, EMB), jnp.float32) * s, 'Wo': jax.random.normal(ks[5], (EMB, EMB), jnp.float32) * s, 'g2': jnp.ones((EMB,), jnp.float32), 'gate_w': jax.random.normal(ks[6], (EMB, N_EXP), jnp.float32) * s, 'w1': jax.random.normal(ks[7], (N_EXP, EMB, EXP_DIM), jnp.float32) * s, 'w2': jax.random.normal(ks[8], (N_EXP, EXP_DIM, EMB), jnp.float32) * s}
    _L0_ffn_all = _L0_ffn_setup()
    _L0_ffn_in = {k: v for k, v in _L0_ffn_all.items() if k in ('g1', 'Wq', 'Wdkv', 'Wuk', 'Wuv', 'Wo', 'g2', 'gate_w', 'w1', 'w2')}
    del _L0_ffn_all
    return {'x': x, 'ctx_1024': ctx_1024, 'L0_attn_ln_gamma': _L0_attn_in['ln_gamma'], 'L0_attn_ln_beta': _L0_attn_in['ln_beta'], 'L0_attn_q_gamma': _L0_attn_in['q_gamma'], 'L0_attn_k_gamma': _L0_attn_in['k_gamma'], 'L0_attn_w_q': _L0_attn_in['w_q'], 'L0_attn_w_k': _L0_attn_in['w_k'], 'L0_attn_w_v': _L0_attn_in['w_v'], 'L0_attn_w_o': _L0_attn_in['w_o'], 'L0_attn_b_o': _L0_attn_in['b_o'], 'L0_xattn_cos': _L0_xattn_in['cos'], 'L0_xattn_sin': _L0_xattn_in['sin'], 'L0_xattn_ln_lat_g': _L0_xattn_in['ln_lat_g'], 'L0_xattn_ln_lat_b': _L0_xattn_in['ln_lat_b'], 'L0_xattn_ln_ctx_g': _L0_xattn_in['ln_ctx_g'], 'L0_xattn_ln_ctx_b': _L0_xattn_in['ln_ctx_b'], 'L0_xattn_Wq': _L0_xattn_in['Wq'], 'L0_xattn_Wkv': _L0_xattn_in['Wkv'], 'L0_xattn_Wo': _L0_xattn_in['Wo'], 'L0_xattn_bo': _L0_xattn_in['bo'], 'L0_ffn_g1': _L0_ffn_in['g1'], 'L0_ffn_Wq': _L0_ffn_in['Wq'], 'L0_ffn_Wdkv': _L0_ffn_in['Wdkv'], 'L0_ffn_Wuk': _L0_ffn_in['Wuk'], 'L0_ffn_Wuv': _L0_ffn_in['Wuv'], 'L0_ffn_Wo': _L0_ffn_in['Wo'], 'L0_ffn_g2': _L0_ffn_in['g2'], 'L0_ffn_gate_w': _L0_ffn_in['gate_w'], 'L0_ffn_w1': _L0_ffn_in['w1'], 'L0_ffn_w2': _L0_ffn_in['w2']}

def reference(x, ctx_1024, L0_attn_ln_gamma, L0_attn_ln_beta, L0_attn_q_gamma, L0_attn_k_gamma, L0_attn_w_q, L0_attn_w_k, L0_attn_w_v, L0_attn_w_o, L0_attn_b_o, L0_xattn_cos, L0_xattn_sin, L0_xattn_ln_lat_g, L0_xattn_ln_lat_b, L0_xattn_ln_ctx_g, L0_xattn_ln_ctx_b, L0_xattn_Wq, L0_xattn_Wkv, L0_xattn_Wo, L0_xattn_bo, L0_ffn_g1, L0_ffn_Wq, L0_ffn_Wdkv, L0_ffn_Wuk, L0_ffn_Wuv, L0_ffn_Wo, L0_ffn_g2, L0_ffn_gate_w, L0_ffn_w1, L0_ffn_w2):
    import jax
    import jax.numpy as jnp

    def _L0_attn_ref(x, ln_gamma, ln_beta, q_gamma, k_gamma, w_q, w_k, w_v, w_o, b_o):
        import jax, jax.numpy as jnp
        import numpy as np
        DIM = 256
        DIM_HEAD = 64
        HEADS = DIM // DIM_HEAD
        B, N = (2, 512)
        LN_EPS = 1e-05
        RMS_EPS = 1e-08

        def _rmsnorm(x, gamma):
            d = x.shape[-1]
            norm = jnp.linalg.norm(x, axis=-1, keepdims=True) * d ** (-0.5)
            return x / jnp.maximum(norm, RMS_EPS) * gamma

        def _layernorm(x, gamma, beta):
            mu = jnp.mean(x, axis=-1, keepdims=True)
            var = jnp.var(x, axis=-1, keepdims=True)
            return (x - mu) * jax.lax.rsqrt(var + LN_EPS) * gamma + beta
        h, dh = (HEADS, DIM_HEAD)
        xn = _layernorm(x, ln_gamma, ln_beta)

        def proj(w):
            y = xn @ w.T
            b, n, _ = y.shape
            return y.reshape(b, n, h, dh).transpose(0, 2, 1, 3)
        q = proj(w_q)
        k = proj(w_k)
        v = proj(w_v)
        qn = _rmsnorm(q, q_gamma) * dh ** (-0.5)
        kn = _rmsnorm(k, k_gamma)
        sim = jnp.einsum('bhid,bhjd->bhij', qn, kn)
        attn = jax.nn.softmax(sim, axis=-1)
        out = jnp.einsum('bhij,bhjd->bhid', attn, v)
        b, _, n, _ = out.shape
        out = out.transpose(0, 2, 1, 3).reshape(b, n, h * dh)
        return out @ w_o.T + b_o

    def _L0_xattn_ref(latents, context, cos, sin, ln_lat_g, ln_lat_b, ln_ctx_g, ln_ctx_b, Wq, Wkv, Wo, bo):
        import jax, jax.numpy as jnp
        import numpy as np
        DIM = 256
        HEADS = 16
        DHEAD = 64
        INNER = HEADS * DHEAD
        EPS = 1e-05

        def layer_norm(x, g, b):
            mu = jnp.mean(x, axis=-1, keepdims=True)
            var = jnp.mean(jnp.square(x - mu), axis=-1, keepdims=True)
            return (x - mu) * jax.lax.rsqrt(var + EPS) * g + b

        def apply_rope(x, cos, sin):
            d2 = x.shape[-1] // 2
            x1, x2 = (x[..., :d2], x[..., d2:])
            return jnp.concatenate([x1 * cos - x2 * sin, x2 * cos + x1 * sin], axis=-1)
        b, n, _ = latents.shape
        s = context.shape[1]
        lat = layer_norm(latents, ln_lat_g, ln_lat_b)
        ctx = layer_norm(context, ln_ctx_g, ln_ctx_b)
        q = (lat @ Wq).reshape(b, n, HEADS, DHEAD).transpose(0, 2, 1, 3)
        kv = ctx @ Wkv
        k, v = jnp.split(kv, 2, axis=-1)
        k = k.reshape(b, s, HEADS, DHEAD).transpose(0, 2, 1, 3)
        v = v.reshape(b, s, HEADS, DHEAD).transpose(0, 2, 1, 3)
        k = apply_rope(k, cos[None, None], sin[None, None])
        scale = DHEAD ** (-0.5)
        attn = jnp.einsum('bhnd,bhsd->bhns', q, k) * scale
        attn = jnp.clip(attn, -11.0, 11.0)
        attn = jax.nn.softmax(attn, axis=-1)
        out = jnp.einsum('bhns,bhsd->bhnd', attn, v)
        out = out.transpose(0, 2, 1, 3).reshape(b, n, INNER)
        return out @ Wo + bo

    def _L0_ffn_ref(x, g1, Wq, Wdkv, Wuk, Wuv, Wo, g2, gate_w, w1, w2):
        import jax, jax.numpy as jnp
        import numpy as np
        EMB = 256
        HEADS = 16
        SEQ = 512
        LATENT = 128
        N_EXP = 8
        TOP_K = 2
        EXP_DIM = 512
        BATCH = 2
        EPS = 1e-06

        def _rmsnorm(x, g):
            return x * jax.lax.rsqrt(jnp.mean(x * x, axis=-1, keepdims=True) + EPS) * g

        def _mla(h, Wq, Wdkv, Wuk, Wuv, Wo):
            B, S, D = h.shape
            hd = D // HEADS
            q = (h @ Wq).reshape(B, S, HEADS, hd)
            c = h @ Wdkv
            k = (c @ Wuk).reshape(B, S, HEADS, hd)
            v = (c @ Wuv).reshape(B, S, HEADS, hd)
            scores = jnp.einsum('bqhd,bkhd->bhqk', q, k) / jnp.sqrt(jnp.asarray(hd, h.dtype))
            causal = jnp.tril(jnp.ones((S, S), bool))
            scores = jnp.where(causal, scores, jnp.asarray(-1000000000.0, h.dtype))
            a = jax.nn.softmax(scores, axis=-1)
            out = jnp.einsum('bhqk,bkhd->bqhd', a, v).reshape(B, S, D)
            return out @ Wo

        def _moe(h, gate_w, w1, w2):
            B, S, D = h.shape
            t = h.reshape(B * S, D)
            logits = t @ gate_w
            top_v, top_i = jax.lax.top_k(logits, TOP_K)
            gates = jax.nn.softmax(top_v, axis=-1)
            T = t.shape[0]
            combine = jnp.zeros((T, N_EXP), t.dtype).at[jnp.arange(T)[:, None], top_i].add(gates)
            hid = jax.nn.silu(jnp.einsum('td,edh->teh', t, w1))
            ye = jnp.einsum('teh,ehd->ted', hid, w2)
            out = jnp.einsum('te,ted->td', combine, ye)
            return out.reshape(B, S, D)
        x = x + _mla(_rmsnorm(x, g1), Wq, Wdkv, Wuk, Wuv, Wo)
        x = x + _moe(_rmsnorm(x, g2), gate_w, w1, w2)
        return x
    x = _layernorm(x + _L0_attn_ref(x, L0_attn_ln_gamma, L0_attn_ln_beta, L0_attn_q_gamma, L0_attn_k_gamma, L0_attn_w_q, L0_attn_w_k, L0_attn_w_v, L0_attn_w_o, L0_attn_b_o), axis=-1)
    x = _layernorm(x + _L0_xattn_ref(x, ctx_1024, L0_xattn_cos, L0_xattn_sin, L0_xattn_ln_lat_g, L0_xattn_ln_lat_b, L0_xattn_ln_ctx_g, L0_xattn_ln_ctx_b, L0_xattn_Wq, L0_xattn_Wkv, L0_xattn_Wo, L0_xattn_bo), axis=-1)
    x = _layernorm(x + _L0_ffn_ref(x, L0_ffn_g1, L0_ffn_Wq, L0_ffn_Wdkv, L0_ffn_Wuk, L0_ffn_Wuv, L0_ffn_Wo, L0_ffn_g2, L0_ffn_gate_w, L0_ffn_w1, L0_ffn_w2), axis=-1)
    return x

_drawn_inputs = setup_inputs


def setup_inputs(seed=0):
    import zlib

    import numpy as np

    out = dict(_drawn_inputs(seed))
    spreads = {'L0_attn_ln_gamma': (1.0, 0.2),
     'L0_attn_ln_beta': (0.0, 0.1),
     'L0_attn_q_gamma': (1.0, 0.6),
     'L0_attn_k_gamma': (1.0, 0.6),
     'L0_attn_b_o': (0.0, 0.1),
     'L0_xattn_ln_lat_g': (1.0, 0.6),
     'L0_xattn_ln_lat_b': (0.0, 0.628),
     'L0_xattn_ln_ctx_g': (1.0, 0.2),
     'L0_xattn_ln_ctx_b': (0.0, 0.1),
     'L0_xattn_bo': (0.0, 0.1),
     'L0_ffn_g1': (1.0, 0.6),
     'L0_ffn_g2': (1.0, 0.6)}
    factors = {'L0_xattn_cos': 5.55,
     'L0_xattn_sin': 5.538,
     'L0_ffn_Wq': 8.0,
     'L0_ffn_Wdkv': 8.0,
     'L0_ffn_Wuk': 8.0,
     'L0_ffn_Wuv': 8.0,
     'L0_ffn_Wo': 8.0,
     'L0_ffn_gate_w': 8.0,
     'L0_ffn_w1': 8.0,
     'L0_ffn_w2': 8.0}
    for name, (base, spread) in spreads.items():
        noise = np.random.default_rng([zlib.crc32(name.encode()), seed]).standard_normal(out[name].shape)
        drawn = base * np.exp(spread * noise) if base else spread * noise
        out[name] = jnp.asarray(drawn.astype(out[name].dtype))
    for name, factor in factors.items():
        out[name] = (out[name] * factor).astype(out[name].dtype)
    return out
```

```python
from contextlib import ExitStack

import numpy as np
import concourse.bass as bass
from concourse import mybir

ALU = mybir.AluOpType
ACT = mybir.ActivationFunctionType
AX = mybir.AxisListType
F32 = mybir.dt.float32
F32R = mybir.dt.float32r
I32 = mybir.dt.int32
BF16 = mybir.dt.bfloat16

P = 128
B, S, D = 4, 512, 256
KD = D // P
TB = S // P
NT = B * TB
UP = 1
RSQRT_MAGIC = 0x5F3759DF


def as32(ap):
    return ap.bitcast(F32)


class Chain:

    def __init__(self, eng, sem):
        self.eng, self.sem, self.n, self.base = eng, sem, 0, 0

    def start(self, base):
        self.n, self.base = 0, base

    def step(self, ins):
        self.n += 1
        ins.then_inc(self.sem, 1)
        self.eng.wait_ge(self.sem, UP + self.base + self.n)


def newton_rsqrt(nc, ch, y, v, t, c_magic):
    ch.step(nc.vector.tensor_scalar(t.bitcast(I32), v.bitcast(I32), 1, None, ALU.arith_shift_right))
    ch.step(nc.vector.tensor_scalar(y.bitcast(I32), t.bitcast(I32), -1.0, float(RSQRT_MAGIC), ALU.mult, ALU.add))
    for _ in range(4):
        ch.step(nc.vector.tensor_tensor(t, y, y, ALU.mult))
        ch.step(nc.vector.scalar_tensor_tensor(t, t, -0.5, v, ALU.mult, ALU.mult))
        ch.step(nc.vector.scalar_tensor_tensor(y, t, 1.5, y, ALU.add, ALU.mult))


RSQRT_STEPS = 2 + 3 * 4


class Semaphores:

    def __init__(self, nc, ctx, names):
        self.of = {n: ctx.enter_context(nc.semaphore(n)) for n in names}

    def raise_all(self, eng):
        for s in self.of.values():
            eng.sem_inc(s, UP)


class Scope:

    def __init__(self, nc, ctx, tag, sems):
        self.nc, self.ctx, self.tag, self.sems = nc, ctx, tag, sems

    def sb(self, name, shape, dt=F32):
        return self.ctx.enter_context(self.nc.sbuf_tensor(f"{self.tag}_{name}", shape, dt))

    def ps(self, name, shape, dt=F32):
        return self.ctx.enter_context(self.nc.psum_tensor(f"{self.tag}_{name}", shape, dt))

    def sem(self, name):
        return self.sems.of[f"{self.tag}_{name}"]

    def dma_sem(self, name):
        return self.ctx.enter_context(self.nc.semaphore(f"{self.tag}_{name}"))


def tile_of(x, t, n=1):
    return x[:, bass.ds(t, n), :]


def flat(ap):
    return ap.rearrange("p a n -> p (a n)")


def row_stats(nc, ch, tiles, st, mv, tmp):
    nc.vector.memset(tmp[:, 0:1], 0.0)
    for i, x in enumerate(tiles):
        last = nc.vector.bn_stats(st[:, i, :], x)
    ch.step(last)
    nc.vector.memset(tmp[:, 0:1], 0.0)
    for i, _ in enumerate(tiles):
        last = nc.vector.bn_aggr(mv[:, i, :], st[:, i, :])
    ch.step(last)


def layer_norm_stats(nc, ch, tiles, st, mv, rstd, tmp, eps):
    row_stats(nc, ch, tiles, st, mv, tmp)
    ch.step(nc.vector.tensor_scalar_add(mv[:, 0:len(tiles), 1], mv[:, 0:len(tiles), 1], eps))
    newton_rsqrt(nc, ch, rstd[:, 0:len(tiles)], mv[:, 0:len(tiles), 1], tmp[:, 0:len(tiles)], None)


LN_STEPS = 3 + RSQRT_STEPS


AH, AD = 4, 64
AG = 2 * AH
SA_SEMS = ("split_done", "dve_steps", "xn_ready", "xs_ready", "tp_full", "tp_free_act", "tp_free_dve", "qkv_full",
           "qkv_free", "stacked", "s_full", "max_ready", "exp_ready", "norm_ready", "av_done", "o_free", "y_full")


def self_attention(nc, sems, X, ident, x_dram, ln_g, ln_b, q_g, k_g, wqT, wkT, wvT, woT, b_o):
    with ExitStack() as ctx:
        sc = Scope(nc, ctx, "sa", sems)
        w_st = sc.sb("w_st", [P, KD, 3 * D])
        w_hi = sc.sb("w_hi", [P, KD, 3 * D], F32R)
        w_lo = sc.sb("w_lo", [P, KD, 3 * D], F32R)
        wo = sc.sb("wo", [P, KD, D])
        g_in = sc.sb("g_in", [P, KD])
        b_in = sc.sb("b_in", [P, KD])
        gam = sc.sb("gam", [P, AG, AD])
        bo = sc.sb("bo", [P, D])
        st = sc.sb("st", [P, TB, 6])
        mv = sc.sb("mv", [P, TB, 2])
        rstd = sc.sb("rstd", [P, TB])
        tmp = sc.sb("tmp", [P, TB * AG])
        xn = sc.sb("xn", [P, TB, D])
        xT = sc.sb("xT", [P, KD, S])
        xh = sc.sb("xh", [P, KD, S], F32R)
        xl = sc.sb("xl", [P, KD, S], F32R)
        qk = sc.sb("qk", [P, TB, AG * AD])
        sq = sc.sb("sq", [P, TB, AG * AD])
        ss = sc.sb("ss", [P, TB * AG])
        rn = sc.sb("rn", [P, TB * AG])
        v = sc.sb("v", [P, TB, D])
        stk = sc.sb("stk", [P, TB, 3 * AH, P])
        stT = sc.sb("stT", [P, 3 * AH, S], F32R)
        nmx = sc.sb("nmx", [P, AH * TB])
        rs = sc.sb("rs", [P, AH * TB])
        ri = sc.sb("ri", [P, AH * TB])
        prob = sc.sb("prob", [P, 8, S])
        pT = sc.sb("pT", [P, 2, TB, S])
        oT = sc.sb("oT", [P, KD, S])
        p_tp = sc.ps("p_tp", [P, 2, S])
        p_s = sc.ps("p_s", [P, 2, S])
        p_qk = sc.ps("p_qk", [P, S])
        p_v = sc.ps("p_v", [P, S])
        p_o = sc.ps("p_o", [P, S])
        p_y = sc.ps("p_y", [P, S])

        loaded, x_loaded = sc.dma_sem("loaded"), sc.dma_sem("x_loaded")
        split_done = sc.sem("split_done")
        dve_steps = sc.sem("dve_steps")
        xn_ready, xs_ready = sc.sem("xn_ready"), sc.sem("xs_ready")
        tp_full, tp_free_act, tp_free_dve = sc.sem("tp_full"), sc.sem("tp_free_act"), sc.sem("tp_free_dve")
        qkv_full, qkv_free = sc.sem("qkv_full"), sc.sem("qkv_free")
        stacked = sc.sem("stacked")
        s_full, max_ready, exp_ready, norm_ready = (sc.sem(n) for n in ("s_full", "max_ready", "exp_ready", "norm_ready"))
        av_done, o_free = sc.sem("av_done"), sc.sem("o_free")
        y_full = sc.sem("y_full")

        N_ST = 3 * AH
        T2, T3 = KD, KD + N_ST
        FILLS = KD + N_ST + AH * TB
        HALF = FILLS // 2
        UN = AH * TB
        assert FILLS % 2 == 0
        STEPS = 2 * LN_STEPS + RSQRT_STEPS + TB + UN + 10

        block = ctx.enter_context(nc.Block())

        @block.sync
        def _(sp):
            sp.dma_start(X[:, 0:NT, :], x_dram.rearrange("b (i p) d -> p (b i) d", p=P)).then_inc(x_loaded, 16)
            for n, w in enumerate((wqT, wkT, wvT)):
                sp.dma_start(w_st[:, :, n * D:(n + 1) * D], w.rearrange("(k p) n -> p k n", p=P)).then_inc(loaded, 16)
            sp.dma_start(wo[:, :, :], woT.rearrange("(k p) n -> p k n", p=P)).then_inc(loaded, 16)
            with nc.allow_non_contiguous_dma("small vectors"):
                sp.dma_start(g_in[:, :], ln_g.rearrange("(k p) -> p k", p=P)).then_inc(loaded, 16)
                sp.dma_start(b_in[:, :], ln_b.rearrange("(k p) -> p k", p=P)).then_inc(loaded, 16)
            for h in range(AG):
                g = q_g if h < AH else k_g
                sp.dma_start(gam[:, h, :], g.unsqueeze(0).broadcast_to([P, AD])).then_inc(loaded, 16)
            sp.dma_start(bo[:, :], b_o.unsqueeze(0).broadcast_to([P, D])).then_inc(loaded, 16)
        LOADS = 16 * (7 + AG)

        @block.gpsimd
        def _(pool):
            pass

        @block.tensor
        def _(pe):
            def fill(b, n):
                free = tp_free_dve if n % 2 else tp_free_act
                pe.wait_ge(free, UP + b * HALF + n // 2)
                return p_tp[:, n % 2, :]

            pe.wait_ge(split_done, UP + 1)
            with pe.Fori(0, B) as b:
                pe.wait_ge(xn_ready, UP + b + 1)
                for k in range(KD):
                    bank = fill(b, k)
                    for i in range(TB):
                        last = nc.tensor.transpose(bank[:, i * P:(i + 1) * P], xn[:, i, k * P:(k + 1) * P], ident[:, :])
                    last.then_inc(tp_full, 1)
                pe.wait_ge(xs_ready, UP + b + 1)
                for i in range(TB):
                    pe.wait_ge(qkv_free, UP + b * TB + i)
                    for out, c0, n in ((p_qk, 0, 2 * D), (p_v, 2 * D, D)):
                        steps = [(x, w, k) for x, w in ((xh, w_hi), (xh, w_lo), (xl, w_hi)) for k in range(KD)]
                        for j, (x, w, k) in enumerate(steps):
                            last = nc.tensor.matmul(out[:, 0:n], x[:, k, i * P:(i + 1) * P], w[:, k, c0:c0 + n],
                                                    start=(j == 0), stop=(j == len(steps) - 1))
                    last.then_inc(qkv_full, 1)
                pe.wait_ge(stacked, UP + b + 1)
                for m in range(N_ST):
                    bank = fill(b, T2 + m)
                    for i in range(TB):
                        last = nc.tensor.transpose(bank[:, i * P:(i + 1) * P], stk[:, i, m, :], ident[:, :])
                    last.then_inc(tp_full, 1)
                pe.wait_ge(tp_free_act, UP + b * HALF + T3 // 2)
                pe.wait_ge(tp_free_dve, UP + b * HALF + T3 // 2)

                def scores(u):
                    h, i = divmod(u, TB)
                    if u >= 2:
                        pe.wait_ge(exp_ready, UP + b * UN + u - 1)
                    nc.tensor.matmul(p_s[:, u % 2, :], stT[:, AH + h, i * P:(i + 1) * P], stT[:, h, :], start=True, stop=False)
                    nc.tensor.matmul(p_s[:, u % 2, :], stT[:, 2 * AH + h, i * P:(i + 1) * P], stT[:, h, :],
                                     start=False, stop=True).then_inc(s_full, 1)

                def turn(h):
                    pe.wait_ge(norm_ready, UP + b * UN + (h + 1) * TB)
                    for j in range(TB):
                        bank = fill(b, T3 + h * TB + j)
                        for i in range(TB):
                            last = nc.tensor.transpose(bank[:, i * P:(i + 1) * P],
                                                       prob[:, (h * TB + i) % 8, j * P:(j + 1) * P], ident[:, :])
                        last.then_inc(tp_full, 1)

                def values(h):
                    n = (T3 + (h + 1) * TB) // 2
                    pe.wait_ge(tp_free_act, UP + b * HALF + n)
                    pe.wait_ge(tp_free_dve, UP + b * HALF + n)
                    if h % 2 == 0:
                        pe.wait_ge(o_free, UP + b * KD + h // 2)
                    r = (h % 2) * AD
                    for j in range(TB):
                        last = nc.tensor.matmul(p_o[r:r + AD, :], v[:, j, h * AD:(h + 1) * AD], pT[:, h % 2, j, :],
                                                start=(j == 0), stop=(j == TB - 1))
                    last.then_inc(av_done, 1)

                for u in range(UN + 3):
                    if u < UN:
                        scores(u)
                    if u >= 5 and (u - 5) % TB == 0:
                        turn((u - 5) // TB)
                    if u >= 6 and (u - 6) % TB == 0:
                        values((u - 6) // TB)
                pe.wait_ge(o_free, UP + b * KD + KD)
                for i in range(TB):
                    bank = (p_y, p_qk)[i // 2]
                    c = (i % 2) * D
                    for k in range(KD):
                        last = nc.tensor.matmul(bank[:, c:c + D], oT[:, k, i * P:(i + 1) * P], wo[:, k, :],
                                                start=(k == 0), stop=(k == KD - 1))
                    last.then_inc(y_full, 1)

        @block.scalar
        def _(act):
            act.wait_ge(loaded, LOADS)
            with act.Fori(0, B) as b:
                act.wait_ge(tp_full, UP + b * FILLS + 1)
                nc.scalar.activation(xT[:, 0, :], p_tp[:, 0, :], ACT.Identity, bias=b_in[:, 0:1], scale=g_in[:, 0:1]).then_inc(tp_free_act, 1)
                for i in range(TB):
                    act.wait_ge(qkv_full, UP + b * TB + i + 1)
                    nc.scalar.activation(qk[:, i, :], p_qk[:, :], ACT.Copy)
                    nc.scalar.activation(v[:, i, :], p_v[:, 0:D], ACT.Copy).then_inc(qkv_free, 1)
                for n in range(T2, T3, 2):
                    act.wait_ge(tp_full, UP + b * FILLS + n + 1)
                    nc.scalar.activation(stT[:, n - T2, :], p_tp[:, 0, :], ACT.Copy).then_inc(tp_free_act, 1)

                def turned(h):
                    for j in range(0, TB, 2):
                        act.wait_ge(tp_full, UP + b * FILLS + T3 + h * TB + j + 1)
                        act.wait_ge(av_done, UP + b * AH + max(h - 1, 0))
                        nc.scalar.activation(pT[:, h % 2, j, :], p_tp[:, 0, :], ACT.Copy).then_inc(tp_free_act, 1)

                def pair_out(k):
                    act.wait_ge(av_done, UP + b * AH + 2 * k + 2)
                    nc.scalar.activation(oT[:, k, :], p_o[:, :], ACT.Copy).then_inc(o_free, 1)

                for u in range(UN + 3):
                    if u < UN:
                        act.wait_ge(max_ready, UP + b * UN + u + 1)
                        if u >= 8:
                            act.wait_ge(tp_full, UP + b * FILLS + T3 + (u // TB - 1) * TB)
                        nc.scalar.activation(prob[:, u % 8, :], p_s[:, u % 2, :], ACT.Exp, bias=nmx[:, u:u + 1],
                                             accum_out=rs[:, u:u + 1]).then_inc(exp_ready, 1)
                    if u >= 5 and (u - 5) % TB == 0:
                        turned((u - 5) // TB)
                    if u >= 7 and (u - 7) % (2 * TB) == TB:
                        pair_out((u - 7) // (2 * TB))
                pair_out(AH // 2 - 1)

        @block.vector
        def _(dve):
            ch = Chain(dve, dve_steps)
            dve.wait_ge(loaded, LOADS)
            dve.wait_ge(x_loaded, 16)
            ch.step(nc.vector.tensor_copy(w_hi[:, :, :], w_st[:, :, :]))
            ch.step(nc.vector.tensor_scalar(gam[:, 0:AH, :], gam[:, 0:AH, :], AD ** -0.5, None, ALU.mult))
            nc.vector.tensor_tensor(w_lo[:, :, :], w_st[:, :, :], as32(w_hi[:, :, :]), ALU.subtract).then_inc(split_done, 1)
            START = 2
            with dve.Fori(0, B) as b:
                ch.start(b * STEPS + START)
                layer_norm_stats(nc, ch, [flat(tile_of(X, b * TB + i)) for i in range(TB)], st, mv, rstd, tmp, 1e-5)
                for i in range(TB):
                    last = nc.vector.tensor_scalar(xn[:, i, :], flat(tile_of(X, b * TB + i)), mv[:, i, 0:1], rstd[:, i:i + 1],
                                                   ALU.subtract, ALU.mult)
                last.then_inc(xn_ready, 1)
                dve.wait_ge(tp_full, UP + b * FILLS + 2)
                nc.vector.tensor_scalar(xT[:, 1, :], p_tp[:, 1, :], g_in[:, 1:2], b_in[:, 1:2], ALU.mult, ALU.add).then_inc(tp_free_dve, 1)
                dve.wait_ge(tp_free_act, UP + b * HALF + 1)
                dve.wait_ge(tp_free_dve, UP + b * HALF + 1)
                ch.step(nc.vector.tensor_copy(xh[:, :, :], xT[:, :, :]))
                nc.vector.tensor_tensor(xl[:, :, :], xT[:, :, :], as32(xh[:, :, :]), ALU.subtract).then_inc(xs_ready, 1)
                for i in range(TB):
                    dve.wait_ge(qkv_free, UP + b * TB + i + 1)
                    ch.step(nc.vector.tensor_tensor(sq[:, i, :], qk[:, i, :], qk[:, i, :], ALU.mult))
                    last = nc.vector.reduce_sum(ss[:, i * AG:(i + 1) * AG], sq[:, i, :].rearrange("p (g d) -> p g d", d=AD), AX.X)
                ch.step(last)
                ch.step(nc.vector.tensor_scalar(ss[:, :], ss[:, :], 1.0 / AD, 1e-16, ALU.mult, ALU.max))
                newton_rsqrt(nc, ch, rn[:, :], ss[:, :], tmp[:, :], None)
                heads = qk[:, :, :].rearrange("p i (g d) -> p (i g) d", d=AD)
                ch.step(nc.vector.tensor_tensor(heads, heads, rn[:, :].unsqueeze(2).broadcast_to([P, TB * AG, AD]), ALU.mult))
                ch.step(nc.vector.tensor_tensor(qk[:, :, :], qk[:, :, :],
                                                gam[:, :, :].rearrange("p g d -> p (g d)").unsqueeze(1).broadcast_to([P, TB, AG * AD]), ALU.mult))
                q4 = qk[:, :, 0:AH * AD].rearrange("p i (h d) -> p i h d", d=AD)
                k4 = qk[:, :, AH * AD:2 * AH * AD].rearrange("p i (h d) -> p i h d", d=AD)
                kh, kl = stk[:, :, 0:AH, 0:AD], stk[:, :, 0:AH, AD:P]
                qh, qh2 = stk[:, :, AH:2 * AH, 0:AD], stk[:, :, AH:2 * AH, AD:P]
                ql, ql2 = stk[:, :, 2 * AH:3 * AH, 0:AD], stk[:, :, 2 * AH:3 * AH, AD:P]
                nc.vector.tensor_copy(kh.bitcast(F32R), k4)
                ch.step(nc.vector.tensor_copy(qh.bitcast(F32R), q4))
                nc.vector.tensor_tensor(kl, k4, kh, ALU.subtract)
                ch.step(nc.vector.tensor_tensor(ql, q4, qh, ALU.subtract))
                nc.vector.tensor_copy(qh2, qh)
                nc.vector.tensor_copy(ql2, ql).then_inc(stacked, 1)
                for n in range(T2 + 1, T3, 2):
                    dve.wait_ge(tp_full, UP + b * FILLS + n + 1)
                    nc.vector.tensor_copy(stT[:, n - T2, :], p_tp[:, 1, :]).then_inc(tp_free_dve, 1)

                def norm(u):
                    dve.wait_ge(exp_ready, UP + b * UN + u + 1)
                    ch.step(nc.vector.reciprocal(ri[:, u:u + 1], rs[:, u:u + 1]))
                    nc.vector.tensor_scalar(prob[:, u % 8, :], prob[:, u % 8, :], ri[:, u:u + 1], None, ALU.mult).then_inc(norm_ready, 1)

                def turned(h):
                    for j in range(1, TB, 2):
                        dve.wait_ge(tp_full, UP + b * FILLS + T3 + h * TB + j + 1)
                        dve.wait_ge(av_done, UP + b * AH + max(h - 1, 0))
                        nc.vector.tensor_copy(pT[:, h % 2, j, :], p_tp[:, 1, :]).then_inc(tp_free_dve, 1)

                for u in range(UN + 3):
                    if u < UN:
                        dve.wait_ge(s_full, UP + b * UN + u + 1)
                        nc.vector.tensor_reduce(nmx[:, u:u + 1], p_s[:, u % 2, :], AX.X, ALU.max, negate=True).then_inc(max_ready, 1)
                    if 1 <= u <= UN:
                        norm(u - 1)
                    if u >= 5 and (u - 5) % TB == 0:
                        turned((u - 5) // TB)
                for i in range(TB):
                    dve.wait_ge(y_full, UP + b * TB + i // 2 * 2 + 2)
                    xi = flat(tile_of(X, b * TB + i))
                    bank = (p_y, p_qk)[i // 2]
                    c = (i % 2) * D
                    last = nc.vector.tensor_tensor(xi, bank[:, c:c + D], xi, ALU.add)
                ch.step(last)
                xs = tile_of(X, b * TB, TB)
                ch.step(nc.vector.tensor_tensor(xs, xs, bo[:, :].unsqueeze(1).broadcast_to([P, TB, D]), ALU.add))
                layer_norm_stats(nc, ch, [flat(tile_of(X, b * TB + i)) for i in range(TB)], st, mv, rstd, tmp, 1e-5)
                for i in range(TB):
                    xi = flat(tile_of(X, b * TB + i))
                    last = nc.vector.tensor_scalar(xi, xi, mv[:, i, 0:1], rstd[:, i:i + 1], ALU.subtract, ALU.mult)
                ch.step(last)
                assert ch.n == STEPS, (ch.n, STEPS)


XH, XD = 16, 64
XP = XH // 2
SC = 1024
CT = SC // P
HC = CT // 2
PC = 2 * HC
CLIP = 11.0


XA_SEMS = ("cx_used", "w_split", "dve_steps", "normed", "xs_ready", "bg_full", "bg_act", "bg_dve", "rot_ready",
           "kr_ready", "khi_ready", "stk_ready", "pool_steps", "s_full", "exp_ready", "clipped", "added",
           "esum_ready", "sum_full", "sum_used", "av_done", "o_out", "oT_ready", "y_full")
XA_DMA_SEMS = ("w_loaded", "c_loaded", "cx_loaded")


def cross_attention(nc, sems, X, ident, ctx_dram, cos, sin, lat_g, lat_b, ctx_g, ctx_b, w_q, w_kv, w_o, b_o):
    with ExitStack() as ctx:
        sc = Scope(nc, ctx, "xa", sems)
        wq = sc.sb("wq", [P, 2, KD, XH * XD], F32R)
        wqd = sc.sb("wqd", [P, 2, 2 * KD, P], F32R)
        wkv_hi = sc.sb("wkv_hi", [P, KD, XP, 2 * P], F32R)
        wkv_lo = sc.sb("wkv_lo", [P, KD, XP, 2 * P], F32R)
        wo = sc.sb("wo", [P, XP, D])
        g_in = sc.sb("g_in", [P, 2, KD])
        b_in = sc.sb("b_in", [P, 2, KD])
        bo = sc.sb("bo", [P, D])
        c2 = sc.sb("c2", [P, CT, XD])
        s2 = sc.sb("s2", [P, CT, XD])
        ones = sc.sb("ones", [P, XD])
        cx = sc.sb("cx", [P, CT, D])
        NL = CT + TB
        st = sc.sb("st", [P, NL, 6])
        mv = sc.sb("mv", [P, NL, 2])
        rstd = sc.sb("rstd", [P, NL])
        tmp = sc.sb("tmp", [P, NL])
        cT_hi = sc.sb("cT_hi", [P, KD, SC], F32R)
        cT_lo = sc.sb("cT_lo", [P, KD, SC], F32R)
        lT_hi = sc.sb("lT_hi", [P, KD, S], F32R)
        lT_lo = sc.sb("lT_lo", [P, KD, S], F32R)
        kv = sc.sb("kv", [P, 2, CT, 2 * P])
        t1 = sc.sb("t1", [P, 4, 2, XD])
        t2 = sc.sb("t2", [P, 4, 2, XD])
        stk = sc.sb("stk", [P, 2, CT, 2, P])
        kT = sc.sb("kT", [P, 2, SC], F32R)
        qT = sc.sb("qT", [P, 2, 2, S], F32R)
        ex = sc.sb("ex", [P, 4, 2, S])
        acc = sc.sb("acc", [P, 2, S])
        esum = sc.sb("esum", [P, S])
        rcp = sc.sb("rcp", [P, S])
        oT = sc.sb("oT", [P, XP, S])
        ex_flat = ex[:, :, :, :].rearrange("p a b n -> p (a b n)")
        cT = ex_flat[:, 0:KD * SC].rearrange("p (k n) -> p k n", k=KD)
        lT = ex_flat[:, KD * SC:KD * SC + KD * S].rearrange("p (k n) -> p k n", k=KD)
        oT_flat = oT[:, :, :].rearrange("p a n -> p (a n)")
        ln = oT_flat[:, 0:TB * D].rearrange("p (i d) -> p i d", d=D)
        wkv_st = oT_flat.rearrange("p (k a n) -> p k a n", k=KD, a=XP)
        wq_st = ex_flat[:, 0:KD * XH * XD].rearrange("p (k n) -> p k n", k=KD)

        p_s = sc.ps("p_s", [P, 2, 2, S])
        p_o = sc.ps("p_o", [P, S])
        p_sum = sc.ps("p_sum", [P, S])
        p_bg = sc.ps("p_bg", [P, 2, S])

        m = {n: sc.sem(n) for n in XA_SEMS} | {n: sc.dma_sem(n) for n in XA_DMA_SEMS}
        wqd_loaded = [sc.dma_sem(f"wqd_loaded{i}") for i in range(2)]

        order = [("T", i) for i in range(6)]
        order += [("KV", 0, i) for i in range(4)] + [("Q", 0), ("KT", 0, 0), ("KT", 0, 1)]
        slot_fills = {}
        for p in range(XP):
            a, h, nx = p * PC, 2 * p + 1, p + 1
            slot_fills[a] = [("KT", h, 0)]
            slot_fills[a + 1] = [("KT", h, 1)]
            slot_fills[a + 2] = [("Q", h)]
            if nx < XP:
                slot_fills[a + 1] += [("KV", nx, 0)]
                slot_fills[a + 2] += [("KV", nx, 1)]
                slot_fills[a + 3] = [("KV", nx, 2)]
                slot_fills[a + 4] = [("KV", nx, 3), ("Q", 2 * nx)]
                slot_fills[a + 6] = [("KT", 2 * nx, 0)]
                slot_fills[a + 7] = [("KT", 2 * nx, 1)]
        NU = XP * PC
        for u in range(NU):
            order += slot_fills.get(u, [])
        NF = len(order)
        by_act = lambda f: f[0] == "KV" or f[0] == "Q" or (f[0] == "KT" and f[2] == 0) or (f[0] == "T" and f[1] % 2 == 0)
        by_dve = lambda f: f[0] == "Q" or (f[0] == "KT" and f[2] == 1) or (f[0] == "T" and f[1] % 2 == 1)
        no = {f: i for i, f in enumerate(order)}
        act_by = [sum(map(by_act, order[:i + 1])) for i in range(NF)]
        dve_by = [sum(map(by_dve, order[:i + 1])) for i in range(NF)]
        NA, NV = act_by[-1], dve_by[-1]
        assert NF % 2 == 0

        block = ctx.enter_context(nc.Block())

        @block.sync
        def _(sp):
            for k in range(KD):
                rows = w_kv[k * P:(k + 1) * P, :]
                for j in range(2):
                    sp.dma_start(wkv_st[:, k, :, j * P:(j + 1) * P],
                                 rows[:, j * XH * XD:(j + 1) * XH * XD].rearrange("p (a n) -> p a n", a=XP)).then_inc(m["w_loaded"], 16)
            sp.dma_start(wq_st, w_q.rearrange("(k p) n -> p k n", p=P)).then_inc(m["w_loaded"], 16)
            sp.dma_start(wo[:, :, :], w_o.rearrange("(k p) n -> p k n", p=P)).then_inc(m["w_loaded"], 16)
            with nc.allow_non_contiguous_dma("small vectors"):
                for n, (g, bb) in enumerate(((ctx_g, ctx_b), (lat_g, lat_b))):
                    sp.dma_start(g_in[:, n, :], g.rearrange("(k p) -> p k", p=P)).then_inc(m["c_loaded"], 16)
                    sp.dma_start(b_in[:, n, :], bb.rearrange("(k p) -> p k", p=P)).then_inc(m["c_loaded"], 16)
                for j in range(2):
                    sp.dma_start(c2[:, :, j * 32:(j + 1) * 32], cos.rearrange("(t p) d -> p t d", p=P)).then_inc(m["c_loaded"], 16)
                    sp.dma_start(s2[:, :, j * 32:(j + 1) * 32], sin.rearrange("(t p) d -> p t d", p=P)).then_inc(m["c_loaded"], 16)
            sp.dma_start(bo[:, :], b_o.unsqueeze(0).broadcast_to([P, D])).then_inc(m["c_loaded"], 16)
            sp.dma_start(cx[:, :, :], ctx_dram[0].rearrange("(t p) d -> p t d", p=P)).then_inc(m["cx_loaded"], 16)
            sp.wait_ge(m["w_split"], UP + 1)

            def query_weights(b, prefetch):
                for h in range(XH):
                    if h < 2:
                        sp.wait_ge(m["bg_full"], UP + b * NF)
                    else:
                        sp.wait_ge(m["bg_full"], UP + b * NF + no[("Q", h - 2)] + 1)
                    for j in range(2):
                        sp.dma_start(as32(wqd[:, h % 2, :, j * XD:(j + 1) * XD]),
                                     as32(wq[:, :, :, h * XD:(h + 1) * XD].rearrange("p a k n -> p (a k) n"))).then_inc(wqd_loaded[h % 2], 16)
                    if prefetch and h == 2:
                        sp.wait_ge(m["cx_used"], UP + b + 1)
                        sp.dma_start(cx[:, :, :], ctx_dram[bass.ds(b + 1, 1), :, :].rearrange("b (t p) d -> p (b t) d", p=P))\
                            .then_inc(m["cx_loaded"], 16)

            with sp.Fori(0, B - 1) as b:
                query_weights(b, True)
            query_weights(B - 1, False)
        W_LOADS, C_LOADS = 16 * (2 * KD + 2), 16 * 9

        @block.gpsimd
        def _(pool):
            nc.gpsimd.memset(ones[:, :], 1.0).then_inc(m["pool_steps"], 1)
            ROPES = 2 * XP
            with pool.Fori(0, B) as b:
                for r in range(ROPES):
                    p, q = divmod(r, 2)
                    pool.wait_ge(m["rot_ready"], UP + b * ROPES + r + 1)
                    nc.gpsimd.tensor_tensor(t1[:, :, :, 0:32], t1[:, :, :, 0:32], t2[:, :, :, 32:64], ALU.add)
                    nc.gpsimd.tensor_tensor(t1[:, :, :, 32:64], t1[:, :, :, 32:64], t2[:, :, :, 0:32], ALU.add).then_inc(m["kr_ready"], 1)
                    pool.wait_ge(m["khi_ready"], UP + b * ROPES + r + 1)
                    pool.wait_ge(m["kr_ready"], UP + b * ROPES + r + 1)
                    t = slice(4 * q, 4 * q + 4)
                    nc.gpsimd.tensor_tensor(stk[:, p % 2, t, :, XD:P], t1[:, :, :, :], stk[:, p % 2, t, :, 0:XD], ALU.subtract)\
                        .then_inc(m["stk_ready"], 1)

        ROPES = 2 * XP

        @block.tensor
        def _(pe):
            pe.wait_ge(m["pool_steps"], UP + 1)
            pe.wait_ge(m["w_split"], UP + 2)
            with pe.Fori(0, B) as b:
                def fill(f):
                    n = no[f]
                    if n < 2:
                        pe.wait_ge(m["bg_act"], UP + b * NA)
                        pe.wait_ge(m["bg_dve"], UP + b * NV)
                    else:
                        pe.wait_ge(m["bg_act"], UP + b * NA + act_by[n - 2])
                        pe.wait_ge(m["bg_dve"], UP + b * NV + dve_by[n - 2])
                    return p_bg[:, n % 2, :]

                def product(out, x, w, halves):
                    steps = [(x[i], w[j], k) for i, j in halves for k in range(KD)]
                    for n, (xx, ww, k) in enumerate(steps):
                        last = nc.tensor.matmul(out, xx(k), ww(k), start=(n == 0), stop=(n == len(steps) - 1))
                    return last

                def background(f):
                    out = fill(f)
                    if f[0] == "T":
                        i = f[1]
                        for j in range(4):
                            if i < 4:
                                k, t = divmod(4 * i + j, CT)
                                src = cx[:, t, k * P:(k + 1) * P]
                            else:
                                src = ln[:, j, (i - 4) * P:(i - 3) * P]
                            last = nc.tensor.transpose(out[:, j * P:(j + 1) * P], src, ident[:, :])
                    elif f[0] == "KV":
                        _, p, i = f
                        for j in range(2):
                            t = 2 * i + j
                            last = product(out[:, j * 2 * P:(j + 1) * 2 * P],
                                           [lambda k, x=x, t=t: x[:, k, t * P:(t + 1) * P] for x in (cT_hi, cT_lo)],
                                           [lambda k, w=w: w[:, k, p, :] for w in (wkv_hi, wkv_lo)], ((0, 0), (0, 1), (1, 0)))
                    elif f[0] == "Q":
                        h = f[1]
                        pe.wait_ge(wqd_loaded[h % 2], b * 32 * XP + 32 * (h // 2 + 1))
                        last = product(out, [lambda k, i=i: wqd[:, h % 2, i * KD + k, :] for i in range(2)],
                                       [lambda k, x=x: x[:, k, :] for x in (lT_hi, lT_lo)], ((0, 0), (0, 1), (1, 0)))
                    else:
                        _, h, q = f
                        pe.wait_ge(m["stk_ready"], UP + b * ROPES + h // 2 * 2 + q + 1)
                        for j in range(4):
                            last = nc.tensor.transpose(out[:, j * P:(j + 1) * P], stk[:, h // 2 % 2, 4 * q + j, h % 2, :], ident[:, :])
                    last.then_inc(m["bg_full"], 1)

                def scores(u):
                    h, c = divmod(u, HC)
                    if c == 0:
                        n = max(no[("KT", h, 1)], no[("Q", h)])
                        pe.wait_ge(m["bg_act"], UP + b * NA + act_by[n])
                        pe.wait_ge(m["bg_dve"], UP + b * NV + dve_by[n])
                    if u >= 2:
                        pe.wait_ge(m["exp_ready"], UP + b * NU + u - 1)
                    for j in range(2):
                        t = 2 * c + j
                        for half in range(2):
                            last = nc.tensor.matmul(p_s[:, u % 2, j, :], kT[:, h % 2, t * P:(t + 1) * P], qT[:, h % 2, half, :],
                                                    start=(half == 0), stop=(half == 1))
                    last.then_inc(m["s_full"], 1)

                def values(u):
                    h, c = divmod(u, HC)
                    pe.wait_ge(m["clipped"], UP + b * NU + u + 1)
                    if c == 0 and h % 2 == 0:
                        pe.wait_ge(m["o_out"], UP + b * XP + h // 2)
                    r = (h % 2) * XD
                    for j in range(2):
                        last = nc.tensor.matmul(p_o[r:r + XD, :], kv[:, h // 2 % 2, 2 * c + j, P + r:P + r + XD], ex[:, u % 4, j, :],
                                                start=(c == 0 and j == 0), stop=(c == HC - 1 and j == 1))
                    last.then_inc(m["av_done"], 1)

                def sums(h):
                    pe.wait_ge(m["esum_ready"], UP + b * XH + h + 1)
                    if h % 2 == 0:
                        pe.wait_ge(m["sum_used"], UP + b * XP + h // 2)
                    r = (h % 2) * XD
                    nc.tensor.matmul(p_sum[r:r + XD, :], ones[:, :], esum[:, :], start=True, stop=True).then_inc(m["sum_full"], 1)

                pe.wait_ge(m["normed"], UP + b + 1)
                for f in order[0:6]:
                    background(f)
                pe.wait_ge(m["xs_ready"], UP + b + 1)
                for f in order[6:13]:
                    background(f)
                for u in range(NU + 2):
                    if u < NU:
                        scores(u)
                    if u >= 2:
                        values(u - 2)
                    for f in slot_fills.get(u, []):
                        background(f)
                    if u % HC == 0 and u > 0:
                        sums(u // HC - 1)
                pe.wait_ge(m["oT_ready"], UP + b * XP + XP)
                pe.wait_ge(m["exp_ready"], UP + b * NU + NU)
                for i in range(TB):
                    for k in range(XP):
                        last = nc.tensor.matmul(p_s[:, i // 2, 0, (i % 2) * D:(i % 2 + 1) * D], oT[:, k, i * P:(i + 1) * P], wo[:, k, :],
                                                start=(k == 0), stop=(k == XP - 1))
                    last.then_inc(m["y_full"], 1)

        @block.scalar
        def _(act):
            act.wait_ge(m["c_loaded"], C_LOADS)
            act.wait_ge(m["w_loaded"], W_LOADS)
            act.wait_ge(m["w_split"], UP + 2)
            with act.Fori(0, B) as b:
                def evacuate(f):
                    if not by_act(f):
                        return
                    n = no[f]
                    act.wait_ge(m["bg_full"], UP + b * NF + n + 1)
                    src = p_bg[:, n % 2, :]
                    if f[0] == "T":
                        i = f[1]
                        if i < 4:
                            k, t = divmod(4 * i, CT)
                            out, s = cT[:, k, t * P:t * P + S], 0
                        else:
                            k, out, s = i - 4, lT[:, i - 4, :], 1
                        ins = nc.scalar.activation(out, src, ACT.Identity, bias=b_in[:, s, k:k + 1], scale=g_in[:, s, k:k + 1])
                    elif f[0] == "KV":
                        _, p, i = f
                        if p < 2:
                            act.wait_ge(m["rot_ready"], UP + b * ROPES)
                            act.wait_ge(m["av_done"], UP + b * NU)
                        else:
                            act.wait_ge(m["rot_ready"], UP + b * ROPES + 2 * (p - 1))
                            act.wait_ge(m["av_done"], UP + b * NU + (p - 1) * PC)
                        ins = nc.scalar.activation(kv[:, p % 2, 2 * i:2 * i + 2, :], src.rearrange("p (t n) -> p t n", t=2), ACT.Copy)
                    elif f[0] == "Q":
                        h = f[1]
                        if h < 2:
                            act.wait_ge(m["s_full"], UP + b * NU)
                        else:
                            act.wait_ge(m["s_full"], UP + b * NU + (h - 1) * HC)
                        ins = nc.scalar.activation(qT[:, h % 2, 0, :], src, ACT.Copy)
                        ins.then_inc(m["bg_act"], 1)
                        return
                    else:
                        _, h, q = f
                        act.wait_ge(m["s_full"], UP + b * NU + max(h - 1, 0) * HC)
                        ins = nc.scalar.activation(kT[:, h % 2, 0:S], src, ACT.Copy)
                    ins.then_inc(m["bg_act"], 1)

                def k_high(r):
                    p, q = divmod(r, 2)
                    act.wait_ge(m["kr_ready"], UP + b * ROPES + r + 1)
                    if p >= 2:
                        act.wait_ge(m["bg_full"], UP + b * NF + no[("KT", 2 * (p - 2) + 1, 1)] + 1)
                    else:
                        act.wait_ge(m["bg_full"], UP + b * NF)
                    t = slice(4 * q, 4 * q + 4)
                    nc.scalar.activation(stk[:, p % 2, t, :, 0:XD].bitcast(F32R), t1[:, :, :, :], ACT.Copy).then_inc(m["khi_ready"], 1)

                def pair_out(k):
                    act.wait_ge(m["av_done"], UP + b * NU + (k + 1) * PC)
                    if k == 0:
                        act.wait_ge(m["y_full"], UP + b * TB)
                    nc.scalar.activation(oT[:, k, :], p_o[:, :], ACT.Copy).then_inc(m["o_out"], 1)

                act.wait_ge(m["added"], UP + b * 3 * XH)
                for f in order[0:10]:
                    evacuate(f)
                k_high(0)
                k_high(1)
                for f in order[10:13]:
                    evacuate(f)
                for u in range(NU + 2):
                    h, c = divmod(u, HC)
                    if u < NU:
                        act.wait_ge(m["s_full"], UP + b * NU + u + 1)
                        if u >= 4:
                            act.wait_ge(m["av_done"], UP + b * NU + u - 3)
                            act.wait_ge(m["added"], UP + b * 3 * XH + 3 * (h - 1) + max(c, 1))
                        else:
                            act.wait_ge(m["xs_ready"], UP + b + 1)
                        nc.scalar.activation(ex[:, u % 4, :, :], p_s[:, u % 2, :, :], ACT.Exp, scale=XD ** -0.5).then_inc(m["exp_ready"], 1)
                    if u % PC == 1 and u > PC:
                        pair_out(u // PC - 1)
                    for f in slot_fills.get(u, []):
                        evacuate(f)
                    p, v = divmod(u, PC)
                    if p + 1 < XP and v in (4, 6):
                        k_high(2 * (p + 1) + (v == 6))

        @block.vector
        def _(dve):
            ch = Chain(dve, m["dve_steps"])
            dve.wait_ge(m["c_loaded"], C_LOADS)
            dve.wait_ge(m["w_loaded"], W_LOADS)
            nc.vector.tensor_copy(wq[:, 0, :, :], wq_st)
            nc.vector.tensor_scalar(s2[:, :, 32:64], s2[:, :, 32:64], -1.0, None, ALU.mult)
            ch.step(nc.vector.tensor_copy(wkv_hi[:, :, :, :], wkv_st))
            nc.vector.tensor_tensor(wq[:, 1, :, :], wq_st, as32(wq[:, 0, :, :]), ALU.subtract).then_inc(m["w_split"], 1)
            for k in range(KD):
                last = nc.vector.tensor_tensor(wkv_lo[:, k, :, :], wkv_st[:, k, :, :], as32(wkv_hi[:, k, :, :]), ALU.subtract)
            last.then_inc(m["w_split"], 1)
            dve.wait_ge(m["w_split"], UP + 2)
            LO, HI = float(np.exp(np.float32(-CLIP))), float(np.exp(np.float32(CLIP)))
            STEPS = 2 * LN_STEPS + 4
            with dve.Fori(0, B) as b:
                ch.start(1 + b * STEPS)

                def evacuate(f):
                    if not by_dve(f):
                        return
                    n = no[f]
                    dve.wait_ge(m["bg_full"], UP + b * NF + n + 1)
                    src = p_bg[:, n % 2, :]
                    if f[0] == "T":
                        i = f[1]
                        if i < 4:
                            k, t = divmod(4 * i, CT)
                            out, s = cT[:, k, t * P:t * P + S], 0
                        else:
                            k, out, s = i - 4, lT[:, i - 4, :], 1
                        ins = nc.vector.tensor_scalar(out, src, g_in[:, s, k:k + 1], b_in[:, s, k:k + 1], ALU.mult, ALU.add)
                    elif f[0] == "Q":
                        h = f[1]
                        dve.wait_ge(m["bg_act"], UP + b * NA + act_by[n])
                        ins = nc.vector.tensor_tensor(qT[:, h % 2, 1, :], src, as32(qT[:, h % 2, 0, :]), ALU.subtract)
                    else:
                        _, h, q = f
                        dve.wait_ge(m["s_full"], UP + b * NU + max(h - 1, 0) * HC)
                        ins = nc.vector.tensor_copy(kT[:, h % 2, S:2 * S], src)
                    ins.then_inc(m["bg_dve"], 1)

                def rotate(r):
                    p, q = divmod(r, 2)
                    dve.wait_ge(m["bg_act"], UP + b * NA + act_by[no[("KV", p, 2 * q + 1)]])
                    dve.wait_ge(m["stk_ready"], UP + b * ROPES + r)
                    t = slice(4 * q, 4 * q + 4)
                    k4 = kv[:, p % 2, t, 0:P].rearrange("p t (h d) -> p t h d", d=XD)
                    nc.vector.tensor_tensor(t1[:, :, :, :], k4, c2[:, t, :].unsqueeze(2).broadcast_to([P, 4, 2, XD]), ALU.mult)
                    nc.vector.tensor_tensor(t2[:, :, :, :], k4, s2[:, t, :].unsqueeze(2).broadcast_to([P, 4, 2, XD]), ALU.mult)\
                        .then_inc(m["rot_ready"], 1)

                def recip(k):
                    dve.wait_ge(m["sum_full"], UP + b * XH + 2 * k + 2)
                    if k > 0:
                        dve.wait_ge(m["oT_ready"], UP + b * XP + k)
                    else:
                        dve.wait_ge(m["oT_ready"], UP + b * XP)
                    nc.vector.reciprocal(rcp[:, :], p_sum[:, :]).then_inc(m["sum_used"], 1)

                def divide(k):
                    dve.wait_ge(m["sum_used"], UP + b * XP + k + 1)
                    dve.wait_ge(m["o_out"], UP + b * XP + k + 1)
                    nc.vector.tensor_tensor(oT[:, k, :], oT[:, k, :], rcp[:, :], ALU.mult).then_inc(m["oT_ready"], 1)

                dve.wait_ge(m["cx_loaded"], b * 16 + 16)
                lats = [flat(tile_of(X, b * TB + i)) for i in range(TB)]
                tiles = [cx[:, t, :] for t in range(CT)] + lats
                layer_norm_stats(nc, ch, tiles, st, mv, rstd, tmp, 1e-5)
                for i, x in enumerate(tiles):
                    out = x if i < CT else ln[:, i - CT, :]
                    last = nc.vector.tensor_scalar(out, x, mv[:, i, 0:1], rstd[:, i:i + 1], ALU.subtract, ALU.mult)
                last.then_inc(m["normed"], 1)
                for f in order[0:6]:
                    evacuate(f)
                dve.wait_ge(m["bg_act"], UP + b * NA + act_by[5])
                dve.wait_ge(m["bg_dve"], UP + b * NV + dve_by[5])
                dve.wait_ge(m["bg_full"], UP + b * NF + 6)
                nc.vector.tensor_copy(lT_hi[:, :, :], lT).then_inc(m["cx_used"], 1)
                ch.step(nc.vector.tensor_copy(cT_hi[:, :, :], cT))
                nc.vector.tensor_tensor(lT_lo[:, :, :], lT, as32(lT_hi[:, :, :]), ALU.subtract)
                nc.vector.tensor_tensor(cT_lo[:, :, :], cT, as32(cT_hi[:, :, :]), ALU.subtract).then_inc(m["xs_ready"], 1)
                rotate(0)
                rotate(1)
                for f in order[10:13]:
                    evacuate(f)
                for u in range(NU + 2):
                    h, c = divmod(u, HC)
                    if u < NU:
                        dve.wait_ge(m["exp_ready"], UP + b * NU + u + 1)
                        e = ex[:, u % 4, :, :]
                        nc.vector.tensor_scalar(e, e, LO, HI, ALU.max, ALU.min).then_inc(m["clipped"], 1)
                        dve.wait_ge(m["clipped"], UP + b * NU + u + 1)
                        if c >= 1:
                            base = b * 3 * XH + 3 * h
                            if c == 1:
                                dve.wait_ge(m["esum_ready"], UP + b * XH + h)
                                first = ex[:, (u - 1) % 4, :, :]
                            else:
                                dve.wait_ge(m["added"], UP + base + c - 1)
                                first = acc[:, :, :]
                            nc.vector.tensor_tensor(acc[:, :, :], first, e, ALU.add).then_inc(m["added"], 1)
                        if c == HC - 1:
                            dve.wait_ge(m["added"], UP + base + 3)
                            dve.wait_ge(m["sum_full"], UP + b * XH + h)
                            nc.vector.tensor_tensor(esum[:, :], acc[:, 0, :], acc[:, 1, :], ALU.add).then_inc(m["esum_ready"], 1)
                    for f in slot_fills.get(u, []):
                        evacuate(f)
                    p, v = divmod(u, PC)
                    if p + 1 < XP and v in (3, 5):
                        rotate(2 * (p + 1) + (v == 5))
                    if v == 1 and p >= 1:
                        recip(p - 1)
                    if v == 2 and 1 <= p < XP:
                        divide(p - 1)
                divide(XP - 1)
                for i in range(TB):
                    dve.wait_ge(m["y_full"], UP + b * TB + i // 2 * 2 + 2)
                    last = nc.vector.tensor_tensor(lats[i], p_s[:, i // 2, 0, (i % 2) * D:(i % 2 + 1) * D], lats[i], ALU.add)
                ch.step(last)
                xs = tile_of(X, b * TB, TB)
                ch.step(nc.vector.tensor_tensor(xs, xs, bo[:, :].unsqueeze(1).broadcast_to([P, TB, D]), ALU.add))
                layer_norm_stats(nc, ch, lats, st, mv, rstd, tmp, 1e-5)
                for i in range(TB):
                    last = nc.vector.tensor_scalar(lats[i], lats[i], mv[:, i, 0:1], rstd[:, i:i + 1], ALU.subtract, ALU.mult)
                ch.step(last)
                assert ch.n == STEPS, (ch.n, STEPS)


LH, LD = 16, 16
LAT = 128
LP = LH // 2
LG = LH // 4
MASKED = -1e30


LA_SEMS = ("w_split", "dve_steps", "pool_steps", "xn_ready", "xs_ready", "tp_full", "tp_free_act", "tp_free_dve",
           "c_full", "cs_ready", "qkv_full", "qkv_free", "stacked", "s_full", "max_ready", "exp_ready", "norm_ready",
           "av_done", "o_free", "y_full")
LA_DMA_SEMS = ("loaded", "x2_stored")


def latent_attention(nc, sems, X, ident, x2_dram, g_dram, w_q, w_dkv, w_uk, w_uv, w_o):
    with ExitStack() as ctx:
        sc = Scope(nc, ctx, "la", sems)
        w_st = sc.sb("w_st", [P, KD, D + LAT])
        u_st = sc.sb("u_st", [P, 2 * D])
        w_hi = sc.sb("w_hi", [P, KD, D + LAT], F32R)
        w_lo = sc.sb("w_lo", [P, KD, D + LAT], F32R)
        u_hi = sc.sb("u_hi", [P, 2 * D], F32R)
        u_lo = sc.sb("u_lo", [P, 2 * D], F32R)
        wo = sc.sb("wo", [P, LG, D])
        g_in = sc.sb("g_in", [P, KD])
        st = sc.sb("st", [P, TB, 6])
        mv = sc.sb("mv", [P, TB, 2])
        rstd = sc.sb("rstd", [P, TB])
        tmp = sc.sb("tmp", [P, TB])
        xn = sc.sb("xn", [P, TB, D])
        xT = sc.sb("xT", [P, KD, S])
        xh = sc.sb("xh", [P, KD, S], F32R)
        xl = sc.sb("xl", [P, KD, S], F32R)
        cT = sc.sb("cT", [P, S])
        ch_ = sc.sb("ch", [P, S], F32R)
        cl_ = sc.sb("cl", [P, S], F32R)
        q = sc.sb("q", [P, TB, D])
        k = sc.sb("k", [P, TB, D])
        v = sc.sb("v", [P, TB, LH, 32])
        big = sc.sb("big", [P, 2 * TB * LP * P])
        kst = big[:, 0:TB * LP * P].rearrange("p (i a n) -> p i a n", i=TB, a=LP)
        qst = big[:, TB * LP * P:2 * TB * LP * P].rearrange("p (i a n) -> p i a n", i=TB, a=LP)
        kT = sc.sb("kT", [P, LP, S], F32R)
        qT = sc.sb("qT", [P, LH, S], F32R)
        nmx = sc.sb("nmx", [P, LH, TB])
        rs = sc.sb("rs", [P, LH, TB])
        ri = sc.sb("ri", [P, LH, TB])
        prob = sc.sb("prob", [P, 2, TB, S])
        pT0 = sc.sb("pT0", [P, 4, 3, S])
        pT = [pT0[:, :, :, :], big[:, 0:4 * 3 * S].rearrange("p (h t n) -> p h t n", h=4, t=3)]
        oT = sc.sb("oT", [P, LG, S])
        ident_b = sc.sb("ident_b", [P, P], BF16)
        mask_b = sc.sb("mask_b", [P, P], BF16)
        p_tp = sc.ps("p_tp", [P, 2, S])
        p_s = sc.ps("p_s", [P, 3, S])
        p_o = sc.ps("p_o", [P, S])
        p_y = sc.ps("p_y", [P, 2, S])

        m = {n: sc.sem(n) for n in LA_SEMS} | {n: sc.dma_sem(n) for n in LA_DMA_SEMS}

        T2, T3 = KD, KD + 2 * LP
        FILLS = T3 + 3 * LH
        HALF = FILLS // 2
        assert FILLS % 2 == 0
        BANKS = [[(3, 0)], [(2, P), (0, 0)], [(1, 0)]]
        NQ = TB
        TURN = {0: (0, 0), 1: (1, P), 3: (1, 0), 2: (2, 2 * P)}

        block = ctx.enter_context(nc.Block())

        @block.sync
        def _(sp):
            sp.dma_start(w_st[:, :, 0:D], w_q.rearrange("(k p) n -> p k n", p=P)).then_inc(m["loaded"], 16)
            sp.dma_start(w_st[:, :, D:D + LAT], w_dkv.rearrange("(k p) n -> p k n", p=P)).then_inc(m["loaded"], 16)
            sp.dma_start(u_st[:, 0:D], w_uk).then_inc(m["loaded"], 16)
            sp.dma_start(u_st[:, D:2 * D], w_uv).then_inc(m["loaded"], 16)
            with nc.allow_non_contiguous_dma("small vector"):
                sp.dma_start(g_in[:, :], g_dram.rearrange("(k p) -> p k", p=P)).then_inc(m["loaded"], 16)
            sp.dma_start(x2_dram, X[:, :, :]).then_inc(m["x2_stored"], 16)
            sp.wait_ge(m["pool_steps"], UP + 2)
            rows = w_o.rearrange("(g a p) n -> a p g n", a=4, p=LD)
            for a in range(4):
                sp.dma_start(wo[32 * a:32 * a + LD, :, :], rows[a]).then_inc(m["loaded"], 16)
        LOADS = 16 * 9

        @block.gpsimd
        def _(pool):
            nc.gpsimd.memset(v[:, :, :, :], 0.0).then_inc(m["pool_steps"], 1)
            nc.gpsimd.memset(wo[:, :, :], 0.0).then_inc(m["pool_steps"], 1)
            nc.gpsimd.memset(as32(qT[:, :, :]), 0.0).then_inc(m["pool_steps"], 1)
            nc.gpsimd.memset(mask_b[:, :], 0.0).then_inc(m["pool_steps"], 1)
            nc.gpsimd.memset(ident_b[:, :], 0.0).then_inc(m["pool_steps"], 1)
            pool.wait_ge(m["pool_steps"], UP + 5)
            nc.gpsimd.affine_select(out=mask_b[:, :], in_=mask_b[:, :], compare_op=ALU.is_ge, fill=MASKED, base=0,
                                    pattern=[[-1, P]], channel_multiplier=1).then_inc(m["pool_steps"], 1)
            nc.gpsimd.affine_select(out=ident_b[:, :], in_=ident_b[:, :], compare_op=ALU.not_equal, fill=1.0, base=0,
                                    pattern=[[-1, P]], channel_multiplier=1).then_inc(m["pool_steps"], 1)

        @block.tensor
        def _(pe):
            pe.wait_ge(m["w_split"], UP + 1)
            pe.wait_ge(m["pool_steps"], UP + 7)
            pe.wait_ge(m["loaded"], LOADS)
            with pe.Fori(0, B) as b:
                def fill(n):
                    pe.wait_ge(m["tp_free_dve" if n % 2 else "tp_free_act"], UP + b * HALF + n // 2)
                    return p_tp[:, n % 2, :]

                def emptied(n):
                    pe.wait_ge(m["tp_free_act"], UP + b * HALF + (n + 1) // 2)
                    pe.wait_ge(m["tp_free_dve"], UP + b * HALF + n // 2)

                pe.wait_ge(m["xn_ready"], UP + b + 1)
                for kk in range(KD):
                    bank = fill(kk)
                    for i in range(TB):
                        last = nc.tensor.transpose(bank[:, i * P:(i + 1) * P], xn[:, i, kk * P:(kk + 1) * P], ident[:, :])
                    last.then_inc(m["tp_full"], 1)
                pe.wait_ge(m["xs_ready"], UP + b + 1)
                steps = [(x, w, kk) for x, w in ((xh, w_hi), (xh, w_lo), (xl, w_hi)) for kk in range(KD)]
                for n, (x, w, kk) in enumerate(steps):
                    last = nc.tensor.matmul(p_o[:, :], w[:, kk, D:D + LAT], x[:, kk, :], start=(n == 0), stop=(n == len(steps) - 1))
                last.then_inc(m["c_full"], 1)
                for i in range(TB):
                    for n, (x, w, kk) in enumerate(steps):
                        last = nc.tensor.matmul(p_s[:, i % 2, (i // 2) * D:(i // 2 + 1) * D], x[:, kk, i * P:(i + 1) * P], w[:, kk, 0:D],
                                                start=(n == 0), stop=(n == len(steps) - 1))
                last.then_inc(m["qkv_full"], 1)
                pe.wait_ge(m["cs_ready"], UP + b + 1)
                for i in range(TB):
                    if i >= 2:
                        pe.wait_ge(m["qkv_free"], UP + b * (TB + 2) + i + 1)
                    for n, (x, w) in enumerate(((ch_, u_hi), (ch_, u_lo), (cl_, u_hi))):
                        last = nc.tensor.matmul(p_y[:, i % 2, :], x[:, i * P:(i + 1) * P], w[:, :], start=(n == 0), stop=(n == 2))
                    last.then_inc(m["qkv_full"], 1)
                pe.wait_ge(m["stacked"], UP + b + 1)
                for a in range(2 * LP):
                    bank = fill(T2 + a)
                    src = kst if a < LP else qst
                    for i in range(TB):
                        last = nc.tensor.transpose(bank[:, i * P:(i + 1) * P], src[:, i, a % LP, :], ident[:, :])
                    last.then_inc(m["tp_full"], 1)
                emptied(T3)

                def scores(h):
                    for n, tiles in enumerate(BANKS):
                        pe.wait_ge(m["exp_ready"], UP + b * 3 * LH + max(3 * (h - 1) + n + 1, 0))
                        for i, c0 in tiles:
                            nk = (i + 1) * P
                            nc.tensor.matmul(p_s[:, n, c0:c0 + nk], qT[:, h, i * P:(i + 1) * P], kT[:, h // 2, 0:nk], start=True, stop=False)
                            last = nc.tensor.matmul(p_s[:, n, c0 + nk - P:c0 + nk], ident_b[:, :], mask_b[:, :], start=False, stop=True)
                        last.then_inc(m["s_full"], 1)

                def turn(h):
                    pe.wait_ge(m["norm_ready"], UP + b * LH + h + 1)
                    for n in range(3):
                        bank = fill(T3 + 3 * h + n)
                        for j, (nn, c0) in TURN.items():
                            if nn != n:
                                continue
                            for i in range(j, TB):
                                c = c0 + (i - j) * P
                                last = nc.tensor.transpose(bank[:, c:c + P], prob[:, h % 2, i, j * P:(j + 1) * P], ident[:, :])
                        last.then_inc(m["tp_full"], 1)

                def values(g):
                    emptied(T3 + 12 * (g + 1))
                    pe.wait_ge(m["o_free"], UP + b * (LG + 1) + g + 1)
                    for j in range(TB):
                        n, c0 = TURN[j]
                        w = (TB - j) * P
                        for a in range(4):
                            last = nc.tensor.matmul(p_o[32 * a:32 * a + 32, j * P:S], v[:, j, 4 * g + a, :], pT[g % 2][:, a, n, c0:c0 + w],
                                                    start=(j == 0), stop=(j == TB - 1))
                    last.then_inc(m["av_done"], 1)

                for s in range(LH + 2):
                    if s < LH:
                        scores(s)
                    if 1 <= s <= LH:
                        turn(s - 1)
                    if s >= 5 and s % 4 == 1:
                        values((s - 5) // 4)
                pe.wait_ge(m["o_free"], UP + (b + 1) * (LG + 1))
                for i in range(TB):
                    for g in range(LG):
                        last = nc.tensor.matmul(p_y[:, i // 2, (i % 2) * D:(i % 2 + 1) * D], oT[:, g, i * P:(i + 1) * P], wo[:, g, :],
                                                start=(g == 0), stop=(g == LG - 1))
                last.then_inc(m["y_full"], 1)

        @block.scalar
        def _(act):
            act.wait_ge(m["loaded"], LOADS)
            act.wait_ge(m["pool_steps"], UP + 7)
            with act.Fori(0, B) as b:
                act.wait_ge(m["tp_full"], UP + b * FILLS + 1)
                nc.scalar.activation(xT[:, 0, :], p_tp[:, 0, :], ACT.Identity, scale=g_in[:, 0:1]).then_inc(m["tp_free_act"], 1)
                act.wait_ge(m["c_full"], UP + b + 1)
                nc.scalar.activation(cT[:, :], p_o[:, :], ACT.Copy).then_inc(m["o_free"], 1)
                act.wait_ge(m["qkv_full"], UP + b * (TB + 1) + 1)
                for n in range(2):
                    nc.scalar.activation(q[:, n:TB:2, :], p_s[:, n, :].rearrange("p (a d) -> p a d", a=2), ACT.Copy, scale=LD ** -0.5)\
                        .then_inc(m["qkv_free"], 1)
                for i in range(TB):
                    act.wait_ge(m["qkv_full"], UP + b * (TB + 1) + i + 2)
                    nc.scalar.activation(k[:, i, :], p_y[:, i % 2, 0:D], ACT.Copy)
                    nc.scalar.activation(v[:, i, :, 0:LD], p_y[:, i % 2, D:2 * D].rearrange("p (h d) -> p h d", d=LD), ACT.Copy)\
                        .then_inc(m["qkv_free"], 1)

                def stack_out(a):
                    act.wait_ge(m["tp_full"], UP + b * FILLS + T2 + a + 1)
                    if a < LP:
                        last = nc.scalar.activation(kT[:, a, :], p_tp[:, 0, :], ACT.Copy)
                    else:
                        h = 2 * (a - LP)
                        nc.scalar.activation(qT[0:64, h, :], p_tp[0:64, 0, :], ACT.Copy)
                        last = nc.scalar.activation(qT[64:P, h + 1, :], p_tp[64:P, 0, :], ACT.Copy)
                    last.then_inc(m["tp_free_act"], 1)

                for a in range(0, 2 * LP, 2):
                    stack_out(a)

                def turned(h):
                    for n in range(3):
                        f = T3 + 3 * h + n
                        if f % 2 == 0:
                            act.wait_ge(m["tp_full"], UP + b * FILLS + f + 1)
                            act.wait_ge(m["av_done"], UP + b * LG + max(h // 4 - 1, 0))
                            c0 = 2 * P if n == 2 else 0
                            nc.scalar.activation(pT[h // 4 % 2][:, h % 4, n, c0:S], p_tp[:, 0, c0:S], ACT.Copy).then_inc(m["tp_free_act"], 1)

                for s in range(LH + 2):
                    if s < LH:
                        act.wait_ge(m["tp_full"], UP + b * FILLS + T3 + max(3 * (s - 1), 0))
                        for n, tiles in enumerate(BANKS):
                            act.wait_ge(m["max_ready"], UP + b * 3 * LH + 3 * s + n + 1)
                            for i, c0 in tiles:
                                nk = (i + 1) * P
                                last = nc.scalar.activation(prob[:, s % 2, i, 0:nk], p_s[:, n, c0:c0 + nk], ACT.Exp, bias=nmx[:, s, i:i + 1],
                                                            accum_out=rs[:, s, i:i + 1])
                            last.then_inc(m["exp_ready"], 1)
                    if 1 <= s <= LH:
                        turned(s - 1)
                    if s >= 5 and s % 4 == 1:
                        g = (s - 5) // 4
                        act.wait_ge(m["av_done"], UP + b * LG + g + 1)
                        nc.scalar.activation(oT[:, g, :], p_o[:, :], ACT.Copy).then_inc(m["o_free"], 1)

        @block.vector
        def _(dve):
            ch = Chain(dve, m["dve_steps"])
            dve.wait_ge(m["loaded"], LOADS)
            nc.vector.tensor_copy(u_hi[:, :], u_st[:, :])
            ch.step(nc.vector.tensor_copy(w_hi[:, :, :], w_st[:, :, :]))
            nc.vector.tensor_tensor(u_lo[:, :], u_st[:, :], as32(u_hi[:, :]), ALU.subtract)
            nc.vector.tensor_tensor(w_lo[:, :, :], w_st[:, :, :], as32(w_hi[:, :, :]), ALU.subtract).then_inc(m["w_split"], 1)
            STEPS = 4 + RSQRT_STEPS + 4 + LH
            with dve.Fori(0, B) as b:
                ch.start(1 + b * STEPS)
                xs = [flat(tile_of(X, b * TB + i)) for i in range(TB)]
                row_stats(nc, ch, xs, st, mv, tmp)
                ch.step(nc.vector.tensor_tensor(tmp[:, :], mv[:, :, 0], mv[:, :, 0], ALU.mult))
                ch.step(nc.vector.scalar_tensor_tensor(mv[:, :, 1], mv[:, :, 1], 1e-6, tmp[:, :], ALU.add, ALU.add))
                newton_rsqrt(nc, ch, rstd[:, :], mv[:, :, 1], tmp[:, :], None)
                for i in range(TB):
                    last = nc.vector.tensor_scalar(xn[:, i, :], xs[i], rstd[:, i:i + 1], None, ALU.mult)
                last.then_inc(m["xn_ready"], 1)
                dve.wait_ge(m["tp_full"], UP + b * FILLS + 2)
                nc.vector.tensor_scalar(xT[:, 1, :], p_tp[:, 1, :], g_in[:, 1:2], None, ALU.mult).then_inc(m["tp_free_dve"], 1)
                dve.wait_ge(m["tp_free_act"], UP + b * HALF + 1)
                dve.wait_ge(m["tp_free_dve"], UP + b * HALF + 1)
                ch.step(nc.vector.tensor_copy(xh[:, :, :], xT[:, :, :]))
                nc.vector.tensor_tensor(xl[:, :, :], xT[:, :, :], as32(xh[:, :, :]), ALU.subtract).then_inc(m["xs_ready"], 1)
                dve.wait_ge(m["o_free"], UP + b * (LG + 1) + 1)
                ch.step(nc.vector.tensor_copy(ch_[:, :], cT[:, :]))
                nc.vector.tensor_tensor(cl_[:, :], cT[:, :], as32(ch_[:, :]), ALU.subtract).then_inc(m["cs_ready"], 1)
                dve.wait_ge(m["qkv_free"], UP + b * (TB + 2) + TB + 2)
                for i in range(TB):
                    kk = kst[:, i, :, :].rearrange("p a (e r d) -> p (a e) r d", e=2, r=4)
                    qq = qst[:, i, :, :].rearrange("p a (e r d) -> p (a e) r d", e=2, r=4)
                    k3 = k[:, i, :].rearrange("p (h d) -> p h d", d=LD)
                    q3 = q[:, i, :].rearrange("p (h d) -> p h d", d=LD)
                    nc.vector.tensor_copy(kk[:, :, 0, :].bitcast(F32R), k3)
                    last = nc.vector.tensor_copy(qq[:, :, 0, :].bitcast(F32R), q3)
                ch.step(last)
                for i in range(TB):
                    kk = kst[:, i, :, :].rearrange("p a (e r d) -> p (a e) r d", e=2, r=4)
                    qq = qst[:, i, :, :].rearrange("p a (e r d) -> p (a e) r d", e=2, r=4)
                    k3 = k[:, i, :].rearrange("p (h d) -> p h d", d=LD)
                    q3 = q[:, i, :].rearrange("p (h d) -> p h d", d=LD)
                    nc.vector.tensor_copy(kk[:, :, 1, :], kk[:, :, 0, :])
                    nc.vector.tensor_copy(qq[:, :, 2, :], qq[:, :, 0, :])
                    for r in (2, 3):
                        nc.vector.tensor_tensor(kk[:, :, r, :], k3, kk[:, :, 0, :], ALU.subtract)
                    for r in (1, 3):
                        last = nc.vector.tensor_tensor(qq[:, :, r, :], q3, qq[:, :, 0, :], ALU.subtract)
                last.then_inc(m["stacked"], 1)
                for a in range(1, 2 * LP, 2):
                    dve.wait_ge(m["tp_full"], UP + b * FILLS + T2 + a + 1)
                    if a < LP:
                        last = nc.vector.tensor_copy(kT[:, a, :], p_tp[:, 1, :])
                    else:
                        h = 2 * (a - LP)
                        nc.vector.tensor_copy(qT[0:64, h, :], p_tp[0:64, 1, :])
                        last = nc.vector.tensor_copy(qT[64:P, h + 1, :], p_tp[64:P, 1, :])
                    last.then_inc(m["tp_free_dve"], 1)

                def norm(h):
                    dve.wait_ge(m["exp_ready"], UP + b * 3 * LH + 3 * h + 3)
                    ch.step(nc.vector.reciprocal(ri[:, h, :], rs[:, h, :]))
                    for i in range(TB):
                        nk = (i + 1) * P
                        last = nc.vector.tensor_scalar(prob[:, h % 2, i, 0:nk], prob[:, h % 2, i, 0:nk], ri[:, h, i:i + 1], None, ALU.mult)
                    last.then_inc(m["norm_ready"], 1)

                def turned(h):
                    for n in range(3):
                        f = T3 + 3 * h + n
                        if f % 2 == 1:
                            dve.wait_ge(m["tp_full"], UP + b * FILLS + f + 1)
                            dve.wait_ge(m["av_done"], UP + b * LG + max(h // 4 - 1, 0))
                            c0 = 2 * P if n == 2 else 0
                            nc.vector.tensor_copy(pT[h // 4 % 2][:, h % 4, n, c0:S], p_tp[:, 1, c0:S]).then_inc(m["tp_free_dve"], 1)

                for s in range(LH + 1):
                    if s < LH:
                        for n, tiles in enumerate(BANKS):
                            dve.wait_ge(m["s_full"], UP + b * 3 * LH + 3 * s + n + 1)
                            for i, c0 in tiles:
                                nk = (i + 1) * P
                                last = nc.vector.tensor_reduce(nmx[:, s, i:i + 1], p_s[:, n, c0:c0 + nk], AX.X, ALU.max, negate=True)
                            last.then_inc(m["max_ready"], 1)
                    if s >= 1:
                        norm(s - 1)
                        turned(s - 1)
                dve.wait_ge(m["y_full"], UP + b + 1)
                dve.wait_ge(m["x2_stored"], 16)
                for i in range(TB):
                    last = nc.vector.tensor_tensor(xs[i], p_y[:, i // 2, (i % 2) * D:(i % 2 + 1) * D], xs[i], ALU.add)
                ch.step(last)
                assert ch.n == STEPS, (ch.n, STEPS)


NE, EH = 8, 512
EC = EH // P
NB = NT // TB


ME_SEMS = ("dve_steps", "iota_ready", "xn_ready", "tp_full", "tp_free", "ts_ready", "lg_full", "diff_ready",
           "ediff_ready", "comb_ready", "combT_full", "combT_ready", "w_split", "h_full", "silu_ready", "h_ready",
           "y_full", "y_added", "final")
ME_DMA_SEMS = ("loaded", "comb_stored", "stored", "x2_loaded", "w_loaded")


def experts(nc, sems, X, ident, x2_dram, g_dram, gate_w, w1, w2, comb_dram, out):
    with ExitStack() as ctx:
        sc = Scope(nc, ctx, "me", sems)
        T = NT * P
        g_in = sc.sb("g_in", [P, KD])
        gate = sc.sb("gate", [P, KD, NE])
        st = sc.sb("st", [P, NT, 6])
        mv = sc.sb("mv", [P, NT, 2])
        rstd = sc.sb("rstd", [P, NT])
        tmp = sc.sb("tmp", [P, NT])
        t_hi = sc.sb("t_hi", [P, KD, T], F32R)
        t_lo = sc.sb("t_lo", [P, KD, T], F32R)
        lg = sc.sb("lg", [P, NT, NE])
        mx = sc.sb("mx", [P, NT, NE])
        ix = sc.sb("ix", [P, NT, NE], mybir.dt.uint32)
        top = sc.sb("top", [P, NT, 2])
        gt = sc.sb("gt", [P, 3, NT])
        num = sc.sb("num", [P, NE])
        oh = sc.sb("oh", [P, 2, NT, NE])
        comb = sc.sb("comb", [P, NT, NE])
        combT = sc.sb("combT", [P, P])
        w_st = sc.sb("w_st", [P, 2, KD * EH])
        w_hi = sc.sb("w_hi", [P, 2, 2, KD * EH], F32R)
        w_lo = sc.sb("w_lo", [P, 2, 2, KD * EH], F32R)
        cb = sc.sb("cb", [P, 2, T])
        sg = sc.sb("sg", [P, 2, S])
        h_hi = sc.sb("h_hi", [P, 2, EC, S], F32R)
        h_lo = sc.sb("h_lo", [P, 2, EC, S], F32R)
        xn = sc.sb("xn", [P, TB, D])
        tT = sc.sb("tT", [P, KD, S])
        x2 = sc.sb("x2", [P, NT, D])
        p_h = sc.ps("p_h", [P, 4, S])
        p_y = sc.ps("p_y", [P, 2, 2, S])

        m = {n: sc.sem(n) for n in ME_SEMS} | {n: sc.dma_sem(n) for n in ME_DMA_SEMS}
        w_loaded = m["w_loaded"]
        cb_loaded = [sc.dma_sem(f"cb_loaded{i}") for i in range(2)]
        NC = NB * EC

        block = ctx.enter_context(nc.Block())

        @block.sync
        def _(sp):
            sp.dma_start(x2[:, :, :], x2_dram).then_inc(m["x2_loaded"], 16)
            with nc.allow_non_contiguous_dma("small vectors"):
                sp.dma_start(g_in[:, :], g_dram.rearrange("(k p) -> p k", p=P)).then_inc(m["loaded"], 16)
                sp.dma_start(gate[:, :, :], gate_w.rearrange("(k p) n -> p k n", p=P)).then_inc(m["loaded"], 16)
            sp.wait_ge(m["combT_ready"], UP + 1)
            sp.dma_start(comb_dram.rearrange("e (t n) -> t e n", n=P), combT[:, :]).then_inc(m["comb_stored"], 16)
            sp.wait_ge(m["comb_stored"], 16)
            with sp.Fori(0, NE // 2) as ep:
                for j in range(2):
                    sp.wait_ge(m["h_ready"], UP + ep * 2 * NC)
                    sp.dma_start(cb[:, j, :], comb_dram[bass.ds(2 * ep + j, 1), :].broadcast_to([P, T])).then_inc(cb_loaded[j], 16)
            sp.wait_ge(m["final"], UP + 1)
            sp.dma_start(out.rearrange("b (i p) d -> p (b i) d", p=P), X[:, 0:NT, :]).then_inc(m["stored"], 16)
            sp.wait_ge(m["stored"], 16)

        @block.gpsimd
        def _(pool):
            nc.gpsimd.iota(num[:, :], [[1, NE]], base=0, channel_multiplier=0, allow_small_or_imprecise_dtypes=True).then_inc(m["iota_ready"], 1)
            with pool.Fori(0, NE) as e:
                pool.wait_ge(m["w_split"], UP + e)
                pool.dma_start(w_st[:, 0, :].rearrange("p (k n) -> p k n", k=KD),
                               w1[bass.ds(e, 1), :, :].rearrange("e (k p) n -> p (e k) n", p=P)).then_inc(w_loaded, 16)
                pool.dma_start(w_st[:, 1, :].rearrange("p (k n) -> p k n", k=EC),
                               w2[bass.ds(e, 1), :, :].rearrange("e (k p) n -> p (e k) n", p=P)).then_inc(w_loaded, 16)

        @block.tensor
        def _(pe):
            pe.wait_ge(m["loaded"], 32)
            for nb in range(NB):
                pe.wait_ge(m["xn_ready"], UP + nb + 1)
                for k in range(KD):
                    if nb > 0:
                        pe.wait_ge(m["tp_free"], UP + KD * (nb - 1) + k + 1)
                    for i in range(TB):
                        last = nc.tensor.transpose(p_h[:, k, i * P:(i + 1) * P], xn[:, i, k * P:(k + 1) * P], ident[:, :])
                    last.then_inc(m["tp_full"], 1)
                pe.wait_ge(m["tp_free"], UP + KD * (nb + 1))
                for i in range(TB):
                    t = nb * TB + i
                    for k in range(KD):
                        last = nc.tensor.matmul(p_h[:, 2, t * NE:(t + 1) * NE], tT[:, k, i * P:(i + 1) * P], gate[:, k, :],
                                                start=(k == 0), stop=(k == KD - 1))
                last.then_inc(m["lg_full"], 1)
            pe.wait_ge(m["comb_ready"], UP + 1)
            nc.tensor.transpose(p_h[:, 3, 0:P], comb[:, :, :].rearrange("p t e -> p (t e)"), ident[:, :]).then_inc(m["combT_full"], 1)
            pe.wait_ge(m["combT_ready"], UP + 1)
            pe.wait_ge(m["ts_ready"], UP + NB)
            with pe.Fori(0, NE // 2) as ep:
                for j in range(2):
                    e = 2 * ep + j
                    w1h, w1l = (w[:, j, 0, :].rearrange("p (k n) -> p k n", k=KD) for w in (w_hi, w_lo))
                    w2h, w2l = (w[:, j, 1, :].rearrange("p (k n) -> p k n", k=EC) for w in (w_hi, w_lo))

                    def hidden(nb, c):
                        r = nb * EC + c
                        pe.wait_ge(m["silu_ready"], UP + ep * 2 * NC + max(j * NC + r - 3, 0))
                        steps = [(w, x, k) for w, x in ((w1h, t_hi), (w1l, t_hi), (w1h, t_lo)) for k in range(KD)]
                        for n, (w, x, k) in enumerate(steps):
                            last = nc.tensor.matmul(p_h[:, r % 4, :], w[:, k, c * P:(c + 1) * P], x[:, k, nb * S:(nb + 1) * S],
                                                    start=(n == 0), stop=(n == len(steps) - 1))
                        last.then_inc(m["h_full"], 1)

                    def back(nb):
                        pe.wait_ge(m["h_ready"], UP + e * NC + (nb + 1) * EC)
                        pe.wait_ge(m["y_added"], UP + ep * 2 * NB + max(j * NB + nb - 1, 0))
                        for i in range(TB):
                            steps = [(x, w, c) for c in range(EC) for x, w in ((h_hi, w2h), (h_hi, w2l), (h_lo, w2h))]
                            for n, (x, w, c) in enumerate(steps):
                                last = nc.tensor.matmul(p_y[:, nb % 2, i // 2, (i % 2) * D:(i % 2 + 1) * D], x[:, nb % 2, c, i * P:(i + 1) * P],
                                                        w[:, c, :], start=(n == 0), stop=(n == len(steps) - 1))
                        last.then_inc(m["y_full"], 1)

                    pe.wait_ge(m["w_split"], UP + e + 1)
                    for nb in range(NB):
                        for c in range(EC):
                            hidden(nb, c)
                        if nb > 0:
                            back(nb - 1)
                    back(NB - 1)

        @block.scalar
        def _(act):
            act.wait_ge(m["loaded"], 32)
            for nb in range(NB):
                for k in range(KD):
                    act.wait_ge(m["tp_full"], UP + KD * nb + k + 1)
                    if k == 0 and nb > 0:
                        act.wait_ge(m["lg_full"], UP + nb)
                        act.wait_ge(m["ts_ready"], UP + nb)
                    nc.scalar.activation(tT[:, k, :], p_h[:, k, :], ACT.Identity, scale=g_in[:, k:k + 1]).then_inc(m["tp_free"], 1)
            act.wait_ge(m["diff_ready"], UP + 1)
            nc.scalar.activation(gt[:, 2, :], gt[:, 1, :], ACT.Exp).then_inc(m["ediff_ready"], 1)
            act.wait_ge(m["combT_full"], UP + 1)
            nc.scalar.activation(combT[:, :], p_h[:, 3, 0:P], ACT.Copy).then_inc(m["combT_ready"], 1)
            with act.Fori(0, NE // 2) as ep:
                for r in range(2 * NC):
                    act.wait_ge(m["h_full"], UP + ep * 2 * NC + r + 1)
                    act.wait_ge(m["h_ready"], UP + ep * 2 * NC + max(r - 1, 0))
                    nc.scalar.activation(sg[:, r % 2, :], p_h[:, r % 4, :], ACT.Silu).then_inc(m["silu_ready"], 1)

        @block.vector
        def _(dve):
            ch = Chain(dve, m["dve_steps"])
            dve.wait_ge(m["loaded"], 32)
            dve.wait_ge(m["iota_ready"], UP + 1)
            xs = [X[:, t, :] for t in range(NT)]
            row_stats(nc, ch, xs, st, mv, tmp)
            ch.step(nc.vector.tensor_tensor(tmp[:, :], mv[:, :, 0], mv[:, :, 0], ALU.mult))
            ch.step(nc.vector.scalar_tensor_tensor(mv[:, :, 1], mv[:, :, 1], 1e-6, tmp[:, :], ALU.add, ALU.add))
            newton_rsqrt(nc, ch, rstd[:, :], mv[:, :, 1], tmp[:, :], None)
            for nb in range(NB):
                if nb > 0:
                    dve.wait_ge(m["tp_full"], UP + KD * nb)
                for i in range(TB):
                    t = nb * TB + i
                    last = nc.vector.tensor_scalar(xn[:, i, :], xs[t], rstd[:, t:t + 1], None, ALU.mult)
                last.then_inc(m["xn_ready"], 1)
                dve.wait_ge(m["tp_free"], UP + KD * (nb + 1))
                c = slice(nb * S, (nb + 1) * S)
                ch.step(nc.vector.tensor_copy(t_hi[:, :, c], tT[:, :, :]))
                nc.vector.tensor_tensor(t_lo[:, :, c], tT[:, :, :], as32(t_hi[:, :, c]), ALU.subtract).then_inc(m["ts_ready"], 1)
            dve.wait_ge(m["x2_loaded"], 16)
            nc.vector.tensor_tensor(X[:, :, :], X[:, :, :], x2[:, :, :], ALU.add)
            dve.wait_ge(m["lg_full"], UP + NB)
            ch.step(nc.vector.tensor_copy(lg[:, :, :], p_h[:, 2, 0:NT * NE].rearrange("p (t e) -> p t e", e=NE)))
            for t in range(NT):
                last = nc.vector.max(mx[:, t, :], lg[:, t, :])
            ch.step(last)
            for t in range(NT):
                last = nc.vector.max_index(ix[:, t, :], mx[:, t, :], lg[:, t, :])
            nc.vector.tensor_tensor(gt[:, 1, :], mx[:, :, 1], mx[:, :, 0], ALU.subtract).then_inc(m["diff_ready"], 1)
            ch.step(nc.vector.memset(tmp[:, :], 0.0))
            ch.step(nc.vector.tensor_copy(top[:, :, :], ix[:, :, 0:2]))
            dve.wait_ge(m["ediff_ready"], UP + 1)
            ch.step(nc.vector.tensor_scalar_add(tmp[:, :], gt[:, 2, :], 1.0))
            ch.step(nc.vector.reciprocal(gt[:, 0, :], tmp[:, :]))
            nc.vector.tensor_tensor(gt[:, 1, :], gt[:, 2, :], gt[:, 0, :], ALU.mult)
            for j in range(2):
                last = nc.vector.tensor_tensor(oh[:, j, :, :], num[:, :].unsqueeze(1).broadcast_to([P, NT, NE]),
                                               top[:, :, j:j + 1].broadcast_to([P, NT, NE]), ALU.is_equal)
            ch.step(last)
            for j in range(2):
                last = nc.vector.tensor_tensor(oh[:, j, :, :], oh[:, j, :, :], gt[:, j, :].unsqueeze(2).broadcast_to([P, NT, NE]), ALU.mult)
            ch.step(last)
            nc.vector.tensor_tensor(comb[:, :, :], oh[:, 0, :, :], oh[:, 1, :, :], ALU.add).then_inc(m["comb_ready"], 1)
            START = ch.n

            STEPS = 2 + 4 * NC
            with dve.Fori(0, NE // 2) as ep:
                ch.start(START + ep * STEPS)

                def split_weights(j):
                    e = 2 * ep + j
                    dve.wait_ge(w_loaded, 32 * (e + 1))
                    dve.wait_ge(m["y_full"], UP + ep * 2 * NB)
                    ch.step(nc.vector.tensor_copy(w_hi[:, j, :, :], w_st[:, :, :]))
                    nc.vector.tensor_tensor(w_lo[:, j, :, :], w_st[:, :, :], as32(w_hi[:, j, :, :]), ALU.subtract).then_inc(m["w_split"], 1)

                def add(j, nb):
                    dve.wait_ge(m["y_full"], UP + ep * 2 * NB + j * NB + nb + 1)
                    xb = X[:, nb * TB:(nb + 1) * TB, :]
                    nc.vector.tensor_tensor(xb, p_y[:, nb % 2, :, :].rearrange("p a (c d) -> p (a c) d", d=D), xb, ALU.add).then_inc(m["y_added"], 1)

                for j in range(2):
                    split_weights(j)
                    dve.wait_ge(cb_loaded[j], 16 * ep + 16)
                    for nb in range(NB):
                        for c in range(EC):
                            r = j * NC + nb * EC + c
                            dve.wait_ge(m["silu_ready"], UP + ep * 2 * NC + r + 1)
                            s = sg[:, r % 2, :]
                            ch.step(nc.vector.tensor_tensor(s, s, cb[:, j, nb * S:(nb + 1) * S], ALU.mult))
                            dve.wait_ge(m["y_full"], UP + ep * 2 * NB + max(j * NB + nb - 1, 0))
                            ch.step(nc.vector.tensor_copy(h_hi[:, nb % 2, c, :], s))
                            nc.vector.tensor_tensor(h_lo[:, nb % 2, c, :], s, as32(h_hi[:, nb % 2, c, :]), ALU.subtract).then_inc(m["h_ready"], 1)
                            dve.wait_ge(m["h_ready"], UP + ep * 2 * NC + r + 1)
                        if nb > 0:
                            add(j, nb - 1)
                    add(j, NB - 1)
                assert ch.n == STEPS, (ch.n, STEPS)
            dve.wait_ge(m["y_added"], UP + NE * NB)
            ch.start(START + NE // 2 * STEPS)
            layer_norm_stats(nc, ch, xs, st, mv, rstd, tmp, 1e-5)
            for t in range(NT):
                last = nc.vector.tensor_scalar(xs[t], xs[t], mv[:, t, 0:1], rstd[:, t:t + 1], ALU.subtract, ALU.mult)
            last.then_inc(m["final"], 1)


def program(nc, x, w, out, until=9):
    with ExitStack() as ctx:
        X = ctx.enter_context(nc.sbuf_tensor("X", [P, NT, D], F32))
        ident = ctx.enter_context(nc.sbuf_tensor("ident", [P, P], F32))
        id_ready = ctx.enter_context(nc.semaphore("id_ready"))
        stored = ctx.enter_context(nc.semaphore("stored"))
        sems = Semaphores(nc, ctx, [f"{tag}_{n}" for tag, names in (("sa", SA_SEMS), ("xa", XA_SEMS), ("la", LA_SEMS), ("me", ME_SEMS))
                                    for n in names])
        with nc.Block() as block:
            @block.sync
            def _(sp):
                sems.raise_all(sp)

            @block.gpsimd
            def _(pool):
                nc.gpsimd.memset(ident[:, :], 0.0).then_inc(id_ready, 1)
                pool.wait_ge(id_ready, 1)
                nc.gpsimd.affine_select(out=ident[:, :], in_=ident[:, :], compare_op=ALU.not_equal, fill=1.0, base=0,
                                        pattern=[[-1, P]], channel_multiplier=1).then_inc(id_ready, 1)
        self_attention(nc, sems, X, ident, x, w["L0_attn_ln_gamma"], w["L0_attn_ln_beta"], w["L0_attn_q_gamma"], w["L0_attn_k_gamma"],
                       w["L0_attn_w_q"], w["L0_attn_w_k"], w["L0_attn_w_v"], w["L0_attn_w_o"], w["L0_attn_b_o"])
        if until >= 2:
            cross_attention(nc, sems, X, ident, w["ctx_1024"], w["L0_xattn_cos"], w["L0_xattn_sin"], w["L0_xattn_ln_lat_g"], w["L0_xattn_ln_lat_b"],
                            w["L0_xattn_ln_ctx_g"], w["L0_xattn_ln_ctx_b"], w["L0_xattn_Wq"], w["L0_xattn_Wkv"], w["L0_xattn_Wo"],
                            w["L0_xattn_bo"])
        if until >= 3:
            x2_dram = nc.dram_tensor("x2", [P, NT, D], F32).ap()
            latent_attention(nc, sems, X, ident, x2_dram, w["L0_ffn_g1"], w["L0_ffn_Wq"], w["L0_ffn_Wdkv"], w["L0_ffn_Wuk"], w["L0_ffn_Wuv"], w["L0_ffn_Wo"])
        if until >= 4:
            comb_dram = nc.dram_tensor("comb", [NE, NT * P], F32).ap()
            experts(nc, sems, X, ident, x2_dram, w["L0_ffn_g2"], w["L0_ffn_gate_w"], w["L0_ffn_w1"], w["L0_ffn_w2"], comb_dram, out)
            return
        with nc.Block() as block:
            @block.sync
            def _(sp):
                sp.dma_start(out.rearrange("b (i p) d -> p (b i) d", p=P), X[:, 0:NT, :]).then_inc(stored, 16)
                sp.wait_ge(stored, 16)


_TRANSPOSED = ("L0_attn_w_q", "L0_attn_w_k", "L0_attn_w_v", "L0_attn_w_o")


def kernel(**inputs):
    import numpy as _np
    import concourse.bacc as _bacc
    from concourse import mybir as _mybir
    from concourse.bass_utils import run_bass_kernel_spmd as _run

    nc = _bacc.Bacc("TRN2", target_bir_lowering=False, num_devices=1)
    arrays, aps = {}, {}
    for name, a in inputs.items():
        a = _np.asarray(a)
        a = _np.ascontiguousarray(a.T if name in _TRANSPOSED else a)
        arrays[f"in_{name}"] = a
        aps[name] = nc.dram_tensor(f"in_{name}", a.shape, _mybir.dt.from_np(a.dtype), kind="ExternalInput").ap()
    out = nc.dram_tensor("out_x", (B, S, D), _mybir.dt.float32, kind="ExternalOutput").ap()
    program(nc, aps["x"], aps, out)
    r = _run(nc, [arrays], core_ids=[0])
    return r.results[0]["out_x"]
```

```python
from contextlib import ExitStack

import numpy as np
import concourse.bass as bass
from concourse import mybir

ALU = mybir.AluOpType
ACT = mybir.ActivationFunctionType
AX = mybir.AxisListType
F32 = mybir.dt.float32
F32R = mybir.dt.float32r
I32 = mybir.dt.int32
BF16 = mybir.dt.bfloat16

P = 128
B, S, D = 4, 512, 256
KD = D // P
TB = S // P
NT = B * TB
UP = 16
RSQRT_MAGIC = 0x5F3759DF


def as32(ap):
    return ap.bitcast(F32)


class Chain:

    def __init__(self, eng, sem):
        self.eng, self.sem, self.n, self.base = eng, sem, 0, 0

    def start(self, base):
        self.n, self.base = 0, base

    def step(self, ins):
        self.n += 1
        ins.then_inc(self.sem, 1)
        self.eng.wait_ge(self.sem, UP + self.base + self.n)


def newton_rsqrt(nc, ch, y, v, t, c_magic):
    ch.step(nc.vector.tensor_scalar(t.bitcast(I32), v.bitcast(I32), 1, None, ALU.arith_shift_right))
    ch.step(nc.vector.tensor_scalar(y.bitcast(I32), t.bitcast(I32), -1.0, float(RSQRT_MAGIC), ALU.mult, ALU.add))
    for _ in range(4):
        ch.step(nc.vector.tensor_tensor(t, y, y, ALU.mult))
        ch.step(nc.vector.scalar_tensor_tensor(t, t, -0.5, v, ALU.mult, ALU.mult))
        ch.step(nc.vector.scalar_tensor_tensor(y, t, 1.5, y, ALU.add, ALU.mult))


RSQRT_STEPS = 2 + 3 * 4


class Semaphores:

    def __init__(self, nc, ctx, names):
        self.of = {n: ctx.enter_context(nc.semaphore(n)) for n in names}

    def raise_all(self, eng):
        for s in self.of.values():
            eng.sem_inc(s, UP)


class Scope:

    def __init__(self, nc, ctx, tag, sems):
        self.nc, self.ctx, self.tag, self.sems = nc, ctx, tag, sems

    def sb(self, name, shape, dt=F32):
        return self.ctx.enter_context(self.nc.sbuf_tensor(f"{self.tag}_{name}", shape, dt))

    def ps(self, name, shape, dt=F32):
        return self.ctx.enter_context(self.nc.psum_tensor(f"{self.tag}_{name}", shape, dt))

    def sem(self, name):
        return self.sems.of[f"{self.tag}_{name}"]

    def dma_sem(self, name):
        return self.ctx.enter_context(self.nc.semaphore(f"{self.tag}_{name}"))


def tile_of(x, t, n=1):
    return x[:, bass.ds(t, n), :]


def flat(ap):
    return ap.rearrange("p a n -> p (a n)")


def row_stats(nc, ch, tiles, st, mv, tmp):
    nc.vector.memset(tmp[:, 0:1], 0.0)
    for i, x in enumerate(tiles):
        last = nc.vector.bn_stats(st[:, i, :], x)
    ch.step(last)
    nc.vector.memset(tmp[:, 0:1], 0.0)
    for i, _ in enumerate(tiles):
        last = nc.vector.bn_aggr(mv[:, i, :], st[:, i, :])
    ch.step(last)


def layer_norm_stats(nc, ch, tiles, st, mv, rstd, tmp, eps):
    row_stats(nc, ch, tiles, st, mv, tmp)
    ch.step(nc.vector.tensor_scalar_add(mv[:, 0:len(tiles), 1], mv[:, 0:len(tiles), 1], eps))
    newton_rsqrt(nc, ch, rstd[:, 0:len(tiles)], mv[:, 0:len(tiles), 1], tmp[:, 0:len(tiles)], None)


LN_STEPS = 3 + RSQRT_STEPS


AH, AD = 4, 64
AG = 2 * AH
SA_SEMS = ("split_done", "dve_steps", "xn_ready", "xs_ready", "tp_full", "tp_free_act", "tp_free_dve", "qkv_full",
           "qkv_free", "stacked", "s_full", "max_ready", "exp_ready", "norm_ready", "av_done", "o_free", "y_full")


def self_attention(nc, sems, X, ident, x_dram, ln_g, ln_b, q_g, k_g, wqT, wkT, wvT, woT, b_o):
    with ExitStack() as ctx:
        sc = Scope(nc, ctx, "sa", sems)
        w_st = sc.sb("w_st", [P, KD, 3 * D])
        w_hi = sc.sb("w_hi", [P, KD, 3 * D], F32R)
        w_lo = sc.sb("w_lo", [P, KD, 3 * D], F32R)
        wo = sc.sb("wo", [P, KD, D])
        g_in = sc.sb("g_in", [P, KD])
        b_in = sc.sb("b_in", [P, KD])
        gam = sc.sb("gam", [P, AG, AD])
        bo = sc.sb("bo", [P, D])
        st = sc.sb("st", [P, TB, 6])
        mv = sc.sb("mv", [P, TB, 2])
        rstd = sc.sb("rstd", [P, TB])
        tmp = sc.sb("tmp", [P, TB * AG])
        xn = sc.sb("xn", [P, TB, D])
        xT = sc.sb("xT", [P, KD, S])
        xh = sc.sb("xh", [P, KD, S], F32R)
        xl = sc.sb("xl", [P, KD, S], F32R)
        qk = sc.sb("qk", [P, TB, AG * AD])
        sq = sc.sb("sq", [P, TB, AG * AD])
        ss = sc.sb("ss", [P, TB * AG])
        rn = sc.sb("rn", [P, TB * AG])
        v = sc.sb("v", [P, TB, D])
        stk = sc.sb("stk", [P, TB, 3 * AH, P])
        stT = sc.sb("stT", [P, 3 * AH, S], F32R)
        nmx = sc.sb("nmx", [P, AH * TB])
        rs = sc.sb("rs", [P, AH * TB])
        ri = sc.sb("ri", [P, AH * TB])
        prob = sc.sb("prob", [P, 8, S])
        pT = sc.sb("pT", [P, 2, TB, S])
        oT = sc.sb("oT", [P, KD, S])
        p_tp = sc.ps("p_tp", [P, 2, S])
        p_s = sc.ps("p_s", [P, 2, S])
        p_qk = sc.ps("p_qk", [P, S])
        p_v = sc.ps("p_v", [P, S])
        p_o = sc.ps("p_o", [P, S])
        p_y = sc.ps("p_y", [P, S])

        loaded, x_loaded = sc.dma_sem("loaded"), sc.dma_sem("x_loaded")
        split_done = sc.sem("split_done")
        dve_steps = sc.sem("dve_steps")
        xn_ready, xs_ready = sc.sem("xn_ready"), sc.sem("xs_ready")
        tp_full, tp_free_act, tp_free_dve = sc.sem("tp_full"), sc.sem("tp_free_act"), sc.sem("tp_free_dve")
        qkv_full, qkv_free = sc.sem("qkv_full"), sc.sem("qkv_free")
        stacked = sc.sem("stacked")
        s_full, max_ready, exp_ready, norm_ready = (sc.sem(n) for n in ("s_full", "max_ready", "exp_ready", "norm_ready"))
        av_done, o_free = sc.sem("av_done"), sc.sem("o_free")
        y_full = sc.sem("y_full")

        N_ST = 3 * AH
        T2, T3 = KD, KD + N_ST
        FILLS = KD + N_ST + AH * TB
        HALF = FILLS // 2
        UN = AH * TB
        assert FILLS % 2 == 0
        STEPS = 2 * LN_STEPS + RSQRT_STEPS + TB + UN + 10

        block = ctx.enter_context(nc.Block())

        @block.sync
        def _(sp):
            sp.dma_start(X[:, 0:NT, :], x_dram.rearrange("b (i p) d -> p (b i) d", p=P)).then_inc(x_loaded, 16)
            for n, w in enumerate((wqT, wkT, wvT)):
                sp.dma_start(w_st[:, :, n * D:(n + 1) * D], w.rearrange("(k p) n -> p k n", p=P)).then_inc(loaded, 16)
            sp.dma_start(wo[:, :, :], woT.rearrange("(k p) n -> p k n", p=P)).then_inc(loaded, 16)
            with nc.allow_non_contiguous_dma("small vectors"):
                sp.dma_start(g_in[:, :], ln_g.rearrange("(k p) -> p k", p=P)).then_inc(loaded, 16)
                sp.dma_start(b_in[:, :], ln_b.rearrange("(k p) -> p k", p=P)).then_inc(loaded, 16)
            for h in range(AG):
                g = q_g if h < AH else k_g
                sp.dma_start(gam[:, h, :], g.unsqueeze(0).broadcast_to([P, AD])).then_inc(loaded, 16)
            sp.dma_start(bo[:, :], b_o.unsqueeze(0).broadcast_to([P, D])).then_inc(loaded, 16)
        LOADS = 16 * (7 + AG)

        @block.gpsimd
        def _(pool):
            pass

        @block.tensor
        def _(pe):
            def fill(b, n):
                free = tp_free_dve if n % 2 else tp_free_act
                pe.wait_ge(free, UP + b * HALF + n // 2)
                return p_tp[:, n % 2, :]

            pe.wait_ge(split_done, UP + 1)
            with pe.Fori(0, B) as b:
                pe.wait_ge(xn_ready, UP + b + 1)
                for k in range(KD):
                    bank = fill(b, k)
                    for i in range(TB):
                        last = nc.tensor.transpose(bank[:, i * P:(i + 1) * P], xn[:, i, k * P:(k + 1) * P], ident[:, :])
                    last.then_inc(tp_full, 1)
                pe.wait_ge(xs_ready, UP + b + 1)
                for i in range(TB):
                    pe.wait_ge(qkv_free, UP + b * TB + i)
                    for out, c0, n in ((p_qk, 0, 2 * D), (p_v, 2 * D, D)):
                        steps = [(x, w, k) for x, w in ((xh, w_hi), (xh, w_lo), (xl, w_hi)) for k in range(KD)]
                        for j, (x, w, k) in enumerate(steps):
                            last = nc.tensor.matmul(out[:, 0:n], x[:, k, i * P:(i + 1) * P], w[:, k, c0:c0 + n],
                                                    start=(j == 0), stop=(j == len(steps) - 1))
                    last.then_inc(qkv_full, 1)
                pe.wait_ge(stacked, UP + b + 1)
                for m in range(N_ST):
                    bank = fill(b, T2 + m)
                    for i in range(TB):
                        last = nc.tensor.transpose(bank[:, i * P:(i + 1) * P], stk[:, i, m, :], ident[:, :])
                    last.then_inc(tp_full, 1)
                pe.wait_ge(tp_free_act, UP + b * HALF + T3 // 2)
                pe.wait_ge(tp_free_dve, UP + b * HALF + T3 // 2)

                def scores(u):
                    h, i = divmod(u, TB)
                    if u >= 2:
                        pe.wait_ge(exp_ready, UP + b * UN + u - 1)
                    nc.tensor.matmul(p_s[:, u % 2, :], stT[:, AH + h, i * P:(i + 1) * P], stT[:, h, :], start=True, stop=False)
                    nc.tensor.matmul(p_s[:, u % 2, :], stT[:, 2 * AH + h, i * P:(i + 1) * P], stT[:, h, :],
                                     start=False, stop=True).then_inc(s_full, 1)

                def turn(h):
                    pe.wait_ge(norm_ready, UP + b * UN + (h + 1) * TB)
                    for j in range(TB):
                        bank = fill(b, T3 + h * TB + j)
                        for i in range(TB):
                            last = nc.tensor.transpose(bank[:, i * P:(i + 1) * P],
                                                       prob[:, (h * TB + i) % 8, j * P:(j + 1) * P], ident[:, :])
                        last.then_inc(tp_full, 1)

                def values(h):
                    n = (T3 + (h + 1) * TB) // 2
                    pe.wait_ge(tp_free_act, UP + b * HALF + n)
                    pe.wait_ge(tp_free_dve, UP + b * HALF + n)
                    if h % 2 == 0:
                        pe.wait_ge(o_free, UP + b * KD + h // 2)
                    r = (h % 2) * AD
                    for j in range(TB):
                        last = nc.tensor.matmul(p_o[r:r + AD, :], v[:, j, h * AD:(h + 1) * AD], pT[:, h % 2, j, :],
                                                start=(j == 0), stop=(j == TB - 1))
                    last.then_inc(av_done, 1)

                for u in range(UN + 3):
                    if u < UN:
                        scores(u)
                    if u >= 5 and (u - 5) % TB == 0:
                        turn((u - 5) // TB)
                    if u >= 6 and (u - 6) % TB == 0:
                        values((u - 6) // TB)
                pe.wait_ge(o_free, UP + b * KD + KD)
                for i in range(TB):
                    bank = (p_y, p_qk)[i // 2]
                    c = (i % 2) * D
                    for k in range(KD):
                        last = nc.tensor.matmul(bank[:, c:c + D], oT[:, k, i * P:(i + 1) * P], wo[:, k, :],
                                                start=(k == 0), stop=(k == KD - 1))
                    last.then_inc(y_full, 1)

        @block.scalar
        def _(act):
            act.wait_ge(loaded, LOADS)
            with act.Fori(0, B) as b:
                act.wait_ge(tp_full, UP + b * FILLS + 1)
                nc.scalar.activation(xT[:, 0, :], p_tp[:, 0, :], ACT.Identity, bias=b_in[:, 0:1], scale=g_in[:, 0:1]).then_inc(tp_free_act, 1)
                for i in range(TB):
                    act.wait_ge(qkv_full, UP + b * TB + i + 1)
                    nc.scalar.activation(qk[:, i, :], p_qk[:, :], ACT.Copy)
                    nc.scalar.activation(v[:, i, :], p_v[:, 0:D], ACT.Copy).then_inc(qkv_free, 1)
                for n in range(T2, T3, 2):
                    act.wait_ge(tp_full, UP + b * FILLS + n + 1)
                    nc.scalar.activation(stT[:, n - T2, :], p_tp[:, 0, :], ACT.Copy).then_inc(tp_free_act, 1)

                def turned(h):
                    for j in range(0, TB, 2):
                        act.wait_ge(tp_full, UP + b * FILLS + T3 + h * TB + j + 1)
                        act.wait_ge(av_done, UP + b * AH + max(h - 1, 0))
                        nc.scalar.activation(pT[:, h % 2, j, :], p_tp[:, 0, :], ACT.Copy).then_inc(tp_free_act, 1)

                def pair_out(k):
                    act.wait_ge(av_done, UP + b * AH + 2 * k + 2)
                    nc.scalar.activation(oT[:, k, :], p_o[:, :], ACT.Copy).then_inc(o_free, 1)

                for u in range(UN + 3):
                    if u < UN:
                        act.wait_ge(max_ready, UP + b * UN + u + 1)
                        if u >= 8:
                            act.wait_ge(tp_full, UP + b * FILLS + T3 + (u // TB - 1) * TB)
                        nc.scalar.activation(prob[:, u % 8, :], p_s[:, u % 2, :], ACT.Exp, bias=nmx[:, u:u + 1],
                                             accum_out=rs[:, u:u + 1]).then_inc(exp_ready, 1)
                    if u >= 5 and (u - 5) % TB == 0:
                        turned((u - 5) // TB)
                    if u >= 7 and (u - 7) % (2 * TB) == TB:
                        pair_out((u - 7) // (2 * TB))
                pair_out(AH // 2 - 1)

        @block.vector
        def _(dve):
            ch = Chain(dve, dve_steps)
            dve.wait_ge(loaded, LOADS)
            dve.wait_ge(x_loaded, 16)
            ch.step(nc.vector.tensor_copy(w_hi[:, :, :], w_st[:, :, :]))
            ch.step(nc.vector.tensor_scalar(gam[:, 0:AH, :], gam[:, 0:AH, :], AD ** -0.5, None, ALU.mult))
            nc.vector.tensor_tensor(w_lo[:, :, :], w_st[:, :, :], as32(w_hi[:, :, :]), ALU.subtract).then_inc(split_done, 1)
            START = 2
            with dve.Fori(0, B) as b:
                ch.start(b * STEPS + START)
                layer_norm_stats(nc, ch, [flat(tile_of(X, b * TB + i)) for i in range(TB)], st, mv, rstd, tmp, 1e-5)
                for i in range(TB):
                    last = nc.vector.tensor_scalar(xn[:, i, :], flat(tile_of(X, b * TB + i)), mv[:, i, 0:1], rstd[:, i:i + 1],
                                                   ALU.subtract, ALU.mult)
                last.then_inc(xn_ready, 1)
                dve.wait_ge(tp_full, UP + b * FILLS + 2)
                nc.vector.tensor_scalar(xT[:, 1, :], p_tp[:, 1, :], g_in[:, 1:2], b_in[:, 1:2], ALU.mult, ALU.add).then_inc(tp_free_dve, 1)
                dve.wait_ge(tp_free_act, UP + b * HALF + 1)
                dve.wait_ge(tp_free_dve, UP + b * HALF + 1)
                ch.step(nc.vector.tensor_copy(xh[:, :, :], xT[:, :, :]))
                nc.vector.tensor_tensor(xl[:, :, :], xT[:, :, :], as32(xh[:, :, :]), ALU.subtract).then_inc(xs_ready, 1)
                for i in range(TB):
                    dve.wait_ge(qkv_free, UP + b * TB + i + 1)
                    ch.step(nc.vector.tensor_tensor(sq[:, i, :], qk[:, i, :], qk[:, i, :], ALU.mult))
                    last = nc.vector.reduce_sum(ss[:, i * AG:(i + 1) * AG], sq[:, i, :].rearrange("p (g d) -> p g d", d=AD), AX.X)
                ch.step(last)
                ch.step(nc.vector.tensor_scalar(ss[:, :], ss[:, :], 1.0 / AD, 1e-16, ALU.mult, ALU.max))
                newton_rsqrt(nc, ch, rn[:, :], ss[:, :], tmp[:, :], None)
                heads = qk[:, :, :].rearrange("p i (g d) -> p (i g) d", d=AD)
                ch.step(nc.vector.tensor_tensor(heads, heads, rn[:, :].unsqueeze(2).broadcast_to([P, TB * AG, AD]), ALU.mult))
                ch.step(nc.vector.tensor_tensor(qk[:, :, :], qk[:, :, :],
                                                gam[:, :, :].rearrange("p g d -> p (g d)").unsqueeze(1).broadcast_to([P, TB, AG * AD]), ALU.mult))
                q4 = qk[:, :, 0:AH * AD].rearrange("p i (h d) -> p i h d", d=AD)
                k4 = qk[:, :, AH * AD:2 * AH * AD].rearrange("p i (h d) -> p i h d", d=AD)
                kh, kl = stk[:, :, 0:AH, 0:AD], stk[:, :, 0:AH, AD:P]
                qh, qh2 = stk[:, :, AH:2 * AH, 0:AD], stk[:, :, AH:2 * AH, AD:P]
                ql, ql2 = stk[:, :, 2 * AH:3 * AH, 0:AD], stk[:, :, 2 * AH:3 * AH, AD:P]
                nc.vector.tensor_copy(kh.bitcast(F32R), k4)
                ch.step(nc.vector.tensor_copy(qh.bitcast(F32R), q4))
                nc.vector.tensor_tensor(kl, k4, kh, ALU.subtract)
                ch.step(nc.vector.tensor_tensor(ql, q4, qh, ALU.subtract))
                nc.vector.tensor_copy(qh2, qh)
                nc.vector.tensor_copy(ql2, ql).then_inc(stacked, 1)
                for n in range(T2 + 1, T3, 2):
                    dve.wait_ge(tp_full, UP + b * FILLS + n + 1)
                    nc.vector.tensor_copy(stT[:, n - T2, :], p_tp[:, 1, :]).then_inc(tp_free_dve, 1)

                def norm(u):
                    dve.wait_ge(exp_ready, UP + b * UN + u + 1)
                    ch.step(nc.vector.reciprocal(ri[:, u:u + 1], rs[:, u:u + 1]))
                    nc.vector.tensor_scalar(prob[:, u % 8, :], prob[:, u % 8, :], ri[:, u:u + 1], None, ALU.mult).then_inc(norm_ready, 1)

                def turned(h):
                    for j in range(1, TB, 2):
                        dve.wait_ge(tp_full, UP + b * FILLS + T3 + h * TB + j + 1)
                        dve.wait_ge(av_done, UP + b * AH + max(h - 1, 0))
                        nc.vector.tensor_copy(pT[:, h % 2, j, :], p_tp[:, 1, :]).then_inc(tp_free_dve, 1)

                for u in range(UN + 3):
                    if u < UN:
                        dve.wait_ge(s_full, UP + b * UN + u + 1)
                        nc.vector.tensor_reduce(nmx[:, u:u + 1], p_s[:, u % 2, :], AX.X, ALU.max, negate=True).then_inc(max_ready, 1)
                    if 1 <= u <= UN:
                        norm(u - 1)
                    if u >= 5 and (u - 5) % TB == 0:
                        turned((u - 5) // TB)
                for i in range(TB):
                    dve.wait_ge(y_full, UP + b * TB + i // 2 * 2 + 2)
                    xi = flat(tile_of(X, b * TB + i))
                    bank = (p_y, p_qk)[i // 2]
                    c = (i % 2) * D
                    last = nc.vector.tensor_tensor(xi, bank[:, c:c + D], xi, ALU.add)
                ch.step(last)
                xs = tile_of(X, b * TB, TB)
                ch.step(nc.vector.tensor_tensor(xs, xs, bo[:, :].unsqueeze(1).broadcast_to([P, TB, D]), ALU.add))
                layer_norm_stats(nc, ch, [flat(tile_of(X, b * TB + i)) for i in range(TB)], st, mv, rstd, tmp, 1e-5)
                for i in range(TB):
                    xi = flat(tile_of(X, b * TB + i))
                    last = nc.vector.tensor_scalar(xi, xi, mv[:, i, 0:1], rstd[:, i:i + 1], ALU.subtract, ALU.mult)
                ch.step(last)
                assert ch.n == STEPS, (ch.n, STEPS)


XH, XD = 16, 64
XP = XH // 2
SC = 1024
CT = SC // P
HC = CT // 2
PC = 2 * HC
CLIP = 11.0


XA_SEMS = ("cx_used", "w_split", "dve_steps", "normed", "xs_ready", "bg_full", "bg_act", "bg_dve", "rot_ready",
           "kr_ready", "khi_ready", "stk_ready", "pool_steps", "s_full", "exp_ready", "clipped", "y_added", "added",
           "esum_ready", "sum_full", "sum_used", "av_done", "o_out", "oT_ready", "y_full")
XA_DMA_SEMS = ("w_loaded", "c_loaded", "cx_loaded")


def cross_attention(nc, sems, X, ident, ctx_dram, cos, sin, lat_g, lat_b, ctx_g, ctx_b, w_q, w_kv, w_o, b_o):
    with ExitStack() as ctx:
        sc = Scope(nc, ctx, "xa", sems)
        wq = sc.sb("wq", [P, 2, KD, XH * XD], F32R)
        wqd = sc.sb("wqd", [P, 2, 2 * KD, P], F32R)
        wkv_hi = sc.sb("wkv_hi", [P, KD, XP, 2 * P], F32R)
        wkv_lo = sc.sb("wkv_lo", [P, KD, XP, 2 * P], F32R)
        wo = sc.sb("wo", [P, XP, D])
        g_in = sc.sb("g_in", [P, 2, KD])
        b_in = sc.sb("b_in", [P, 2, KD])
        bo = sc.sb("bo", [P, D])
        c2 = sc.sb("c2", [P, CT, XD])
        s2 = sc.sb("s2", [P, CT, XD])
        ones = sc.sb("ones", [P, XD])
        cx = sc.sb("cx", [P, CT, D])
        NL = max(CT + TB, NT)
        st = sc.sb("st", [P, NL, 6])
        mv = sc.sb("mv", [P, NL, 2])
        rstd = sc.sb("rstd", [P, NL])
        tmp = sc.sb("tmp", [P, NL])
        cT_hi = sc.sb("cT_hi", [P, KD, SC], F32R)
        cT_lo = sc.sb("cT_lo", [P, KD, SC], F32R)
        lT_hi = sc.sb("lT_hi", [P, KD, S], F32R)
        lT_lo = sc.sb("lT_lo", [P, KD, S], F32R)
        kv = sc.sb("kv", [P, 2, CT, 2 * P])
        t1 = sc.sb("t1", [P, 4, 2, XD])
        t2 = sc.sb("t2", [P, 4, 2, XD])
        stk = sc.sb("stk", [P, 2, CT, 2, P])
        kT = sc.sb("kT", [P, 2, SC], F32R)
        qT = sc.sb("qT", [P, 2, 2, S], F32R)
        ex = sc.sb("ex", [P, 4, 2, S])
        acc = sc.sb("acc", [P, 2, S])
        esum = sc.sb("esum", [P, S])
        rcp = sc.sb("rcp", [P, S])
        oT = sc.sb("oT", [P, XP, S])
        ex_flat = ex[:, :, :, :].rearrange("p a b n -> p (a b n)")
        oT_flat = oT[:, :, :].rearrange("p a n -> p (a n)")
        stk_flat = [stk[:, j, :, :, :].rearrange("p t h n -> p (t h n)") for j in range(2)]
        cT = stk_flat[0].rearrange("p (k n) -> p k n", k=KD)
        lT = stk_flat[1][:, 0:KD * S].rearrange("p (k n) -> p k n", k=KD)
        ln = stk_flat[1][:, KD * S:KD * S + TB * D].rearrange("p (i d) -> p i d", d=D)
        wkv_st = oT_flat.rearrange("p (k a n) -> p k a n", k=KD, a=XP)
        wq_st = ex_flat[:, 0:KD * XH * XD].rearrange("p (k n) -> p k n", k=KD)

        p_s = sc.ps("p_s", [P, 2, 2, S])
        p_o = sc.ps("p_o", [P, S])
        p_sum = sc.ps("p_sum", [P, S])
        p_bg = sc.ps("p_bg", [P, 2, S])

        m = {n: sc.sem(n) for n in XA_SEMS} | {n: sc.dma_sem(n) for n in XA_DMA_SEMS}
        wqd_loaded = [sc.dma_sem(f"wqd_loaded{i}") for i in range(2)]

        FIRST_T, FIRST_KV = 6, 10
        first_fills = [("T", i) for i in range(6)] + [("KV", 0, i) for i in range(4)] + [("Q", 0), ("KT", 0, 0), ("KT", 0, 1)]
        slot_fills = {}
        for p in range(XP):
            a, h, nx = p * PC, 2 * p + 1, p + 1
            slot_fills[a] = [("KT", h, 0), ("Q", h)]
            slot_fills[a + 1] = [("KT", h, 1)]
            if nx < XP:
                slot_fills[a + 1] += [("KV", nx, 0), ("KV", nx, 1)]
                slot_fills[a + 2] = [("KV", nx, 2)]
                slot_fills[a + 3] = [("KV", nx, 3)]
                slot_fills[a + 4] = [("Q", 2 * nx)]
                slot_fills[a + 6] = [("KT", 2 * nx, 0)]
                slot_fills[a + 7] = [("KT", 2 * nx, 1)]
        NU = XP * PC
        LAST = NU - PC
        next_fills = {LAST + 1: first_fills[0:2], LAST + 2: first_fills[2:4], LAST + 3: first_fills[4:6],
                      LAST + 6: first_fills[6:8], LAST + 7: first_fills[8:10], LAST + 8: first_fills[10:11]}
        order = list(first_fills)
        for u in range(NU):
            order += slot_fills.get(u, [])
        NF = len(order)
        by_act = lambda f: f[0] == "KV" or f[0] == "Q" or f[0] == "KT" or (f[0] == "T" and f[1] % 2 == 0)
        by_dve = lambda f: f[0] == "Q" or (f[0] == "T" and f[1] % 2 == 1)
        no = {f: i for i, f in enumerate(order)}
        act_by = [sum(map(by_act, order[:i + 1])) for i in range(NF)]
        dve_by = [sum(map(by_dve, order[:i + 1])) for i in range(NF)]
        NA, NV = act_by[-1], dve_by[-1]
        assert NF % 2 == 0

        block = ctx.enter_context(nc.Block())

        @block.sync
        def _(sp):
            for k in range(KD):
                rows = w_kv[k * P:(k + 1) * P, :]
                for j in range(2):
                    sp.dma_start(wkv_st[:, k, :, j * P:(j + 1) * P],
                                 rows[:, j * XH * XD:(j + 1) * XH * XD].rearrange("p (a n) -> p a n", a=XP)).then_inc(m["w_loaded"], 16)
            sp.dma_start(wq_st, w_q.rearrange("(k p) n -> p k n", p=P)).then_inc(m["w_loaded"], 16)
            sp.dma_start(wo[:, :, :], w_o.rearrange("(k p) n -> p k n", p=P)).then_inc(m["w_loaded"], 16)
            with nc.allow_non_contiguous_dma("small vectors"):
                for n, (g, bb) in enumerate(((ctx_g, ctx_b), (lat_g, lat_b))):
                    sp.dma_start(g_in[:, n, :], g.rearrange("(k p) -> p k", p=P)).then_inc(m["c_loaded"], 16)
                    sp.dma_start(b_in[:, n, :], bb.rearrange("(k p) -> p k", p=P)).then_inc(m["c_loaded"], 16)
                for j in range(2):
                    sp.dma_start(c2[:, :, j * 32:(j + 1) * 32], cos.rearrange("(t p) d -> p t d", p=P)).then_inc(m["c_loaded"], 16)
                    sp.dma_start(s2[:, :, j * 32:(j + 1) * 32], sin.rearrange("(t p) d -> p t d", p=P)).then_inc(m["c_loaded"], 16)
            sp.dma_start(bo[:, :], b_o.unsqueeze(0).broadcast_to([P, D])).then_inc(m["c_loaded"], 16)
            sp.dma_start(cx[:, :, :], ctx_dram[0].rearrange("(t p) d -> p t d", p=P)).then_inc(m["cx_loaded"], 16)
            sp.wait_ge(m["w_split"], UP + 1)

            def query_weights(b, prefetch):
                for h in range(XH):
                    sp.wait_ge(m["bg_full"], UP + b * NF + (no[("Q", h - 2)] if h >= 2 else no[("Q", XH + h - 2)] - NF) + 1)
                    for j in range(2):
                        sp.dma_start(as32(wqd[:, h % 2, :, j * XD:(j + 1) * XD]),
                                     as32(wq[:, :, :, h * XD:(h + 1) * XD].rearrange("p a k n -> p (a k) n"))).then_inc(wqd_loaded[h % 2], 16)
                    if prefetch and h == 2:
                        sp.wait_ge(m["cx_used"], UP + b + 1)
                        sp.dma_start(cx[:, :, :], ctx_dram[bass.ds(b + 1, 1), :, :].rearrange("b (t p) d -> p (b t) d", p=P))\
                            .then_inc(m["cx_loaded"], 16)

            with sp.Fori(0, B - 1) as b:
                query_weights(b, True)
            query_weights(B - 1, False)
        W_LOADS, C_LOADS = 16 * (2 * KD + 2), 16 * 9

        @block.gpsimd
        def _(pool):
            nc.gpsimd.memset(ones[:, :], 1.0).then_inc(m["pool_steps"], 1)
            ROPES = 2 * XP
            with pool.Fori(0, B) as b:
                for r in range(ROPES):
                    p, q = divmod(r, 2)
                    pool.wait_ge(m["rot_ready"], UP + b * ROPES + r + 1)
                    nc.gpsimd.tensor_tensor(t1[:, :, :, 0:32], t1[:, :, :, 0:32], t2[:, :, :, 32:64], ALU.add)
                    nc.gpsimd.tensor_tensor(t1[:, :, :, 32:64], t1[:, :, :, 32:64], t2[:, :, :, 0:32], ALU.add).then_inc(m["kr_ready"], 1)
                    pool.wait_ge(m["khi_ready"], UP + b * ROPES + r + 1)
                    pool.wait_ge(m["kr_ready"], UP + b * ROPES + r + 1)
                    t = slice(4 * q, 4 * q + 4)
                    nc.gpsimd.tensor_tensor(stk[:, p % 2, t, :, XD:P], t1[:, :, :, :], stk[:, p % 2, t, :, 0:XD], ALU.subtract)\
                        .then_inc(m["stk_ready"], 1)

        ROPES = 2 * XP

        @block.tensor
        def _(pe):
            pe.wait_ge(m["pool_steps"], UP + 1)
            pe.wait_ge(m["w_split"], UP + 2)

            def fill(f, b):
                n = no[f]
                pe.wait_ge(m["bg_act"], UP + b * NA + (act_by[n - 2] if n >= 2 else act_by[NF + n - 2] - NA))
                pe.wait_ge(m["bg_dve"], UP + b * NV + (dve_by[n - 2] if n >= 2 else dve_by[NF + n - 2] - NV))
                return p_bg[:, n % 2, :]

            def product(out, x, w, halves):
                steps = [(x[i], w[j], k) for i, j in halves for k in range(KD)]
                for n, (xx, ww, k) in enumerate(steps):
                    last = nc.tensor.matmul(out, xx(k), ww(k), start=(n == 0), stop=(n == len(steps) - 1))
                return last

            def background(f, b):
                out = fill(f, b)
                if f == ("T", 0):
                    pe.wait_ge(m["normed"], UP + b + 1)
                if f == ("KV", 0, 0):
                    pe.wait_ge(m["xs_ready"], UP + b + 1)
                if f[0] == "T":
                    i = f[1]
                    for j in range(4):
                        if i < 4:
                            k, t = divmod(4 * i + j, CT)
                            src = cx[:, t, k * P:(k + 1) * P]
                        else:
                            src = ln[:, j, (i - 4) * P:(i - 3) * P]
                        last = nc.tensor.transpose(out[:, j * P:(j + 1) * P], src, ident[:, :])
                elif f[0] == "KV":
                    _, p, i = f
                    for j in range(2):
                        t = 2 * i + j
                        last = product(out[:, j * 2 * P:(j + 1) * 2 * P],
                                       [lambda k, x=x, t=t: x[:, k, t * P:(t + 1) * P] for x in (cT_hi, cT_lo)],
                                       [lambda k, w=w: w[:, k, p, :] for w in (wkv_hi, wkv_lo)], ((0, 0), (0, 1), (1, 0)))
                elif f[0] == "Q":
                    h = f[1]
                    pe.wait_ge(wqd_loaded[h % 2], b * 32 * XP + 32 * (h // 2 + 1))
                    last = product(out, [lambda k, i=i: wqd[:, h % 2, i * KD + k, :] for i in range(2)],
                                   [lambda k, x=x: x[:, k, :] for x in (lT_hi, lT_lo)], ((0, 0), (0, 1), (1, 0)))
                else:
                    _, h, q = f
                    pe.wait_ge(m["stk_ready"], UP + b * ROPES + h // 2 * 2 + q + 1)
                    for j in range(4):
                        last = nc.tensor.transpose(out[:, j * P:(j + 1) * P], stk[:, h // 2 % 2, 4 * q + j, h % 2, :], ident[:, :])
                last.then_inc(m["bg_full"], 1)

            def batch(b, more):
                def scores(u):
                    h, c = divmod(u, HC)
                    if c == 0:
                        n = max(no[("KT", h, 1)], no[("Q", h)])
                        pe.wait_ge(m["bg_act"], UP + b * NA + act_by[n])
                        pe.wait_ge(m["bg_dve"], UP + b * NV + dve_by[n])
                    if u == 0:
                        pe.wait_ge(m["y_added"], UP + b)
                    pe.wait_ge(m["exp_ready"], UP + b * NU + u - 1)
                    for j in range(2):
                        t = 2 * c + j
                        for half in range(2):
                            last = nc.tensor.matmul(p_s[:, u % 2, j, :], kT[:, h % 2, t * P:(t + 1) * P], qT[:, h % 2, half, :],
                                                    start=(half == 0), stop=(half == 1))
                    last.then_inc(m["s_full"], 1)

                def values(u):
                    h, c = divmod(u, HC)
                    pe.wait_ge(m["clipped"], UP + b * NU + u + 1)
                    if c == 0 and h % 2 == 0:
                        pe.wait_ge(m["o_out"], UP + b * XP + h // 2)
                    r = (h % 2) * XD
                    for j in range(2):
                        last = nc.tensor.matmul(p_o[r:r + XD, :], kv[:, h // 2 % 2, 2 * c + j, P + r:P + r + XD], ex[:, u % 4, j, :],
                                                start=(c == 0 and j == 0), stop=(c == HC - 1 and j == 1))
                    last.then_inc(m["av_done"], 1)

                def sums(h):
                    pe.wait_ge(m["esum_ready"], UP + b * XH + h + 1)
                    if h % 2 == 0:
                        pe.wait_ge(m["sum_used"], UP + b * 2 * XP + 2 * (h // 2))
                    r = (h % 2) * XD
                    nc.tensor.matmul(p_sum[r:r + XD, :], ones[:, :], esum[:, :], start=True, stop=True).then_inc(m["sum_full"], 1)

                for u in range(NU + 2):
                    if u < NU:
                        scores(u)
                    if u >= 2:
                        values(u - 2)
                    for f in slot_fills.get(u, []):
                        background(f, b)
                    if u % HC == 0 and u > 0:
                        sums(u // HC - 1)
                    if more:
                        for f in next_fills.get(u, []):
                            background(f, b + 1)
                pe.wait_ge(m["exp_ready"], UP + b * NU + NU)
                for ks in (range(XP - 1), range(XP - 1, XP)):
                    pe.wait_ge(m["oT_ready"], UP + b * XP + ks[-1] + 1)
                    for i in range(TB):
                        for k in ks:
                            last = nc.tensor.matmul(p_s[:, i // 2, i % 2, 0:D], oT[:, k, i * P:(i + 1) * P], wo[:, k, :],
                                                    start=(k == 0), stop=(k == XP - 1))
                        if ks[-1] == XP - 1:
                            last.then_inc(m["y_full"], 1)
                if more:
                    for f in first_fills[11:13]:
                        background(f, b + 1)

            for f in first_fills:
                background(f, 0)
            with pe.Fori(0, B - 1) as b:
                batch(b, True)
            batch(B - 1, False)

        @block.scalar
        def _(act):
            act.wait_ge(m["c_loaded"], C_LOADS)
            act.wait_ge(m["w_loaded"], W_LOADS)
            act.wait_ge(m["w_split"], UP + 2)

            def evacuate(f, b):
                if not by_act(f):
                    return
                n = no[f]
                act.wait_ge(m["bg_full"], UP + b * NF + n + 1)
                src = p_bg[:, n % 2, :]
                if f[0] == "T":
                    i = f[1]
                    if i < 4:
                        k, t = divmod(4 * i, CT)
                        out, s = cT[:, k, t * P:t * P + S], 0
                    else:
                        k, out, s = i - 4, lT[:, i - 4, :], 1
                    ins = nc.scalar.activation(out, src, ACT.Identity, bias=b_in[:, s, k:k + 1], scale=g_in[:, s, k:k + 1])
                elif f[0] == "KV":
                    _, p, i = f
                    act.wait_ge(m["rot_ready"], UP + b * ROPES + 2 * (p - 1))
                    act.wait_ge(m["av_done"], UP + b * NU + (p - 1) * PC)
                    ins = nc.scalar.activation(kv[:, p % 2, 2 * i:2 * i + 2, :], src.rearrange("p (t n) -> p t n", t=2), ACT.Copy)
                elif f[0] == "Q":
                    h = f[1]
                    act.wait_ge(m["s_full"], UP + b * NU + (h - 1) * HC)
                    ins = nc.scalar.activation(qT[:, h % 2, 0, :], src, ACT.Copy)
                    ins.then_inc(m["bg_act"], 1)
                    return
                else:
                    _, h, q = f
                    act.wait_ge(m["s_full"], UP + b * NU + (h - 1) * HC)
                    ins = nc.scalar.activation(kT[:, h % 2, q * S:(q + 1) * S], src, ACT.Copy)
                ins.then_inc(m["bg_act"], 1)

            def k_high(r, b):
                p, q = divmod(r, 2)
                act.wait_ge(m["kr_ready"], UP + b * ROPES + r + 1)
                if p >= 2:
                    act.wait_ge(m["bg_full"], UP + b * NF + no[("KT", 2 * (p - 2) + 1, 1)] + 1)
                else:
                    act.wait_ge(m["bg_full"], UP + b * NF + FIRST_T)
                t = slice(4 * q, 4 * q + 4)
                nc.scalar.activation(stk[:, p % 2, t, :, 0:XD].bitcast(F32R), t1[:, :, :, :], ACT.Copy).then_inc(m["khi_ready"], 1)

            def pair_out(k, b):
                act.wait_ge(m["av_done"], UP + b * NU + (k + 1) * PC)
                if k == 0:
                    act.wait_ge(m["y_full"], UP + b * TB)
                nc.scalar.activation(oT[:, k, :], p_o[:, :], ACT.Copy).then_inc(m["o_out"], 1)

            def batch(b, more):
                for u in range(NU + 2):
                    h, c = divmod(u, HC)
                    if u < NU:
                        act.wait_ge(m["s_full"], UP + b * NU + u + 1)
                        act.wait_ge(m["av_done"], UP + b * NU + u - 3)
                        act.wait_ge(m["added"], UP + b * 3 * XH + 3 * (h - 1) + max(c, 1))
                        nc.scalar.activation(ex[:, u % 4, :, :], p_s[:, u % 2, :, :], ACT.Exp, scale=XD ** -0.5).then_inc(m["exp_ready"], 1)
                    if u % PC == 1 and u > PC:
                        pair_out(u // PC - 1, b)
                    for f in slot_fills.get(u, []):
                        evacuate(f, b)
                    if more:
                        for f in next_fills.get(u, []):
                            evacuate(f, b + 1)
                    p, v = divmod(u, PC)
                    if p + 1 < XP and v in (4, 5):
                        k_high(2 * (p + 1) + (v == 5), b)
                if more:
                    k_high(0, b + 1)
                    k_high(1, b + 1)
                    for f in first_fills[11:13]:
                        evacuate(f, b + 1)

            for f in first_fills[0:11]:
                evacuate(f, 0)
            k_high(0, 0)
            k_high(1, 0)
            for f in first_fills[11:13]:
                evacuate(f, 0)
            with act.Fori(0, B - 1) as b:
                batch(b, True)
            batch(B - 1, False)

        @block.vector
        def _(dve):
            ch = Chain(dve, m["dve_steps"])
            dve.wait_ge(m["c_loaded"], C_LOADS)
            dve.wait_ge(m["w_loaded"], W_LOADS)
            nc.vector.tensor_copy(wq[:, 0, :, :], wq_st)
            nc.vector.tensor_scalar(s2[:, :, 32:64], s2[:, :, 32:64], -1.0, None, ALU.mult)
            ch.step(nc.vector.tensor_copy(wkv_hi[:, :, :, :], wkv_st))
            nc.vector.tensor_tensor(wq[:, 1, :, :], wq_st, as32(wq[:, 0, :, :]), ALU.subtract).then_inc(m["w_split"], 1)
            for k in range(KD):
                last = nc.vector.tensor_tensor(wkv_lo[:, k, :, :], wkv_st[:, k, :, :], as32(wkv_hi[:, k, :, :]), ALU.subtract)
            last.then_inc(m["w_split"], 1)
            dve.wait_ge(m["w_split"], UP + 2)
            LO, HI = float(np.exp(np.float32(-CLIP))), float(np.exp(np.float32(CLIP)))

            def evacuate(f, b):
                if not by_dve(f):
                    return
                n = no[f]
                dve.wait_ge(m["bg_full"], UP + b * NF + n + 1)
                src = p_bg[:, n % 2, :]
                if f[0] == "T":
                    i = f[1]
                    if i < 4:
                        k, t = divmod(4 * i, CT)
                        out, s = cT[:, k, t * P:t * P + S], 0
                    else:
                        k, out, s = i - 4, lT[:, i - 4, :], 1
                    ins = nc.vector.tensor_scalar(out, src, g_in[:, s, k:k + 1], b_in[:, s, k:k + 1], ALU.mult, ALU.add)
                else:
                    h = f[1]
                    dve.wait_ge(m["bg_act"], UP + b * NA + act_by[n])
                    ins = nc.vector.tensor_tensor(qT[:, h % 2, 1, :], src, as32(qT[:, h % 2, 0, :]), ALU.subtract)
                ins.then_inc(m["bg_dve"], 1)

            def rotate(r, b):
                p, q = divmod(r, 2)
                dve.wait_ge(m["bg_act"], UP + b * NA + act_by[no[("KV", p, 2 * q + 1)]])
                dve.wait_ge(m["stk_ready"], UP + b * ROPES + r)
                t = slice(4 * q, 4 * q + 4)
                k4 = kv[:, p % 2, t, 0:P].rearrange("p t (h d) -> p t h d", d=XD)
                nc.vector.tensor_tensor(t1[:, :, :, :], k4, c2[:, t, :].unsqueeze(2).broadcast_to([P, 4, 2, XD]), ALU.mult)
                nc.vector.tensor_tensor(t2[:, :, :, :], k4, s2[:, t, :].unsqueeze(2).broadcast_to([P, 4, 2, XD]), ALU.mult)\
                    .then_inc(m["rot_ready"], 1)

            def recip(k, j, b):
                cols = slice(j * (S // 2), (j + 1) * (S // 2))
                dve.wait_ge(m["sum_full"], UP + b * XH + 2 * k + 2)
                dve.wait_ge(m["oT_ready"], UP + b * XP + k)
                nc.vector.reciprocal(rcp[:, cols], p_sum[:, cols]).then_inc(m["sum_used"], 1)

            def divide(k, b):
                dve.wait_ge(m["sum_used"], UP + b * 2 * XP + 2 * k + 2)
                dve.wait_ge(m["o_out"], UP + b * XP + k + 1)
                nc.vector.tensor_tensor(oT[:, k, :], oT[:, k, :], rcp[:, :], ALU.mult).then_inc(m["oT_ready"], 1)

            def latents(b):
                return [flat(tile_of(X, b * TB + i)) for i in range(TB)]

            def stats(n, b):
                nc.vector.memset(tmp[:, 0:1], 0.0)
                if n == 0:
                    dve.wait_ge(m["cx_loaded"], b * 16 + 16)
                for i in range(4 * n, 4 * n + 4):
                    last = nc.vector.bn_stats(st[:, i, :], cx[:, i, :] if i < CT else latents(b)[i - CT])
                ch.step(last)

            def stats_done():
                n = CT + TB
                nc.vector.memset(tmp[:, 0:1], 0.0)
                for i in range(n):
                    last = nc.vector.bn_aggr(mv[:, i, :], st[:, i, :])
                ch.step(last)
                ch.step(nc.vector.tensor_scalar_add(mv[:, 0:n, 1], mv[:, 0:n, 1], 1e-5))
                newton_rsqrt(nc, ch, rstd[:, 0:n], mv[:, 0:n, 1], tmp[:, 0:n], None)

            def normalise(tiles, b):
                for i in tiles:
                    x = cx[:, i, :] if i < CT else latents(b)[i - CT]
                    out = x if i < CT else ln[:, i - CT, :]
                    last = nc.vector.tensor_scalar(out, x, mv[:, i, 0:1], rstd[:, i:i + 1], ALU.subtract, ALU.mult)
                return last

            def split_high(b):
                dve.wait_ge(m["bg_act"], UP + b * NA + act_by[5])
                dve.wait_ge(m["bg_dve"], UP + b * NV + dve_by[5])
                dve.wait_ge(m["bg_full"], UP + b * NF + 6)
                nc.vector.tensor_copy(lT_hi[:, :, :], lT).then_inc(m["cx_used"], 1)
                ch.step(nc.vector.tensor_copy(cT_hi[:, :, :], cT))

            def split_low():
                nc.vector.tensor_tensor(lT_lo[:, :, :], lT, as32(lT_hi[:, :, :]), ALU.subtract)
                nc.vector.tensor_tensor(cT_lo[:, :, :], cT, as32(cT_hi[:, :, :]), ALU.subtract).then_inc(m["xs_ready"], 1)

            STEPS = 3 + 2 + RSQRT_STEPS + 1

            def batch(b, more):
                for u in range(NU + 2):
                    h, c = divmod(u, HC)
                    if u < NU:
                        dve.wait_ge(m["exp_ready"], UP + b * NU + u + 1)
                        e = ex[:, u % 4, :, :]
                        nc.vector.tensor_scalar(e, e, LO, HI, ALU.max, ALU.min).then_inc(m["clipped"], 1)
                        dve.wait_ge(m["clipped"], UP + b * NU + u + 1)
                        if c >= 1:
                            base = b * 3 * XH + 3 * h
                            if c == 1:
                                dve.wait_ge(m["esum_ready"], UP + b * XH + h)
                                first = ex[:, (u - 1) % 4, :, :]
                            else:
                                dve.wait_ge(m["added"], UP + base + c - 1)
                                first = acc[:, :, :]
                            nc.vector.tensor_tensor(acc[:, :, :], first, e, ALU.add).then_inc(m["added"], 1)
                        if c == HC - 1:
                            dve.wait_ge(m["added"], UP + base + 3)
                            dve.wait_ge(m["sum_full"], UP + b * XH + h)
                            nc.vector.tensor_tensor(esum[:, :], acc[:, 0, :], acc[:, 1, :], ALU.add).then_inc(m["esum_ready"], 1)
                    for f in slot_fills.get(u, []):
                        evacuate(f, b)
                    p, v = divmod(u, PC)
                    if v in (1, 2) and 1 <= p < XP:
                        recip(p - 1, v - 1, b)
                    if v == 3 and 1 <= p < XP:
                        divide(p - 1, b)
                    if p + 1 < XP and v in (3, 4):
                        rotate(2 * (p + 1) + (v == 4), b)
                    if more:
                        if LAST - 8 <= u < LAST - 5:
                            stats(u - LAST + 8, b + 1)
                        if u == LAST - 2:
                            stats_done()
                        if u == LAST:
                            normalise(range(CT), b + 1)
                        if u == LAST + 1:
                            dve.wait_ge(m["bg_full"], UP + (b + 1) * NF)
                            normalise(range(CT, CT + TB), b + 1).then_inc(m["normed"], 1)
                        for f in next_fills.get(u, []):
                            evacuate(f, b + 1)
                        if u == LAST + 4:
                            split_high(b + 1)
                        if u == LAST + 5:
                            split_low()
                recip(XP - 1, 0, b)
                recip(XP - 1, 1, b)
                divide(XP - 1, b)
                if more:
                    rotate(0, b + 1)
                    rotate(1, b + 1)
                    for f in first_fills[11:13]:
                        evacuate(f, b + 1)
                for i, x in enumerate(latents(b)):
                    dve.wait_ge(m["y_full"], UP + b * TB + i + 1)
                    last = nc.vector.tensor_tensor(x, p_s[:, i // 2, i % 2, 0:D], x, ALU.add)
                last.then_inc(m["y_added"], 1)

            ch.start(1)
            for n in range(3):
                stats(n, 0)
            stats_done()
            normalise(range(CT + TB), 0).then_inc(m["normed"], 1)
            for f in first_fills[0:6]:
                evacuate(f, 0)
            split_high(0)
            split_low()
            rotate(0, 0)
            rotate(1, 0)
            for f in first_fills[10:13]:
                evacuate(f, 0)
            assert ch.n == STEPS, (ch.n, STEPS)
            with dve.Fori(0, B - 1) as b:
                ch.start(1 + (b + 1) * STEPS)
                batch(b, True)
                assert ch.n == STEPS, (ch.n, STEPS)
            batch(B - 1, False)
            ch.start(1 + B * STEPS)
            dve.wait_ge(m["y_added"], UP + B)
            ch.step(nc.vector.tensor_tensor(X[:, :, :], X[:, :, :], bo[:, :].unsqueeze(1).broadcast_to([P, NT, D]), ALU.add))
            tiles = [X[:, t, :] for t in range(NT)]
            layer_norm_stats(nc, ch, tiles, st, mv, rstd, tmp, 1e-5)
            for t, x in enumerate(tiles):
                last = nc.vector.tensor_scalar(x, x, mv[:, t, 0:1], rstd[:, t:t + 1], ALU.subtract, ALU.mult)
            ch.step(last)


LH, LD = 16, 16
LAT = 128
LP = LH // 2
LG = LH // 4
MASKED = -1e30
KEPT = TB * (TB + 1) // 2 * P
FIRST = [i * (i + 1) // 2 * P for i in range(TB)]
NB_P = 4
LAG = NB_P - 1
NB_S = 5


LA_SEMS = ("w_split", "dve_steps", "pool_steps", "xn_ready", "xs_ready", "tp_full", "tp_free_act", "tp_free_dve",
           "c_full", "cs_ready", "qkv_full", "qkv_free", "stacked", "s_full", "max_ready", "exp_ready", "inverted",
           "normed_pool", "normed_dve", "av_done", "o_free", "y_full")
LA_DMA_SEMS = ("loaded", "x2_stored")


def latent_attention(nc, sems, X, ident, x2_dram, g_dram, w_q, w_dkv, w_uk, w_uv, w_o):
    with ExitStack() as ctx:
        sc = Scope(nc, ctx, "la", sems)
        w_hi = sc.sb("w_hi", [P, KD, D + LAT], F32R)
        w_lo = sc.sb("w_lo", [P, KD, D + LAT], F32R)
        u_hi = sc.sb("u_hi", [P, 2 * D], F32R)
        u_lo = sc.sb("u_lo", [P, 2 * D], F32R)
        wo = sc.sb("wo", [P, LG, D])
        g_in = sc.sb("g_in", [P, KD])
        st = sc.sb("st", [P, TB, 6])
        mv = sc.sb("mv", [P, TB, 2])
        rstd = sc.sb("rstd", [P, TB])
        tmp = sc.sb("tmp", [P, TB])
        xn = sc.sb("xn", [P, TB, D])
        xT = sc.sb("xT", [P, KD, S])
        xh = sc.sb("xh", [P, KD, S], F32R)
        xl = sc.sb("xl", [P, KD, S], F32R)
        cT = sc.sb("cT", [P, S])
        ch_ = sc.sb("ch", [P, S], F32R)
        cl_ = sc.sb("cl", [P, S], F32R)
        q = sc.sb("q", [P, TB, D])
        k = sc.sb("k", [P, TB, D])
        v = sc.sb("v", [P, TB, LH, 32])
        big = sc.sb("big", [P, 2 * TB * LP * P])
        kst = big[:, 0:TB * LP * P].rearrange("p (i a n) -> p i a n", i=TB, a=LP)
        qst = big[:, TB * LP * P:2 * TB * LP * P].rearrange("p (i a n) -> p i a n", i=TB, a=LP)
        kT = sc.sb("kT", [P, LP, S], F32R)
        qT = sc.sb("qT", [P, LH, S], F32R)
        nmx = sc.sb("nmx", [P, LH, TB])
        rs = sc.sb("rs", [P, LH, TB])
        ri = sc.sb("ri", [P, LH, TB])
        prob = sc.sb("prob", [P, NB_P, KEPT])
        pT0 = sc.sb("pT0", [P, 4, 3, S])
        w_st = flat(pT0[:, 0, :, :])[:, 0:KD * (D + LAT)].rearrange("p (k n) -> p k n", k=KD)
        u_st = pT0[:, 1, 0, :]
        pT = [pT0[:, :, :, :], big[:, 0:4 * 3 * S].rearrange("p (h t n) -> p h t n", h=4, t=3)]
        oT = sc.sb("oT", [P, LG, S])
        ident_b = sc.sb("ident_b", [P, P], BF16)
        mask_b = sc.sb("mask_b", [P, P], BF16)
        p_tp = sc.ps("p_tp", [P, 2, S])
        p_s = sc.ps("p_s", [P, NB_S, S])
        p_o = sc.ps("p_o", [P, S])

        m = {n: sc.sem(n) for n in LA_SEMS} | {n: sc.dma_sem(n) for n in LA_DMA_SEMS}

        T2, T3 = KD, KD + 2 * LP
        FILLS = T3 + 3 * LH
        HALF = FILLS // 2
        assert FILLS % 2 == 0
        BANKS = [[(3, 0)], [(2, P), (0, 0)], [(1, 0)]]
        NQ = TB
        assert 3 * (LH - 1) >= NB_S
        TURN = {0: (0, 0), 1: (1, P), 3: (1, 0), 2: (2, 2 * P)}

        block = ctx.enter_context(nc.Block())

        @block.sync
        def _(sp):
            sp.dma_start(w_st[:, :, 0:D], w_q.rearrange("(k p) n -> p k n", p=P)).then_inc(m["loaded"], 16)
            sp.dma_start(w_st[:, :, D:D + LAT], w_dkv.rearrange("(k p) n -> p k n", p=P)).then_inc(m["loaded"], 16)
            sp.dma_start(u_st[:, 0:D], w_uk).then_inc(m["loaded"], 16)
            sp.dma_start(u_st[:, D:2 * D], w_uv).then_inc(m["loaded"], 16)
            with nc.allow_non_contiguous_dma("small vector"):
                sp.dma_start(g_in[:, :], g_dram.rearrange("(k p) -> p k", p=P)).then_inc(m["loaded"], 16)
            sp.dma_start(x2_dram, X[:, :, :]).then_inc(m["x2_stored"], 16)
            sp.wait_ge(m["pool_steps"], UP + 2)
            rows = w_o.rearrange("(g a p) n -> a p g n", a=4, p=LD)
            for a in range(4):
                sp.dma_start(wo[32 * a:32 * a + LD, :, :], rows[a]).then_inc(m["loaded"], 16)
        LOADS = 16 * 9

        @block.gpsimd
        def _(pool):
            nc.gpsimd.memset(v[:, :, :, :], 0.0).then_inc(m["pool_steps"], 1)
            nc.gpsimd.memset(wo[:, :, :], 0.0).then_inc(m["pool_steps"], 1)
            nc.gpsimd.memset(as32(qT[:, :, :]), 0.0).then_inc(m["pool_steps"], 1)
            nc.gpsimd.memset(mask_b[:, :], 0.0).then_inc(m["pool_steps"], 1)
            nc.gpsimd.memset(ident_b[:, :], 0.0).then_inc(m["pool_steps"], 1)
            pool.wait_ge(m["pool_steps"], UP + 5)
            nc.gpsimd.affine_select(out=mask_b[:, :], in_=mask_b[:, :], compare_op=ALU.is_ge, fill=MASKED, base=0,
                                    pattern=[[-1, P]], channel_multiplier=1).then_inc(m["pool_steps"], 1)
            nc.gpsimd.affine_select(out=ident_b[:, :], in_=ident_b[:, :], compare_op=ALU.not_equal, fill=1.0, base=0,
                                    pattern=[[-1, P]], channel_multiplier=1).then_inc(m["pool_steps"], 1)
            with pool.Fori(0, B) as b:
                for h in range(LH):
                    pool.wait_ge(m["exp_ready"], UP + b * 3 * LH + 3 * h + 3)
                    pool.wait_ge(m["inverted"], UP + b * LH + h + 1)
                    pr = prob[:, h % NB_P, FIRST[TB - 1]:KEPT]
                    nc.gpsimd.tensor_tensor(pr, pr, ri[:, h, TB - 1:TB].broadcast_to([P, S]), ALU.mult).then_inc(m["normed_pool"], 1)

        @block.tensor
        def _(pe):
            pe.wait_ge(m["w_split"], UP + 1)
            pe.wait_ge(m["pool_steps"], UP + 7)
            pe.wait_ge(m["loaded"], LOADS)
            with pe.Fori(0, B) as b:
                def fill(n):
                    pe.wait_ge(m["tp_free_dve" if n % 2 else "tp_free_act"], UP + b * HALF + n // 2)
                    return p_tp[:, n % 2, :]

                def emptied(n):
                    pe.wait_ge(m["tp_free_act"], UP + b * HALF + (n + 1) // 2)
                    pe.wait_ge(m["tp_free_dve"], UP + b * HALF + n // 2)

                pe.wait_ge(m["xn_ready"], UP + b + 1)
                for kk in range(KD):
                    bank = fill(kk)
                    for i in range(TB):
                        last = nc.tensor.transpose(bank[:, i * P:(i + 1) * P], xn[:, i, kk * P:(kk + 1) * P], ident[:, :])
                    last.then_inc(m["tp_full"], 1)
                pe.wait_ge(m["xs_ready"], UP + b + 1)
                steps = [(x, w, kk) for x, w in ((xh, w_hi), (xh, w_lo), (xl, w_hi)) for kk in range(KD)]
                for n, (x, w, kk) in enumerate(steps):
                    last = nc.tensor.matmul(p_o[:, :], w[:, kk, D:D + LAT], x[:, kk, :], start=(n == 0), stop=(n == len(steps) - 1))
                last.then_inc(m["c_full"], 1)
                for i in range(TB):
                    for n, (x, w, kk) in enumerate(steps):
                        last = nc.tensor.matmul(p_s[:, i % 2, (i // 2) * D:(i // 2 + 1) * D], x[:, kk, i * P:(i + 1) * P], w[:, kk, 0:D],
                                                start=(n == 0), stop=(n == len(steps) - 1))
                last.then_inc(m["qkv_full"], 1)
                pe.wait_ge(m["cs_ready"], UP + b + 1)
                for i in range(TB):
                    if i >= 2:
                        pe.wait_ge(m["qkv_free"], UP + b * (TB + 2) + i + 1)
                    for n, (x, w) in enumerate(((ch_, u_hi), (ch_, u_lo), (cl_, u_hi))):
                        last = nc.tensor.matmul(p_s[:, 2 + i % 2, :], x[:, i * P:(i + 1) * P], w[:, :], start=(n == 0), stop=(n == 2))
                    last.then_inc(m["qkv_full"], 1)
                pe.wait_ge(m["stacked"], UP + b + 1)
                for a in range(2 * LP):
                    bank = fill(T2 + a)
                    src = kst if a < LP else qst
                    for i in range(TB):
                        last = nc.tensor.transpose(bank[:, i * P:(i + 1) * P], src[:, i, a % LP, :], ident[:, :])
                    last.then_inc(m["tp_full"], 1)
                emptied(T3)

                def scores(h, n):
                    unit = 3 * h + n
                    bank = unit % NB_S
                    if unit >= NB_S:
                        pe.wait_ge(m["exp_ready"], UP + b * 3 * LH + unit - NB_S + 1)
                    for i, c0 in BANKS[n]:
                        nk = (i + 1) * P
                        nc.tensor.matmul(p_s[:, bank, c0:c0 + nk], qT[:, h, i * P:(i + 1) * P], kT[:, h // 2, 0:nk], start=True, stop=False)
                        last = nc.tensor.matmul(p_s[:, bank, c0 + nk - P:c0 + nk], ident_b[:, :], mask_b[:, :], start=False, stop=True)
                    last.then_inc(m["s_full"], 1)

                def turn(h, n):
                    pe.wait_ge(m["normed_pool"], UP + b * LH + h + 1)
                    pe.wait_ge(m["normed_dve"], UP + b * LH + h + 1)
                    bank = fill(T3 + 3 * h + n)
                    for j, (nn, c0) in TURN.items():
                        if nn == n:
                            for i in range(j, TB):
                                c = c0 + (i - j) * P
                                last = nc.tensor.transpose(bank[:, c:c + P], prob[:, h % NB_P, FIRST[i] + j * P:FIRST[i] + (j + 1) * P], ident[:, :])
                    last.then_inc(m["tp_full"], 1)

                def values(g, j):
                    if j == 0:
                        emptied(T3 + 12 * (g + 1))
                        pe.wait_ge(m["o_free"], UP + b * (LG + 1) + g + 1)
                    n, c0 = TURN[j]
                    w = (TB - j) * P
                    for a in range(4):
                        last = nc.tensor.matmul(p_o[32 * a:32 * a + 32, j * P:S], v[:, j, 4 * g + a, :], pT[g % 2][:, a, n, c0:c0 + w],
                                                start=(j == 0), stop=(j == TB - 1))
                    if j == TB - 1:
                        last.then_inc(m["av_done"], 1)

                for s in range(LH + LAG):
                    for n in range(3):
                        if s < LH:
                            scores(s, n)
                        if s >= LAG:
                            turn(s - LAG, n)
                    if s >= LAG + 4:
                        values((s - LAG) // 4 - 1, (s - LAG) % 4)
                for j in range(TB):
                    values(LG - 1, j)
                pe.wait_ge(m["o_free"], UP + (b + 1) * (LG + 1))
                pe.wait_ge(m["exp_ready"], UP + (b + 1) * 3 * LH)
                for i in range(TB):
                    for g in range(LG):
                        last = nc.tensor.matmul(p_s[:, i // 2, (i % 2) * D:(i % 2 + 1) * D], oT[:, g, i * P:(i + 1) * P], wo[:, g, :],
                                                start=(g == 0), stop=(g == LG - 1))
                last.then_inc(m["y_full"], 1)

        @block.scalar
        def _(act):
            act.wait_ge(m["loaded"], LOADS)
            act.wait_ge(m["pool_steps"], UP + 7)
            with act.Fori(0, B) as b:
                act.wait_ge(m["tp_full"], UP + b * FILLS + 1)
                nc.scalar.activation(xT[:, 0, :], p_tp[:, 0, :], ACT.Identity, scale=g_in[:, 0:1]).then_inc(m["tp_free_act"], 1)
                act.wait_ge(m["c_full"], UP + b + 1)
                nc.scalar.activation(cT[:, :], p_o[:, :], ACT.Copy).then_inc(m["o_free"], 1)
                act.wait_ge(m["qkv_full"], UP + b * (TB + 1) + 1)
                for n in range(2):
                    nc.scalar.activation(q[:, n:TB:2, :], p_s[:, n, :].rearrange("p (a d) -> p a d", a=2), ACT.Copy, scale=LD ** -0.5)\
                        .then_inc(m["qkv_free"], 1)
                for i in range(TB):
                    act.wait_ge(m["qkv_full"], UP + b * (TB + 1) + i + 2)
                    nc.scalar.activation(k[:, i, :], p_s[:, 2 + i % 2, 0:D], ACT.Copy)
                    nc.scalar.activation(v[:, i, :, 0:LD], p_s[:, 2 + i % 2, D:2 * D].rearrange("p (h d) -> p h d", d=LD), ACT.Copy)\
                        .then_inc(m["qkv_free"], 1)

                def stack_out(a):
                    act.wait_ge(m["tp_full"], UP + b * FILLS + T2 + a + 1)
                    if a < LP:
                        last = nc.scalar.activation(kT[:, a, :], p_tp[:, 0, :], ACT.Copy)
                    else:
                        h = 2 * (a - LP)
                        nc.scalar.activation(qT[0:64, h, :], p_tp[0:64, 0, :], ACT.Copy)
                        last = nc.scalar.activation(qT[64:P, h + 1, :], p_tp[64:P, 0, :], ACT.Copy)
                    last.then_inc(m["tp_free_act"], 1)

                for a in range(0, 2 * LP, 2):
                    stack_out(a)

                def turned(h, n):
                    f = T3 + 3 * h + n
                    if f % 2 == 0:
                        act.wait_ge(m["tp_full"], UP + b * FILLS + f + 1)
                        act.wait_ge(m["av_done"], UP + b * LG + max(h // 4 - 1, 0))
                        c0 = 2 * P if n == 2 else 0
                        nc.scalar.activation(pT[h // 4 % 2][:, h % 4, n, c0:S], p_tp[:, 0, c0:S], ACT.Copy).then_inc(m["tp_free_act"], 1)

                for s in range(LH + LAG):
                    if s < LH:
                        act.wait_ge(m["tp_full"], UP + b * FILLS + T3 + max(3 * (s - LAG), 0))
                    for n, tiles in enumerate(BANKS):
                        if s < LH:
                            act.wait_ge(m["max_ready"], UP + b * 3 * LH + 3 * s + n + 1)
                            for i, c0 in tiles:
                                nk = (i + 1) * P
                                last = nc.scalar.activation(prob[:, s % NB_P, FIRST[i]:FIRST[i] + nk], p_s[:, (3 * s + n) % NB_S, c0:c0 + nk],
                                                            ACT.Exp, bias=nmx[:, s, i:i + 1], accum_out=rs[:, s, i:i + 1])
                            last.then_inc(m["exp_ready"], 1)
                        if s >= LAG:
                            turned(s - LAG, n)
                    if s >= LAG + 8 and (s - LAG) % 4 == 0:
                        g = (s - LAG) // 4 - 2
                        act.wait_ge(m["av_done"], UP + b * LG + g + 1)
                        nc.scalar.activation(oT[:, g, :], p_o[:, :], ACT.Copy).then_inc(m["o_free"], 1)
                for g in range(LG - 2, LG):
                    act.wait_ge(m["av_done"], UP + b * LG + g + 1)
                    nc.scalar.activation(oT[:, g, :], p_o[:, :], ACT.Copy).then_inc(m["o_free"], 1)

        @block.vector
        def _(dve):
            ch = Chain(dve, m["dve_steps"])
            dve.wait_ge(m["loaded"], LOADS)
            nc.vector.tensor_copy(u_hi[:, :], u_st[:, :])
            ch.step(nc.vector.tensor_copy(w_hi[:, :, :], w_st[:, :, :]))
            nc.vector.tensor_tensor(u_lo[:, :], u_st[:, :], as32(u_hi[:, :]), ALU.subtract)
            nc.vector.tensor_tensor(w_lo[:, :, :], w_st[:, :, :], as32(w_hi[:, :, :]), ALU.subtract).then_inc(m["w_split"], 1)
            STEPS = 4 + RSQRT_STEPS + 4
            with dve.Fori(0, B) as b:
                ch.start(1 + b * STEPS)
                xs = [flat(tile_of(X, b * TB + i)) for i in range(TB)]
                row_stats(nc, ch, xs, st, mv, tmp)
                ch.step(nc.vector.tensor_tensor(tmp[:, :], mv[:, :, 0], mv[:, :, 0], ALU.mult))
                ch.step(nc.vector.scalar_tensor_tensor(mv[:, :, 1], mv[:, :, 1], 1e-6, tmp[:, :], ALU.add, ALU.add))
                newton_rsqrt(nc, ch, rstd[:, :], mv[:, :, 1], tmp[:, :], None)
                for i in range(TB):
                    last = nc.vector.tensor_scalar(xn[:, i, :], xs[i], rstd[:, i:i + 1], None, ALU.mult)
                last.then_inc(m["xn_ready"], 1)
                dve.wait_ge(m["tp_full"], UP + b * FILLS + 2)
                nc.vector.tensor_scalar(xT[:, 1, :], p_tp[:, 1, :], g_in[:, 1:2], None, ALU.mult).then_inc(m["tp_free_dve"], 1)
                dve.wait_ge(m["tp_free_act"], UP + b * HALF + 1)
                dve.wait_ge(m["tp_free_dve"], UP + b * HALF + 1)
                ch.step(nc.vector.tensor_copy(xh[:, :, :], xT[:, :, :]))
                nc.vector.tensor_tensor(xl[:, :, :], xT[:, :, :], as32(xh[:, :, :]), ALU.subtract).then_inc(m["xs_ready"], 1)
                dve.wait_ge(m["o_free"], UP + b * (LG + 1) + 1)
                ch.step(nc.vector.tensor_copy(ch_[:, :], cT[:, :]))
                nc.vector.tensor_tensor(cl_[:, :], cT[:, :], as32(ch_[:, :]), ALU.subtract).then_inc(m["cs_ready"], 1)
                dve.wait_ge(m["qkv_free"], UP + b * (TB + 2) + TB + 2)
                for i in range(TB):
                    kk = kst[:, i, :, :].rearrange("p a (e r d) -> p (a e) r d", e=2, r=4)
                    qq = qst[:, i, :, :].rearrange("p a (e r d) -> p (a e) r d", e=2, r=4)
                    k3 = k[:, i, :].rearrange("p (h d) -> p h d", d=LD)
                    q3 = q[:, i, :].rearrange("p (h d) -> p h d", d=LD)
                    nc.vector.tensor_copy(kk[:, :, 0, :].bitcast(F32R), k3)
                    last = nc.vector.tensor_copy(qq[:, :, 0, :].bitcast(F32R), q3)
                ch.step(last)
                for i in range(TB):
                    kk = kst[:, i, :, :].rearrange("p a (e r d) -> p (a e) r d", e=2, r=4)
                    qq = qst[:, i, :, :].rearrange("p a (e r d) -> p (a e) r d", e=2, r=4)
                    k3 = k[:, i, :].rearrange("p (h d) -> p h d", d=LD)
                    q3 = q[:, i, :].rearrange("p (h d) -> p h d", d=LD)
                    nc.vector.tensor_copy(kk[:, :, 1, :], kk[:, :, 0, :])
                    nc.vector.tensor_copy(qq[:, :, 2, :], qq[:, :, 0, :])
                    for r in (2, 3):
                        nc.vector.tensor_tensor(kk[:, :, r, :], k3, kk[:, :, 0, :], ALU.subtract)
                    for r in (1, 3):
                        last = nc.vector.tensor_tensor(qq[:, :, r, :], q3, qq[:, :, 0, :], ALU.subtract)
                last.then_inc(m["stacked"], 1)
                for a in range(1, 2 * LP, 2):
                    dve.wait_ge(m["tp_full"], UP + b * FILLS + T2 + a + 1)
                    if a < LP:
                        last = nc.vector.tensor_copy(kT[:, a, :], p_tp[:, 1, :])
                    else:
                        h = 2 * (a - LP)
                        nc.vector.tensor_copy(qT[0:64, h, :], p_tp[0:64, 1, :])
                        last = nc.vector.tensor_copy(qT[64:P, h + 1, :], p_tp[64:P, 1, :])
                    last.then_inc(m["tp_free_dve"], 1)

                def norm(h):
                    dve.wait_ge(m["exp_ready"], UP + b * 3 * LH + 3 * h + 3)
                    nc.vector.reciprocal(ri[:, h, :], rs[:, h, :]).then_inc(m["inverted"], 1)
                    dve.wait_ge(m["inverted"], UP + b * LH + h + 1)
                    for i in range(TB - 1):
                        pr = prob[:, h % NB_P, FIRST[i]:FIRST[i] + (i + 1) * P]
                        last = nc.vector.tensor_scalar(pr, pr, ri[:, h, i:i + 1], None, ALU.mult)
                    last.then_inc(m["normed_dve"], 1)

                def turned(h, n):
                    f = T3 + 3 * h + n
                    if f % 2 == 1:
                        dve.wait_ge(m["tp_full"], UP + b * FILLS + f + 1)
                        dve.wait_ge(m["av_done"], UP + b * LG + max(h // 4 - 1, 0))
                        c0 = 2 * P if n == 2 else 0
                        nc.vector.tensor_copy(pT[h // 4 % 2][:, h % 4, n, c0:S], p_tp[:, 1, c0:S]).then_inc(m["tp_free_dve"], 1)

                for s in range(LH + LAG):
                    for n, tiles in enumerate(BANKS):
                        if s < LH:
                            dve.wait_ge(m["s_full"], UP + b * 3 * LH + 3 * s + n + 1)
                            for i, c0 in tiles:
                                nk = (i + 1) * P
                                last = nc.vector.tensor_reduce(nmx[:, s, i:i + 1], p_s[:, (3 * s + n) % NB_S, c0:c0 + nk], AX.X, ALU.max, negate=True)
                            last.then_inc(m["max_ready"], 1)
                        if s >= LAG:
                            turned(s - LAG, n)
                    if 1 <= s <= LH:
                        norm(s - 1)
                dve.wait_ge(m["y_full"], UP + b + 1)
                dve.wait_ge(m["x2_stored"], 16)
                for i in range(TB):
                    last = nc.vector.tensor_tensor(xs[i], p_s[:, i // 2, (i % 2) * D:(i % 2 + 1) * D], xs[i], ALU.add)
                ch.step(last)
                assert ch.n == STEPS, (ch.n, STEPS)


NE, EH = 8, 512
EC = EH // P
NB = NT // TB


ME_SEMS = ("dve_steps", "iota_ready", "xn_ready", "tp_full", "tp_free", "ts_ready", "lg_full", "diff_ready",
           "ediff_ready", "comb_ready", "combT_full", "combT_ready", "w_split", "h_full", "silu_ready", "h_ready",
           "y_full", "y_added", "final")
ME_DMA_SEMS = ("loaded", "comb_stored", "stored", "x2_loaded", "w_loaded")


def experts(nc, sems, X, ident, x2_dram, g_dram, gate_w, w1, w2, comb_dram, out):
    with ExitStack() as ctx:
        sc = Scope(nc, ctx, "me", sems)
        T = NT * P
        g_in = sc.sb("g_in", [P, KD])
        gate = sc.sb("gate", [P, KD, NE])
        st = sc.sb("st", [P, NT, 6])
        mv = sc.sb("mv", [P, NT, 2])
        rstd = sc.sb("rstd", [P, NT])
        tmp = sc.sb("tmp", [P, NT])
        t_hi = sc.sb("t_hi", [P, KD, T], F32R)
        t_lo = sc.sb("t_lo", [P, KD, T], F32R)
        lg = sc.sb("lg", [P, NT, NE])
        mx = sc.sb("mx", [P, NT, NE])
        ix = sc.sb("ix", [P, NT, NE], mybir.dt.uint32)
        top = sc.sb("top", [P, NT, 2])
        gt = sc.sb("gt", [P, 3, NT])
        num = sc.sb("num", [P, NE])
        oh = sc.sb("oh", [P, 2, NT, NE])
        comb = sc.sb("comb", [P, NT, NE])
        combT = sc.sb("combT", [P, P])
        w_st = sc.sb("w_st", [P, 2, KD * EH])
        w_hi = sc.sb("w_hi", [P, 2, 2, KD * EH], F32R)
        w_lo = sc.sb("w_lo", [P, 2, 2, KD * EH], F32R)
        cb = sc.sb("cb", [P, 2, T])
        sg = sc.sb("sg", [P, 2, S])
        h_hi = sc.sb("h_hi", [P, 2, EC, S], F32R)
        h_lo = sc.sb("h_lo", [P, 2, EC, S], F32R)
        xn = sc.sb("xn", [P, TB, D])
        tT = sc.sb("tT", [P, KD, S])
        x2 = sc.sb("x2", [P, NT, D])
        p_h = sc.ps("p_h", [P, 4, S])
        p_y = sc.ps("p_y", [P, 2, 2, S])

        m = {n: sc.sem(n) for n in ME_SEMS} | {n: sc.dma_sem(n) for n in ME_DMA_SEMS}
        w_loaded = m["w_loaded"]
        cb_loaded = [sc.dma_sem(f"cb_loaded{i}") for i in range(2)]
        NC = NB * EC

        block = ctx.enter_context(nc.Block())

        @block.sync
        def _(sp):
            sp.dma_start(x2[:, :, :], x2_dram).then_inc(m["x2_loaded"], 16)
            with nc.allow_non_contiguous_dma("small vectors"):
                sp.dma_start(g_in[:, :], g_dram.rearrange("(k p) -> p k", p=P)).then_inc(m["loaded"], 16)
                sp.dma_start(gate[:, :, :], gate_w.rearrange("(k p) n -> p k n", p=P)).then_inc(m["loaded"], 16)
            sp.wait_ge(m["combT_ready"], UP + 1)
            sp.dma_start(comb_dram.rearrange("e (t n) -> t e n", n=P), combT[:, :]).then_inc(m["comb_stored"], 16)
            sp.wait_ge(m["comb_stored"], 16)
            with sp.Fori(0, NE // 2) as ep:
                for j in range(2):
                    sp.wait_ge(m["h_ready"], UP + ep * 2 * NC)
                    sp.dma_start(cb[:, j, :], comb_dram[bass.ds(2 * ep + j, 1), :].broadcast_to([P, T])).then_inc(cb_loaded[j], 16)
            sp.wait_ge(m["final"], UP + 1)
            sp.dma_start(out.rearrange("b (i p) d -> p (b i) d", p=P), X[:, 0:NT, :]).then_inc(m["stored"], 16)
            sp.wait_ge(m["stored"], 16)

        @block.gpsimd
        def _(pool):
            nc.gpsimd.iota(num[:, :], [[1, NE]], base=0, channel_multiplier=0, allow_small_or_imprecise_dtypes=True).then_inc(m["iota_ready"], 1)
            with pool.Fori(0, NE) as e:
                pool.wait_ge(m["w_split"], UP + e)
                pool.dma_start(w_st[:, 0, :].rearrange("p (k n) -> p k n", k=KD),
                               w1[bass.ds(e, 1), :, :].rearrange("e (k p) n -> p (e k) n", p=P)).then_inc(w_loaded, 16)
                pool.dma_start(w_st[:, 1, :].rearrange("p (k n) -> p k n", k=EC),
                               w2[bass.ds(e, 1), :, :].rearrange("e (k p) n -> p (e k) n", p=P)).then_inc(w_loaded, 16)

        @block.tensor
        def _(pe):
            pe.wait_ge(m["loaded"], 32)
            for nb in range(NB):
                pe.wait_ge(m["xn_ready"], UP + nb + 1)
                for k in range(KD):
                    if nb > 0:
                        pe.wait_ge(m["tp_free"], UP + KD * (nb - 1) + k + 1)
                    for i in range(TB):
                        last = nc.tensor.transpose(p_h[:, k, i * P:(i + 1) * P], xn[:, i, k * P:(k + 1) * P], ident[:, :])
                    last.then_inc(m["tp_full"], 1)
                pe.wait_ge(m["tp_free"], UP + KD * (nb + 1))
                for i in range(TB):
                    t = nb * TB + i
                    for k in range(KD):
                        last = nc.tensor.matmul(p_h[:, 2, t * NE:(t + 1) * NE], tT[:, k, i * P:(i + 1) * P], gate[:, k, :],
                                                start=(k == 0), stop=(k == KD - 1))
                last.then_inc(m["lg_full"], 1)
            pe.wait_ge(m["comb_ready"], UP + 1)
            nc.tensor.transpose(p_h[:, 3, 0:P], comb[:, :, :].rearrange("p t e -> p (t e)"), ident[:, :]).then_inc(m["combT_full"], 1)
            pe.wait_ge(m["combT_ready"], UP + 1)
            pe.wait_ge(m["ts_ready"], UP + NB)
            with pe.Fori(0, NE // 2) as ep:
                for j in range(2):
                    e = 2 * ep + j
                    w1h, w1l = (w[:, j, 0, :].rearrange("p (k n) -> p k n", k=KD) for w in (w_hi, w_lo))
                    w2h, w2l = (w[:, j, 1, :].rearrange("p (k n) -> p k n", k=EC) for w in (w_hi, w_lo))

                    def hidden(nb, c):
                        r = nb * EC + c
                        pe.wait_ge(m["silu_ready"], UP + ep * 2 * NC + max(j * NC + r - 3, 0))
                        steps = [(w, x, k) for w, x in ((w1h, t_hi), (w1l, t_hi), (w1h, t_lo)) for k in range(KD)]
                        for n, (w, x, k) in enumerate(steps):
                            last = nc.tensor.matmul(p_h[:, r % 4, :], w[:, k, c * P:(c + 1) * P], x[:, k, nb * S:(nb + 1) * S],
                                                    start=(n == 0), stop=(n == len(steps) - 1))
                        last.then_inc(m["h_full"], 1)

                    def back(nb):
                        pe.wait_ge(m["h_ready"], UP + e * NC + (nb + 1) * EC)
                        pe.wait_ge(m["y_added"], UP + ep * 2 * NB + max(j * NB + nb - 1, 0))
                        for i in range(TB):
                            steps = [(x, w, c) for c in range(EC) for x, w in ((h_hi, w2h), (h_hi, w2l), (h_lo, w2h))]
                            for n, (x, w, c) in enumerate(steps):
                                last = nc.tensor.matmul(p_y[:, nb % 2, i // 2, (i % 2) * D:(i % 2 + 1) * D], x[:, nb % 2, c, i * P:(i + 1) * P],
                                                        w[:, c, :], start=(n == 0), stop=(n == len(steps) - 1))
                        last.then_inc(m["y_full"], 1)

                    pe.wait_ge(m["w_split"], UP + e + 1)
                    for nb in range(NB):
                        for c in range(EC):
                            hidden(nb, c)
                        if nb > 0:
                            back(nb - 1)
                    back(NB - 1)

        @block.scalar
        def _(act):
            act.wait_ge(m["loaded"], 32)
            for nb in range(NB):
                for k in range(KD):
                    act.wait_ge(m["tp_full"], UP + KD * nb + k + 1)
                    if k == 0 and nb > 0:
                        act.wait_ge(m["lg_full"], UP + nb)
                        act.wait_ge(m["ts_ready"], UP + nb)
                    nc.scalar.activation(tT[:, k, :], p_h[:, k, :], ACT.Identity, scale=g_in[:, k:k + 1]).then_inc(m["tp_free"], 1)
            act.wait_ge(m["diff_ready"], UP + 1)
            nc.scalar.activation(gt[:, 2, :], gt[:, 1, :], ACT.Exp).then_inc(m["ediff_ready"], 1)
            act.wait_ge(m["combT_full"], UP + 1)
            nc.scalar.activation(combT[:, :], p_h[:, 3, 0:P], ACT.Copy).then_inc(m["combT_ready"], 1)
            with act.Fori(0, NE // 2) as ep:
                for r in range(2 * NC):
                    act.wait_ge(m["h_full"], UP + ep * 2 * NC + r + 1)
                    act.wait_ge(m["h_ready"], UP + ep * 2 * NC + max(r - 1, 0))
                    nc.scalar.activation(sg[:, r % 2, :], p_h[:, r % 4, :], ACT.Silu).then_inc(m["silu_ready"], 1)

        @block.vector
        def _(dve):
            ch = Chain(dve, m["dve_steps"])
            dve.wait_ge(m["loaded"], 32)
            dve.wait_ge(m["iota_ready"], UP + 1)
            xs = [X[:, t, :] for t in range(NT)]
            row_stats(nc, ch, xs, st, mv, tmp)
            ch.step(nc.vector.tensor_tensor(tmp[:, :], mv[:, :, 0], mv[:, :, 0], ALU.mult))
            ch.step(nc.vector.scalar_tensor_tensor(mv[:, :, 1], mv[:, :, 1], 1e-6, tmp[:, :], ALU.add, ALU.add))
            newton_rsqrt(nc, ch, rstd[:, :], mv[:, :, 1], tmp[:, :], None)
            for nb in range(NB):
                if nb > 0:
                    dve.wait_ge(m["tp_full"], UP + KD * nb)
                for i in range(TB):
                    t = nb * TB + i
                    last = nc.vector.tensor_scalar(xn[:, i, :], xs[t], rstd[:, t:t + 1], None, ALU.mult)
                last.then_inc(m["xn_ready"], 1)
                dve.wait_ge(m["tp_free"], UP + KD * (nb + 1))
                c = slice(nb * S, (nb + 1) * S)
                ch.step(nc.vector.tensor_copy(t_hi[:, :, c], tT[:, :, :]))
                nc.vector.tensor_tensor(t_lo[:, :, c], tT[:, :, :], as32(t_hi[:, :, c]), ALU.subtract).then_inc(m["ts_ready"], 1)
            dve.wait_ge(m["x2_loaded"], 16)
            nc.vector.tensor_tensor(X[:, :, :], X[:, :, :], x2[:, :, :], ALU.add)
            dve.wait_ge(m["lg_full"], UP + NB)
            ch.step(nc.vector.tensor_copy(lg[:, :, :], p_h[:, 2, 0:NT * NE].rearrange("p (t e) -> p t e", e=NE)))
            for t in range(NT):
                last = nc.vector.max(mx[:, t, :], lg[:, t, :])
            ch.step(last)
            for t in range(NT):
                last = nc.vector.max_index(ix[:, t, :], mx[:, t, :], lg[:, t, :])
            nc.vector.tensor_tensor(gt[:, 1, :], mx[:, :, 1], mx[:, :, 0], ALU.subtract).then_inc(m["diff_ready"], 1)
            ch.step(nc.vector.memset(tmp[:, :], 0.0))
            ch.step(nc.vector.tensor_copy(top[:, :, :], ix[:, :, 0:2]))
            dve.wait_ge(m["ediff_ready"], UP + 1)
            ch.step(nc.vector.tensor_scalar_add(tmp[:, :], gt[:, 2, :], 1.0))
            ch.step(nc.vector.reciprocal(gt[:, 0, :], tmp[:, :]))
            nc.vector.tensor_tensor(gt[:, 1, :], gt[:, 2, :], gt[:, 0, :], ALU.mult)
            for j in range(2):
                last = nc.vector.tensor_tensor(oh[:, j, :, :], num[:, :].unsqueeze(1).broadcast_to([P, NT, NE]),
                                               top[:, :, j:j + 1].broadcast_to([P, NT, NE]), ALU.is_equal)
            ch.step(last)
            for j in range(2):
                last = nc.vector.tensor_tensor(oh[:, j, :, :], oh[:, j, :, :], gt[:, j, :].unsqueeze(2).broadcast_to([P, NT, NE]), ALU.mult)
            ch.step(last)
            nc.vector.tensor_tensor(comb[:, :, :], oh[:, 0, :, :], oh[:, 1, :, :], ALU.add).then_inc(m["comb_ready"], 1)
            START = ch.n

            STEPS = 2 + 4 * NC
            with dve.Fori(0, NE // 2) as ep:
                ch.start(START + ep * STEPS)

                def split_weights(j):
                    e = 2 * ep + j
                    dve.wait_ge(w_loaded, 32 * (e + 1))
                    dve.wait_ge(m["y_full"], UP + ep * 2 * NB)
                    ch.step(nc.vector.tensor_copy(w_hi[:, j, :, :], w_st[:, :, :]))
                    nc.vector.tensor_tensor(w_lo[:, j, :, :], w_st[:, :, :], as32(w_hi[:, j, :, :]), ALU.subtract).then_inc(m["w_split"], 1)

                def add(j, nb):
                    dve.wait_ge(m["y_full"], UP + ep * 2 * NB + j * NB + nb + 1)
                    xb = X[:, nb * TB:(nb + 1) * TB, :]
                    nc.vector.tensor_tensor(xb, p_y[:, nb % 2, :, :].rearrange("p a (c d) -> p (a c) d", d=D), xb, ALU.add).then_inc(m["y_added"], 1)

                for j in range(2):
                    split_weights(j)
                    dve.wait_ge(cb_loaded[j], 16 * ep + 16)
                    for nb in range(NB):
                        for c in range(EC):
                            r = j * NC + nb * EC + c
                            dve.wait_ge(m["silu_ready"], UP + ep * 2 * NC + r + 1)
                            s = sg[:, r % 2, :]
                            ch.step(nc.vector.tensor_tensor(s, s, cb[:, j, nb * S:(nb + 1) * S], ALU.mult))
                            dve.wait_ge(m["y_full"], UP + ep * 2 * NB + max(j * NB + nb - 1, 0))
                            ch.step(nc.vector.tensor_copy(h_hi[:, nb % 2, c, :], s))
                            nc.vector.tensor_tensor(h_lo[:, nb % 2, c, :], s, as32(h_hi[:, nb % 2, c, :]), ALU.subtract).then_inc(m["h_ready"], 1)
                            dve.wait_ge(m["h_ready"], UP + ep * 2 * NC + r + 1)
                        if nb > 0:
                            add(j, nb - 1)
                    add(j, NB - 1)
                assert ch.n == STEPS, (ch.n, STEPS)
            dve.wait_ge(m["y_added"], UP + NE * NB)
            ch.start(START + NE // 2 * STEPS)
            layer_norm_stats(nc, ch, xs, st, mv, rstd, tmp, 1e-5)
            for t in range(NT):
                last = nc.vector.tensor_scalar(xs[t], xs[t], mv[:, t, 0:1], rstd[:, t:t + 1], ALU.subtract, ALU.mult)
            last.then_inc(m["final"], 1)


def program(nc, x, w, out, until=9):
    with ExitStack() as ctx:
        X = ctx.enter_context(nc.sbuf_tensor("X", [P, NT, D], F32))
        ident = ctx.enter_context(nc.sbuf_tensor("ident", [P, P], F32))
        id_ready = ctx.enter_context(nc.semaphore("id_ready"))
        stored = ctx.enter_context(nc.semaphore("stored"))
        sems = Semaphores(nc, ctx, [f"{tag}_{n}" for tag, names in (("sa", SA_SEMS), ("xa", XA_SEMS), ("la", LA_SEMS), ("me", ME_SEMS))
                                    for n in names])
        with nc.Block() as block:
            @block.sync
            def _(sp):
                sems.raise_all(sp)

            @block.gpsimd
            def _(pool):
                nc.gpsimd.memset(ident[:, :], 0.0).then_inc(id_ready, 1)
                pool.wait_ge(id_ready, 1)
                nc.gpsimd.affine_select(out=ident[:, :], in_=ident[:, :], compare_op=ALU.not_equal, fill=1.0, base=0,
                                        pattern=[[-1, P]], channel_multiplier=1).then_inc(id_ready, 1)
        self_attention(nc, sems, X, ident, x, w["L0_attn_ln_gamma"], w["L0_attn_ln_beta"], w["L0_attn_q_gamma"], w["L0_attn_k_gamma"],
                       w["L0_attn_w_q"], w["L0_attn_w_k"], w["L0_attn_w_v"], w["L0_attn_w_o"], w["L0_attn_b_o"])
        if until >= 2:
            cross_attention(nc, sems, X, ident, w["ctx_1024"], w["L0_xattn_cos"], w["L0_xattn_sin"], w["L0_xattn_ln_lat_g"], w["L0_xattn_ln_lat_b"],
                            w["L0_xattn_ln_ctx_g"], w["L0_xattn_ln_ctx_b"], w["L0_xattn_Wq"], w["L0_xattn_Wkv"], w["L0_xattn_Wo"],
                            w["L0_xattn_bo"])
        if until >= 3:
            x2_dram = nc.dram_tensor("x2", [P, NT, D], F32).ap()
            latent_attention(nc, sems, X, ident, x2_dram, w["L0_ffn_g1"], w["L0_ffn_Wq"], w["L0_ffn_Wdkv"], w["L0_ffn_Wuk"], w["L0_ffn_Wuv"], w["L0_ffn_Wo"])
        if until >= 4:
            comb_dram = nc.dram_tensor("comb", [NE, NT * P], F32).ap()
            experts(nc, sems, X, ident, x2_dram, w["L0_ffn_g2"], w["L0_ffn_gate_w"], w["L0_ffn_w1"], w["L0_ffn_w2"], comb_dram, out)
            return
        with nc.Block() as block:
            @block.sync
            def _(sp):
                sp.dma_start(out.rearrange("b (i p) d -> p (b i) d", p=P), X[:, 0:NT, :]).then_inc(stored, 16)
                sp.wait_ge(stored, 16)


_TRANSPOSED = ("L0_attn_w_q", "L0_attn_w_k", "L0_attn_w_v", "L0_attn_w_o")


def kernel(**inputs):
    import numpy as _np
    import concourse.bacc as _bacc
    from concourse import mybir as _mybir
    from concourse.bass_utils import run_bass_kernel_spmd as _run

    nc = _bacc.Bacc("TRN2", target_bir_lowering=False, num_devices=1)
    arrays, aps = {}, {}
    for name, a in inputs.items():
        a = _np.asarray(a)
        a = _np.ascontiguousarray(a.T if name in _TRANSPOSED else a)
        arrays[f"in_{name}"] = a
        aps[name] = nc.dram_tensor(f"in_{name}", a.shape, _mybir.dt.from_np(a.dtype), kind="ExternalInput").ap()
    out = nc.dram_tensor("out_x", (B, S, D), _mybir.dt.float32, kind="ExternalOutput").ap()
    program(nc, aps["x"], aps, out)
    r = _run(nc, [arrays], core_ids=[0])
    return r.results[0]["out_x"]
```

```python
from contextlib import ExitStack

import numpy as np
import concourse.bass as bass
from concourse import mybir

ALU = mybir.AluOpType
ACT = mybir.ActivationFunctionType
AX = mybir.AxisListType
F32 = mybir.dt.float32
F32R = mybir.dt.float32r
I32 = mybir.dt.int32
BF16 = mybir.dt.bfloat16

P = 128
B, S, D = 4, 512, 256
KD = D // P
TB = S // P
NT = B * TB
UP = 32
RSQRT_MAGIC = 0x5F3759DF


def as32(ap):
    return ap.bitcast(F32)


class Chain:

    def __init__(self, eng, sem):
        self.eng, self.sem, self.n, self.base = eng, sem, 0, 0

    def start(self, base):
        self.n, self.base = 0, base

    def step(self, ins):
        self.n += 1
        ins.then_inc(self.sem, 1)
        self.eng.wait_ge(self.sem, UP + self.base + self.n)


def rsqrt_guess(nc, ch, y, v, t):
    ch.step(nc.vector.tensor_scalar(t.bitcast(I32), v.bitcast(I32), 1, None, ALU.arith_shift_right))
    ch.step(nc.vector.tensor_scalar(y.bitcast(I32), t.bitcast(I32), -1.0, float(RSQRT_MAGIC), ALU.mult, ALU.add))


def rsqrt_newton(nc, ch, y, v, t, steps):
    for _ in range(steps):
        ch.step(nc.vector.tensor_tensor(t, y, y, ALU.mult))
        ch.step(nc.vector.scalar_tensor_tensor(t, t, -0.5, v, ALU.mult, ALU.mult))
        ch.step(nc.vector.scalar_tensor_tensor(y, t, 1.5, y, ALU.add, ALU.mult))


def newton_rsqrt(nc, ch, y, v, t, c_magic):
    rsqrt_guess(nc, ch, y, v, t)
    rsqrt_newton(nc, ch, y, v, t, 4)


RSQRT_STEPS = 2 + 3 * 4


class Semaphores:

    def __init__(self, nc, ctx, names):
        self.of = {n: ctx.enter_context(nc.semaphore(n)) for n in names}

    def raise_all(self, eng):
        for s in self.of.values():
            eng.sem_inc(s, UP)


class Scope:

    def __init__(self, nc, ctx, tag, sems):
        self.nc, self.ctx, self.tag, self.sems = nc, ctx, tag, sems

    def sb(self, name, shape, dt=F32):
        return self.ctx.enter_context(self.nc.sbuf_tensor(f"{self.tag}_{name}", shape, dt))

    def ps(self, name, shape, dt=F32):
        return self.ctx.enter_context(self.nc.psum_tensor(f"{self.tag}_{name}", shape, dt))

    def sem(self, name):
        return self.sems.of[f"{self.tag}_{name}"]

    def dma_sem(self, name):
        return self.ctx.enter_context(self.nc.semaphore(f"{self.tag}_{name}"))


def tile_of(x, t, n=1):
    return x[:, bass.ds(t, n), :]


def flat(ap):
    return ap.rearrange("p a n -> p (a n)")


def row_stats(nc, ch, tiles, st, mv, tmp):
    nc.vector.memset(tmp[:, 0:1], 0.0)
    for i, x in enumerate(tiles):
        last = nc.vector.bn_stats(st[:, i, :], x)
    ch.step(last)
    nc.vector.memset(tmp[:, 0:1], 0.0)
    for i, _ in enumerate(tiles):
        last = nc.vector.bn_aggr(mv[:, i, :], st[:, i, :])
    ch.step(last)


def layer_norm_stats(nc, ch, tiles, st, mv, rstd, tmp, eps):
    row_stats(nc, ch, tiles, st, mv, tmp)
    ch.step(nc.vector.tensor_scalar_add(mv[:, 0:len(tiles), 1], mv[:, 0:len(tiles), 1], eps))
    newton_rsqrt(nc, ch, rstd[:, 0:len(tiles)], mv[:, 0:len(tiles), 1], tmp[:, 0:len(tiles)], None)


LN_STEPS = 3 + RSQRT_STEPS


class Fills:

    def __init__(self, items):
        self.items = items
        self.no = {f: n for n, f in enumerate(items)}
        self.act = [(n + 1) // 2 for n in range(len(items) + 1)]
        self.dve = [n // 2 for n in range(len(items) + 1)]
        self.count = len(items)
        assert self.count % 2 == 0

    def by_act(self, f):
        return self.no[f] % 2 == 0


AH, AD = 4, 64
AG = 2 * AH
SA_SEMS = ("split_done", "dve_steps", "xn_ready", "xs_ready", "tp_full", "tp_free_act", "tp_free_dve", "qkv_full",
           "qkv_free", "stacked", "s_full", "max_ready", "exp_ready", "norm_ready", "av_done", "o_free", "y_full",
           "y_added", "v_ready", "later_split", "w_high")


def self_attention(nc, sems, X, ident, later, ctx_dram, w_kv, w_q, x_dram, ln_g, ln_b, q_g, k_g, wqT, wkT, wvT, woT, b_o):
    with ExitStack() as ctx:
        sc = Scope(nc, ctx, "sa", sems)
        w_hi = sc.sb("w_hi", [P, KD, 3 * D], F32R)
        w_lo = sc.sb("w_lo", [P, KD, 3 * D], F32R)
        wo = sc.sb("wo", [P, KD, D])
        g_in = sc.sb("g_in", [P, KD])
        b_in = sc.sb("b_in", [P, KD])
        gam = sc.sb("gam", [P, AG, AD])
        bo = sc.sb("bo", [P, D])
        st = sc.sb("st", [P, NT, 6])
        mv = sc.sb("mv", [P, NT, 2])
        rstd = sc.sb("rstd", [P, NT])
        tmp = sc.sb("tmp", [P, TB * AG])
        xn = sc.sb("xn", [P, TB, D])
        xT = sc.sb("xT", [P, KD, S])
        xh = sc.sb("xh", [P, KD, S], F32R)
        xl = sc.sb("xl", [P, KD, S], F32R)
        qk = sc.sb("qk", [P, TB, AG * AD])
        ss = sc.sb("ss", [P, TB * AG])
        rn = sc.sb("rn", [P, TB * AG])
        v = sc.sb("v", [P, TB, D])
        v_next = sc.sb("v_next", [P, TB, D])
        stk = sc.sb("stk", [P, TB, 3 * AH, P])
        stT = sc.sb("stT", [P, 3 * AH, S], F32R)
        nmx = sc.sb("nmx", [P, AH * TB])
        rs = sc.sb("rs", [P, AH * TB])
        ri = sc.sb("ri", [P, AH * TB])
        prob = sc.sb("prob", [P, 8, S])
        sq = stk[:, :, 0:AG // 2, :].rearrange("p i a n -> p i (a n)")
        w_st = prob[:, 0:3, :].rearrange("p a n -> p (a n)").rearrange("p (k n) -> p k n", k=KD)
        pT = sc.sb("pT", [P, 2, TB, S])
        oT = sc.sb("oT", [P, KD, S])
        p_tp = sc.ps("p_tp", [P, 2, S])
        p_s = sc.ps("p_s", [P, 3, S])
        p_qk = sc.ps("p_qk", [P, S])
        p_v = sc.ps("p_v", [P, S])
        p_o = sc.ps("p_o", [P, S])

        loaded, x0_loaded, x_loaded, later_loaded = sc.dma_sem("loaded"), sc.dma_sem("x0_loaded"), sc.dma_sem("x_loaded"), sc.dma_sem("later_loaded")
        later_split = sc.sem("later_split")
        w_high, split_done = sc.sem("w_high"), sc.sem("split_done")
        dve_steps = sc.sem("dve_steps")
        xn_ready, xs_ready = sc.sem("xn_ready"), sc.sem("xs_ready")
        tp_full, tp_free_act, tp_free_dve = sc.sem("tp_full"), sc.sem("tp_free_act"), sc.sem("tp_free_dve")
        qkv_full, qkv_free = sc.sem("qkv_full"), sc.sem("qkv_free")
        stacked = sc.sem("stacked")
        s_full, max_ready, exp_ready, norm_ready = (sc.sem(n) for n in ("s_full", "max_ready", "exp_ready", "norm_ready"))
        av_done, o_free = sc.sem("av_done"), sc.sem("o_free")
        y_full, y_added, v_ready = sc.sem("y_full"), sc.sem("y_added"), sc.sem("v_ready")

        N_ST = 3 * AH
        UN = AH * TB
        TURN_AT = [(h + 1) * TB + 1 for h in range(AH)]
        T_AT, QKV_AT = 0, 3
        turns = {TURN_AT[h]: [("P", h, j) for j in range(TB)] for h in range(AH)}
        next_fills = {T_AT: [("T", k) for k in range(KD)], UN: [("ST", n) for n in range(6)],
                      UN + 2: [("ST", n) for n in range(6, N_ST)]}
        first = Fills([f for u in sorted(next_fills) for f in next_fills[u]])
        steady = Fills([f for u in range(UN + 3) for f in turns.get(u, []) + next_fills.get(u, [])])
        final = Fills([f for u in range(UN + 3) for f in turns.get(u, [])])

        def counts(b, more):
            p = steady if more else final
            return p, first.count + b * steady.count, first.act[-1] + b * steady.act[-1], first.dve[-1] + b * steady.dve[-1]

        START = (first, 0, 0, 0)

        block = ctx.enter_context(nc.Block())

        @block.sync
        def _(sp):
            x_tiles = x_dram.rearrange("b (i p) d -> p (b i) d", p=P)
            sp.dma_start(X[:, 0:TB, :], x_tiles[:, 0:TB, :]).then_inc(x0_loaded, 16)
            for n, w in enumerate((wqT, wkT, wvT)):
                sp.dma_start(w_st[:, :, n * D:(n + 1) * D], w.rearrange("(k p) n -> p k n", p=P)).then_inc(loaded, 16)
            sp.dma_start(X[:, TB:NT, :], x_tiles[:, TB:NT, :]).then_inc(x_loaded, 16)
            sp.dma_start(wo[:, :, :], woT.rearrange("(k p) n -> p k n", p=P)).then_inc(loaded, 16)
            with nc.allow_non_contiguous_dma("small vectors"):
                sp.dma_start(g_in[:, :], ln_g.rearrange("(k p) -> p k", p=P)).then_inc(loaded, 16)
                sp.dma_start(b_in[:, :], ln_b.rearrange("(k p) -> p k", p=P)).then_inc(loaded, 16)
            for h in range(AG):
                g = q_g if h < AH else k_g
                sp.dma_start(gam[:, h, :], g.unsqueeze(0).broadcast_to([P, AD])).then_inc(loaded, 16)
            sp.dma_start(bo[:, :], b_o.unsqueeze(0).broadcast_to([P, D])).then_inc(loaded, 16)
            for n in range(3):
                if n > 0:
                    sp.wait_ge(later_split, UP + 2 * n)
                if n < KD:
                    for j in range(2):
                        rows = w_kv[n * P:(n + 1) * P, j * XH * XD:(j + 1) * XH * XD]
                        sp.dma_start(later.staged.rearrange("p (a n) -> p a n", a=XP)[:, :, j * P:(j + 1) * P],
                                     rows.rearrange("p (a n) -> p a n", a=XP)).then_inc(later_loaded, 16)
                else:
                    sp.dma_start(later.staged.rearrange("p (k n) -> p k n", k=KD), w_q.rearrange("(k p) n -> p k n", p=P)).then_inc(later_loaded, 16)
            sp.wait_ge(later_split, UP + 6)
            sp.dma_start(later.cx[:, :, :], ctx_dram[0].rearrange("(t p) d -> p t d", p=P)).then_inc(later_loaded, 16)
            sp.wait_ge(later_loaded, 32 * KD + 32)
        LOADS = 16 * (7 + AG)

        @block.gpsimd
        def _(pool):
            pool.wait_ge(w_high, UP + 1)
            nc.gpsimd.tensor_tensor(w_lo[:, :, :], w_st, as32(w_hi[:, :, :]), ALU.subtract).then_inc(split_done, 1)
            parts = [(later.wkv_hi[:, k, :, :], later.wkv_lo[:, k, :, :], later.staged.rearrange("p (a n) -> p a n", a=XP)) for k in range(KD)]
            parts += [(later.wq[:, 0, :, :], later.wq[:, 1, :, :], later.staged.rearrange("p (k n) -> p k n", k=KD))]
            for n, (high, low, whole) in enumerate(parts):
                pool.wait_ge(later_loaded, 32 * (n + 1) if n < KD else 32 * KD + 16)
                nc.gpsimd.tensor_copy(high, whole).then_inc(later_split, 1)
                pool.wait_ge(later_split, UP + 2 * n + 1)
                nc.gpsimd.tensor_tensor(low, whole, as32(high), ALU.subtract).then_inc(later_split, 1)

        @block.tensor
        def _(pe):
            def fill(c, f):
                plan, _, act0, dve0 = c
                n = plan.no[f]
                pe.wait_ge(tp_free_act, UP + act0 + plan.act[max(n - 1, 0)])
                pe.wait_ge(tp_free_dve, UP + dve0 + plan.dve[max(n - 1, 0)])
                return p_tp[:, n % 2, :]

            def emptied(c, f):
                plan, _, act0, dve0 = c
                n = plan.no[f]
                pe.wait_ge(tp_free_act, UP + act0 + plan.act[n + 1])
                pe.wait_ge(tp_free_dve, UP + dve0 + plan.dve[n + 1])

            def turn(c, f, b):
                if f == ("T", 0):
                    pe.wait_ge(xn_ready, UP + b + 1)
                if f == ("ST", 0):
                    pe.wait_ge(stacked, UP + b + 1)
                if f[0] == "P" and f[2] == 0:
                    pe.wait_ge(norm_ready, UP + b * UN + (f[1] + 1) * TB)
                bank = fill(c, f)
                for i in range(TB):
                    if f[0] == "T":
                        src = xn[:, i, f[1] * P:(f[1] + 1) * P]
                    elif f[0] == "ST":
                        src = stk[:, i, f[1], :]
                    else:
                        src = prob[:, (f[1] * TB + i) % 8, f[2] * P:(f[2] + 1) * P]
                    last = nc.tensor.transpose(bank[:, i * P:(i + 1) * P], src, ident[:, :])
                last.then_inc(tp_full, 1)

            def qkv(i, b):
                if i == 0:
                    pe.wait_ge(xs_ready, UP + b + 1)
                pe.wait_ge(qkv_free, UP + b * TB + i)
                for out, c0, n in ((p_qk, 0, 2 * D), (p_v, 2 * D, D)):
                    steps = [(x, w, k) for x, w in ((xh, w_hi), (xh, w_lo), (xl, w_hi)) for k in range(KD)]
                    for j, (x, w, k) in enumerate(steps):
                        last = nc.tensor.matmul(out[:, 0:n], x[:, k, i * P:(i + 1) * P], w[:, k, c0:c0 + n],
                                                start=(j == 0), stop=(j == len(steps) - 1))
                last.then_inc(qkv_full, 1)

            def attention(b, more):
                c = counts(b, more)

                def scores(u):
                    h, i = divmod(u, TB)
                    pe.wait_ge(exp_ready, UP + b * UN + u - 2)
                    if u == 2:
                        pe.wait_ge(y_added, UP + b)
                    nc.tensor.matmul(p_s[:, u % 3, :], stT[:, AH + h, i * P:(i + 1) * P], stT[:, h, :], start=True, stop=False)
                    nc.tensor.matmul(p_s[:, u % 3, :], stT[:, 2 * AH + h, i * P:(i + 1) * P], stT[:, h, :],
                                     start=False, stop=True).then_inc(s_full, 1)

                def values(h):
                    emptied(c, ("P", h, TB - 1))
                    if h == 0:
                        pe.wait_ge(v_ready, UP + b + 1)
                        pe.wait_ge(y_added, UP + b)
                    if h % 2 == 0:
                        pe.wait_ge(o_free, UP + b * KD + h // 2)
                    r = (h % 2) * AD
                    for j in range(TB):
                        last = nc.tensor.matmul(p_o[r:r + AD, :], v[:, j, h * AD:(h + 1) * AD], pT[:, h % 2, j, :],
                                                start=(j == 0), stop=(j == TB - 1))
                    last.then_inc(av_done, 1)

                scores(0)
                for u in range(UN + 3):
                    if u + 1 < UN:
                        scores(u + 1)
                    for f in turns.get(u, []):
                        turn(c, f, b)
                    if more:
                        for f in next_fills.get(u, []):
                            turn(c, f, b + 1)
                        if QKV_AT <= u < QKV_AT + TB:
                            qkv(u - QKV_AT, b + 1)
                    if u - 1 in TURN_AT:
                        values(TURN_AT.index(u - 1))
                pe.wait_ge(o_free, UP + b * KD + KD)
                for i in range(TB):
                    bank = (p_s[:, 2, :], p_o)[i // 2]
                    cols = slice((i % 2) * D, (i % 2 + 1) * D)
                    for k in range(KD):
                        last = nc.tensor.matmul(bank[:, cols], oT[:, k, i * P:(i + 1) * P], wo[:, k, :], start=(k == 0), stop=(k == KD - 1))
                    last.then_inc(y_full, 1)
                if more:
                    emptied(c, ("ST", N_ST - 1))

            for f in first.items[0:KD]:
                turn(START, f, 0)
            pe.wait_ge(split_done, UP + 1)
            for i in range(TB):
                qkv(i, 0)
            for f in first.items[KD:]:
                turn(START, f, 0)
            emptied(START, ("ST", N_ST - 1))
            with pe.Fori(0, B - 1) as b:
                attention(b, True)
            attention(B - 1, False)

        @block.scalar
        def _(act):
            def out_of_bank(c, f, b):
                plan, fills0, _, _ = c
                if not plan.by_act(f):
                    return
                n = plan.no[f]
                act.wait_ge(tp_full, UP + fills0 + n + 1)
                bank = p_tp[:, n % 2, :]
                if f[0] == "T":
                    ins = nc.scalar.activation(xT[:, 0, :], bank, ACT.Identity, bias=b_in[:, 0:1], scale=g_in[:, 0:1])
                elif f[0] == "ST":
                    act.wait_ge(s_full, UP + b * UN)
                    ins = nc.scalar.activation(stT[:, f[1], :], bank, ACT.Copy)
                else:
                    act.wait_ge(av_done, UP + b * AH + f[1] - 1)
                    ins = nc.scalar.activation(pT[:, f[1] % 2, f[2], :], bank, ACT.Copy)
                ins.then_inc(tp_free_act, 1)

            def qkv_out(i, b):
                act.wait_ge(qkv_full, UP + b * TB + i + 1)
                if i == 0:
                    act.wait_ge(stacked, UP + b)
                    act.wait_ge(v_ready, UP + b)
                nc.scalar.activation(sq[:, i, :], p_qk[:, :], ACT.Square)
                nc.scalar.activation(qk[:, i, :], p_qk[:, :], ACT.Copy)
                nc.scalar.activation(v_next[:, i, :], p_v[:, 0:D], ACT.Copy).then_inc(qkv_free, 1)

            def next_v(b):
                act.wait_ge(qkv_free, UP + b * TB + TB)
                nc.scalar.activation(v[:, :, :], v_next[:, :, :], ACT.Copy).then_inc(v_ready, 1)

            def attention(b, more):
                c = counts(b, more)

                def pair_out(k):
                    act.wait_ge(av_done, UP + b * AH + 2 * k + 2)
                    act.wait_ge(y_full, UP + b * TB)
                    nc.scalar.activation(oT[:, k, :], p_o[:, :], ACT.Copy).then_inc(o_free, 1)

                for u in range(UN + 3):
                    if u < UN:
                        act.wait_ge(max_ready, UP + b * UN + u + 1)
                        act.wait_ge(av_done, UP + b * AH + u // TB - 2)
                        nc.scalar.activation(prob[:, u % 8, :], p_s[:, u % 3, :], ACT.Exp, bias=nmx[:, u:u + 1],
                                             accum_out=rs[:, u:u + 1]).then_inc(exp_ready, 1)
                    for f in turns.get(u, []):
                        out_of_bank(c, f, b)
                    if more:
                        for f in next_fills.get(u, []):
                            out_of_bank(c, f, b + 1)
                        if QKV_AT <= u < QKV_AT + TB:
                            qkv_out(u - QKV_AT, b + 1)
                    if u - 2 == TURN_AT[1]:
                        pair_out(0)
                pair_out(AH // 2 - 1)
                if more:
                    next_v(b + 1)

            act.wait_ge(loaded, LOADS)
            nc.scalar.activation(w_hi[:, :, :], w_st, ACT.Copy).then_inc(w_high, 1)
            for f in first.items[0:KD]:
                out_of_bank(START, f, 0)
            for i in range(TB):
                qkv_out(i, 0)
            next_v(0)
            for f in first.items[KD:]:
                out_of_bank(START, f, 0)
            with act.Fori(0, B - 1) as b:
                attention(b, True)
            attention(B - 1, False)

        @block.vector
        def _(dve):
            ch = Chain(dve, dve_steps)

            def out_of_bank(c, f, b):
                plan, fills0, _, _ = c
                if plan.by_act(f):
                    return
                n = plan.no[f]
                dve.wait_ge(tp_full, UP + fills0 + n + 1)
                bank = p_tp[:, n % 2, :]
                if f[0] == "T":
                    ins = nc.vector.tensor_scalar(xT[:, 1, :], bank, g_in[:, 1:2], b_in[:, 1:2], ALU.mult, ALU.add)
                elif f[0] == "ST":
                    dve.wait_ge(s_full, UP + b * UN)
                    ins = nc.vector.tensor_copy(stT[:, f[1], :], bank)
                else:
                    dve.wait_ge(av_done, UP + b * AH + f[1] - 1)
                    ins = nc.vector.tensor_copy(pT[:, f[1] % 2, f[2], :], bank)
                ins.then_inc(tp_free_dve, 1)

            def in_stats(t0, t1):
                layer_norm_stats(nc, ch, [X[:, t, :] for t in range(t0, t1)], st, mv[:, t0:t1, :], rstd[:, t0:t1], tmp, 1e-5)

            def normalised(b):
                for i in range(TB):
                    last = nc.vector.tensor_scalar(xn[:, i, :], flat(tile_of(X, b * TB + i)), flat(tile_of(mv, b * TB + i))[:, 0:1],
                                                   rstd[:, bass.ds(b * TB + i, 1)], ALU.subtract, ALU.mult)
                last.then_inc(xn_ready, 1)

            def split_rows(c):
                plan, _, act0, dve0 = c
                n = plan.no[("T", KD - 1)] + 1
                dve.wait_ge(tp_free_act, UP + act0 + plan.act[n])
                dve.wait_ge(tp_free_dve, UP + dve0 + plan.dve[n])
                ch.step(nc.vector.tensor_copy(xh[:, :, :], xT[:, :, :]))
                nc.vector.tensor_tensor(xl[:, :, :], xT[:, :, :], as32(xh[:, :, :]), ALU.subtract).then_inc(xs_ready, 1)

            def square_sums(i, b):
                dve.wait_ge(qkv_free, UP + b * TB + i + 1)
                last = nc.vector.reduce_sum(ss[:, i * AG:(i + 1) * AG], sq[:, i, :].rearrange("p (g d) -> p g d", d=AD), AX.X)
                if i == TB - 1:
                    ch.step(last)

            def rms():
                ch.step(nc.vector.tensor_scalar(ss[:, :], ss[:, :], 1.0 / AD, 1e-16, ALU.mult, ALU.max))
                newton_rsqrt(nc, ch, rn[:, :], ss[:, :], tmp[:, :], None)

            q4 = qk[:, :, 0:AH * AD].rearrange("p i (h d) -> p i h d", d=AD)
            k4 = qk[:, :, AH * AD:2 * AH * AD].rearrange("p i (h d) -> p i h d", d=AD)
            kh, kl = stk[:, :, 0:AH, 0:AD], stk[:, :, 0:AH, AD:P]
            qh, qh2 = stk[:, :, AH:2 * AH, 0:AD], stk[:, :, AH:2 * AH, AD:P]
            ql, ql2 = stk[:, :, 2 * AH:3 * AH, 0:AD], stk[:, :, 2 * AH:3 * AH, AD:P]

            def scale_heads():
                heads = qk[:, :, :].rearrange("p i (g d) -> p (i g) d", d=AD)
                ch.step(nc.vector.tensor_tensor(heads, heads, rn[:, :].unsqueeze(2).broadcast_to([P, TB * AG, AD]), ALU.mult))

            def gains():
                ch.step(nc.vector.tensor_tensor(qk[:, :, :], qk[:, :, :],
                                                gam[:, :, :].rearrange("p g d -> p (g d)").unsqueeze(1).broadcast_to([P, TB, AG * AD]), ALU.mult))

            def stack_high():
                nc.vector.tensor_copy(kh.bitcast(F32R), k4)
                ch.step(nc.vector.tensor_copy(qh.bitcast(F32R), q4))

            def stack_low():
                nc.vector.tensor_tensor(kl, k4, kh, ALU.subtract)
                ch.step(nc.vector.tensor_tensor(ql, q4, qh, ALU.subtract))

            def stack_twice():
                nc.vector.tensor_copy(qh2, qh)
                nc.vector.tensor_copy(ql2, ql).then_inc(stacked, 1)

            def add_bias(t0, t1):
                ch.step(nc.vector.tensor_tensor(X[:, t0:t1, :], X[:, t0:t1, :], bo[:, :].unsqueeze(1).broadcast_to([P, t1 - t0, D]), ALU.add))

            def out_stats(t0, t1):
                layer_norm_stats(nc, ch, [X[:, t, :] for t in range(t0, t1)], st, mv, rstd, tmp, 1e-5)

            def out_norm(t0, t1):
                for t in range(t0, t1):
                    last = nc.vector.tensor_scalar(X[:, t, :], X[:, t, :], mv[:, t - t0, 0:1], rstd[:, t - t0:t - t0 + 1], ALU.subtract, ALU.mult)
                ch.step(last)

            def attention(b, more):
                c = counts(b, more)
                DONE = NT - TB

                def norm(u):
                    dve.wait_ge(exp_ready, UP + b * UN + u + 1)
                    ch.step(nc.vector.reciprocal(ri[:, u:u + 1], rs[:, u:u + 1]))
                    nc.vector.tensor_scalar(prob[:, u % 8, :], prob[:, u % 8, :], ri[:, u:u + 1], None, ALU.mult).then_inc(norm_ready, 1)

                for u in range(UN + 3):
                    if u < UN:
                        dve.wait_ge(s_full, UP + b * UN + u + 1)
                        nc.vector.tensor_reduce(nmx[:, u:u + 1], p_s[:, u % 3, :], AX.X, ALU.max, negate=True).then_inc(max_ready, 1)
                    if 1 <= u <= UN:
                        norm(u - 1)
                    for f in turns.get(u, []):
                        out_of_bank(c, f, b)
                    if more:
                        if u == T_AT:
                            normalised(b + 1)
                        for f in next_fills.get(u, []):
                            out_of_bank(c, f, b + 1)
                        if u == T_AT + 1:
                            split_rows(c)
                        if QKV_AT < u <= QKV_AT + TB:
                            square_sums(u - QKV_AT - 1, b + 1)
                        if u == QKV_AT + TB + 1:
                            rms()
                        if u == QKV_AT + TB + 2:
                            scale_heads()
                        if u == QKV_AT + TB + 3:
                            gains()
                        if u == QKV_AT + TB + 4:
                            stack_high()
                        if u == QKV_AT + TB + 5:
                            stack_low()
                        if u == QKV_AT + TB + 6:
                            stack_twice()
                    else:
                        if u == 2:
                            add_bias(0, DONE)
                        if u == 4:
                            out_stats(0, DONE)
                        if u == 7:
                            out_norm(0, DONE)
                for i in range(TB):
                    dve.wait_ge(y_full, UP + b * TB + i // 2 * 2 + 2)
                    xi = flat(tile_of(X, b * TB + i))
                    bank = (p_s[:, 2, :], p_o)[i // 2]
                    last = nc.vector.tensor_tensor(xi, bank[:, (i % 2) * D:(i % 2 + 1) * D], xi, ALU.add)
                last.then_inc(y_added, 1)
                dve.wait_ge(y_added, UP + b + 1)

            dve.wait_ge(x0_loaded, 16)
            ch.start(0)
            in_stats(0, TB)
            BEFORE = ch.n
            normalised(0)
            dve.wait_ge(loaded, LOADS)
            for f in first.items[0:KD]:
                out_of_bank(START, f, 0)
            split_rows(START)
            dve.wait_ge(x_loaded, 16)
            in_stats(TB, NT)
            for i in range(TB):
                square_sums(i, 0)
            ch.step(nc.vector.tensor_scalar(gam[:, 0:AH, :], gam[:, 0:AH, :], AD ** -0.5, None, ALU.mult))
            rms()
            scale_heads()
            gains()
            stack_high()
            stack_low()
            stack_twice()
            for f in first.items[KD:]:
                out_of_bank(START, f, 0)
            first_steps, loop_steps = ch.n, ch.n - BEFORE - 1 - LN_STEPS + UN
            with dve.Fori(0, B - 1) as b:
                ch.start(first_steps + b * loop_steps)
                attention(b, True)
                assert ch.n == loop_steps, (ch.n, loop_steps)
            ch.start(first_steps + (B - 1) * loop_steps)
            attention(B - 1, False)
            add_bias(NT - TB, NT)
            out_stats(NT - TB, NT)
            out_norm(NT - TB, NT)


XH, XD = 16, 64
XP = XH // 2
SC = 1024
CT = SC // P
PC = CT
CLIP = 11.0


XA_SEMS = ("cx_used", "dve_steps", "normed", "xs_ready", "bg_full", "bg_act", "bg_dve", "rot_ready",
           "kr_ready", "khi_ready", "stk_ready", "pool_steps", "s_full", "exp_ready", "clipped", "y_added", "added",
           "sum_full", "sum_used", "av_done", "c_high", "o_out", "oT_ready", "y_full")
XA_DMA_SEMS = ("c_loaded", "cx_loaded")


class CrossWeights:

    def __init__(self, nc, ctx, sems):
        sc = Scope(nc, ctx, "xw", sems)
        self.wq = sc.sb("wq", [P, 2, KD, XH * XD], F32R)
        self.wkv_hi = sc.sb("wkv_hi", [P, KD, XP, 2 * P], F32R)
        self.wkv_lo = sc.sb("wkv_lo", [P, KD, XP, 2 * P], F32R)
        self.cx = sc.sb("cx", [P, CT, D])
        self.staged = flat(self.cx[:, :, :])


def cross_attention(nc, sems, X, ident, weights, ctx_dram, cos, sin, lat_g, lat_b, ctx_g, ctx_b, w_o, b_o):
    with ExitStack() as ctx:
        sc = Scope(nc, ctx, "xa", sems)
        wq, wkv_hi, wkv_lo, cx = weights.wq, weights.wkv_hi, weights.wkv_lo, weights.cx
        wqd = sc.sb("wqd", [P, 2, 2 * KD, P], F32R)
        wo = sc.sb("wo", [P, XP, D])
        g_in = sc.sb("g_in", [P, 2, KD])
        b_in = sc.sb("b_in", [P, 2, KD])
        bo = sc.sb("bo", [P, D])
        c2 = sc.sb("c2", [P, CT, XD])
        s2 = sc.sb("s2", [P, CT, XD])
        ones = sc.sb("ones", [P, XD])
        NL = max(CT + TB, NT)
        st = sc.sb("st", [P, NL, 6])
        mv = sc.sb("mv", [P, NL, 2])
        rstd = sc.sb("rstd", [P, NL])
        tmp = sc.sb("tmp", [P, NL])
        cT_hi = sc.sb("cT_hi", [P, KD, SC], F32R)
        cT_lo = sc.sb("cT_lo", [P, KD, SC], F32R)
        lT_hi = sc.sb("lT_hi", [P, KD, S], F32R)
        lT_lo = sc.sb("lT_lo", [P, KD, S], F32R)
        kv = sc.sb("kv", [P, 2, CT, 2 * P])
        t12 = sc.sb("t12", [P, 2, 4, 2, XD])
        t1, t2 = t12[:, 0, :, :, :], t12[:, 1, :, :, :]
        stk = sc.sb("stk", [P, CT, 2, P])
        kT = sc.sb("kT", [P, 2, SC], F32R)
        qT = sc.sb("qT", [P, 2, 2, 2, S], F32R)
        ex = sc.sb("ex", [P, 4, 2, S])
        acc = sc.sb("acc", [P, 2, S])
        rcp = sc.sb("rcp", [P, S])
        oT = sc.sb("oT", [P, XP, S])
        cT = stk[:, :, :, :].rearrange("p t h n -> p (t h n)").rearrange("p (k n) -> p k n", k=KD)
        lT = kv[:, 0, :, :].rearrange("p t n -> p (t n)")[:, 0:KD * S].rearrange("p (k n) -> p k n", k=KD)
        ln = t12[:, :, :, :, :].rearrange("p a t h d -> p (a t h d)").rearrange("p (i d) -> p i d", d=D)

        p_s = sc.ps("p_s", [P, 2, 2, S])
        p_o = sc.ps("p_o", [P, S])
        p_sum = sc.ps("p_sum", [P, S])
        p_bg = sc.ps("p_bg", [P, 2, S])

        m = {n: sc.sem(n) for n in XA_SEMS} | {n: sc.dma_sem(n) for n in XA_DMA_SEMS}
        wqd_loaded = [sc.dma_sem(f"wqd_loaded{i}") for i in range(2)]

        FIRST_T = 6
        first_fills = [("T", i) for i in range(6)] + [("KV", 0, i) for i in range(4)] + [("Q", 0), ("Q", 1), ("KT", 0, 0), ("KT", 1, 0)]
        slot_fills = {}
        for p in range(XP):
            a, nx = p * PC, p + 1
            slot_fills[a] = [("KT", 2 * p, 1), ("KT", 2 * p + 1, 1)]
            if nx < XP:
                slot_fills[a + 1] = [("KV", nx, 0), ("KV", nx, 1)]
                slot_fills[a + 2] = [("KV", nx, 2), ("KV", nx, 3)]
                slot_fills[a + 3] = [("Q", 2 * nx), ("Q", 2 * nx + 1)]
                slot_fills[a + 6] = [("KT", 2 * nx, 0)]
                slot_fills[a + 7] = [("KT", 2 * nx + 1, 0)]
        NU = XP * PC
        LAST = NU - PC
        next_fills = {LAST + 1: first_fills[0:2], LAST + 2: first_fills[2:4], LAST + 3: first_fills[4:6],
                      LAST + 6: first_fills[6:8], LAST + 7: first_fills[8:10], LAST + 8: first_fills[10:12]}
        order = list(first_fills)
        for u in range(NU):
            order += slot_fills.get(u, [])
        NF = len(order)
        by_act = lambda f: f[0] == "KV" or f[0] == "Q" or f[0] == "KT" or (f[0] == "T" and f[1] % 2 == 0)
        by_dve = lambda f: f[0] == "Q" or (f[0] == "T" and f[1] % 2 == 1)
        no = {f: i for i, f in enumerate(order)}
        act_by = [sum(map(by_act, order[:i + 1])) for i in range(NF)]
        dve_by = [sum(map(by_dve, order[:i + 1])) for i in range(NF)]
        NA, NV = act_by[-1], dve_by[-1]
        assert NF % 2 == 0

        ROTATE_AT, K_HIGH_AT = (2, 4), (4, 7)

        block = ctx.enter_context(nc.Block())

        @block.sync
        def _(sp):
            with nc.allow_non_contiguous_dma("small vectors"):
                for n, (g, bb) in enumerate(((ctx_g, ctx_b), (lat_g, lat_b))):
                    sp.dma_start(g_in[:, n, :], g.rearrange("(k p) -> p k", p=P)).then_inc(m["c_loaded"], 16)
                    sp.dma_start(b_in[:, n, :], bb.rearrange("(k p) -> p k", p=P)).then_inc(m["c_loaded"], 16)
                for j in range(2):
                    sp.dma_start(c2[:, :, j * 32:(j + 1) * 32], cos.rearrange("(t p) d -> p t d", p=P)).then_inc(m["c_loaded"], 16)
                    sp.dma_start(s2[:, :, j * 32:(j + 1) * 32], sin.rearrange("(t p) d -> p t d", p=P)).then_inc(m["c_loaded"], 16)
            sp.dma_start(wo[:, :, :], w_o.rearrange("(k p) n -> p k n", p=P)).then_inc(m["c_loaded"], 16)
            sp.dma_start(bo[:, :], b_o.unsqueeze(0).broadcast_to([P, D])).then_inc(m["c_loaded"], 16)

            def query_weights(b, prefetch):
                for h in range(XH):
                    sp.wait_ge(m["bg_full"], UP + b * NF + (no[("Q", h - 2)] if h >= 2 else no[("Q", XH + h - 2)] - NF) + 1)
                    for j in range(2):
                        sp.dma_start(as32(wqd[:, h % 2, :, j * XD:(j + 1) * XD]),
                                     as32(wq[:, :, :, h * XD:(h + 1) * XD].rearrange("p a k n -> p (a k) n"))).then_inc(wqd_loaded[h % 2], 16)
                    if prefetch and h == 2:
                        sp.wait_ge(m["cx_used"], UP + b + 1)
                        sp.dma_start(cx[:, :, :], ctx_dram[bass.ds(b + 1, 1), :, :].rearrange("b (t p) d -> p (b t) d", p=P))\
                            .then_inc(m["cx_loaded"], 16)

            with sp.Fori(0, B - 1) as b:
                query_weights(b, True)
            query_weights(B - 1, False)
        C_LOADS = 16 * 10

        @block.gpsimd
        def _(pool):
            nc.gpsimd.memset(ones[:, :], 1.0).then_inc(m["pool_steps"], 1)
            ROPES = 2 * XP
            with pool.Fori(0, B) as b:
                for r in range(ROPES):
                    p, q = divmod(r, 2)
                    pool.wait_ge(m["rot_ready"], UP + b * ROPES + r + 1)
                    nc.gpsimd.tensor_tensor(t1[:, :, :, 0:32], t1[:, :, :, 0:32], t2[:, :, :, 32:64], ALU.add)
                    nc.gpsimd.tensor_tensor(t1[:, :, :, 32:64], t1[:, :, :, 32:64], t2[:, :, :, 0:32], ALU.add).then_inc(m["kr_ready"], 1)
                    pool.wait_ge(m["khi_ready"], UP + b * ROPES + r + 1)
                    pool.wait_ge(m["kr_ready"], UP + b * ROPES + r + 1)
                    t = slice(4 * q, 4 * q + 4)
                    nc.gpsimd.tensor_tensor(stk[:, t, :, XD:P], t1[:, :, :, :], stk[:, t, :, 0:XD], ALU.subtract)\
                        .then_inc(m["stk_ready"], 1)

        ROPES = 2 * XP

        @block.tensor
        def _(pe):
            pe.wait_ge(m["pool_steps"], UP + 1)

            def fill(f, b):
                n = no[f]
                pe.wait_ge(m["bg_act"], UP + b * NA + (act_by[n - 2] if n >= 2 else act_by[NF + n - 2] - NA))
                pe.wait_ge(m["bg_dve"], UP + b * NV + (dve_by[n - 2] if n >= 2 else dve_by[NF + n - 2] - NV))
                return p_bg[:, n % 2, :]

            def product(out, x, w, halves):
                steps = [(x[i], w[j], k) for i, j in halves for k in range(KD)]
                for n, (xx, ww, k) in enumerate(steps):
                    last = nc.tensor.matmul(out, xx(k), ww(k), start=(n == 0), stop=(n == len(steps) - 1))
                return last

            def background(f, b):
                out = fill(f, b)
                if f == ("T", 0):
                    pe.wait_ge(m["normed"], UP + b + 1)
                if f == ("KV", 0, 0):
                    pe.wait_ge(m["xs_ready"], UP + b + 1)
                if f[0] == "T":
                    i = f[1]
                    for j in range(4):
                        if i < 4:
                            k, t = divmod(4 * i + j, CT)
                            src = cx[:, t, k * P:(k + 1) * P]
                        else:
                            src = ln[:, j, (i - 4) * P:(i - 3) * P]
                        last = nc.tensor.transpose(out[:, j * P:(j + 1) * P], src, ident[:, :])
                elif f[0] == "KV":
                    _, p, i = f
                    for j in range(2):
                        t = 2 * i + j
                        last = product(out[:, j * 2 * P:(j + 1) * 2 * P],
                                       [lambda k, x=x, t=t: x[:, k, t * P:(t + 1) * P] for x in (cT_hi, cT_lo)],
                                       [lambda k, w=w: w[:, k, p, :] for w in (wkv_hi, wkv_lo)], ((0, 0), (0, 1), (1, 0)))
                elif f[0] == "Q":
                    h = f[1]
                    pe.wait_ge(wqd_loaded[h % 2], b * 32 * XP + 32 * (h // 2 + 1))
                    last = product(out, [lambda k, i=i: wqd[:, h % 2, i * KD + k, :] for i in range(2)],
                                   [lambda k, x=x: x[:, k, :] for x in (lT_hi, lT_lo)], ((0, 0), (0, 1), (1, 0)))
                else:
                    _, h, q = f
                    pe.wait_ge(m["stk_ready"], UP + b * ROPES + h // 2 * 2 + q + 1)
                    for j in range(4):
                        last = nc.tensor.transpose(out[:, j * P:(j + 1) * P], stk[:, 4 * q + j, h % 2, :], ident[:, :])
                last.then_inc(m["bg_full"], 1)

            def batch(b, more):
                def scores(u):
                    p, c = divmod(u, PC)
                    if c in (0, PC // 2):
                        n = max(no[("KT", 2 * p + 1, c // (PC // 2))], no[("Q", 2 * p + 1)])
                        pe.wait_ge(m["bg_act"], UP + b * NA + act_by[n])
                        pe.wait_ge(m["bg_dve"], UP + b * NV + dve_by[n])
                    if u == 0:
                        pe.wait_ge(m["y_added"], UP + b)
                    pe.wait_ge(m["exp_ready"], UP + b * NU + u - 1)
                    for j in range(2):
                        for half in range(2):
                            last = nc.tensor.matmul(p_s[:, u % 2, j, :], kT[:, j, c * P:(c + 1) * P], qT[:, p % 2, j, half, :],
                                                    start=(half == 0), stop=(half == 1))
                    last.then_inc(m["s_full"], 1)

                def values(u):
                    p, c = divmod(u, PC)
                    pe.wait_ge(m["clipped"], UP + b * NU + u + 1)
                    if c == 0:
                        pe.wait_ge(m["o_out"], UP + b * XP + p)
                    for j in range(2):
                        last = nc.tensor.matmul(p_o[j * XD:(j + 1) * XD, :], kv[:, p % 2, c, P + j * XD:P + (j + 1) * XD], ex[:, u % 4, j, :],
                                                start=(c == 0), stop=(c == PC - 1))
                    last.then_inc(m["av_done"], 1)

                def sums(p):
                    pe.wait_ge(m["added"], UP + (b * XP + p + 1) * (PC - 1))
                    pe.wait_ge(m["sum_used"], UP + b * 2 * XP + 2 * p)
                    for j in range(2):
                        last = nc.tensor.matmul(p_sum[j * XD:(j + 1) * XD, :], ones[:, :], acc[:, j, :], start=True, stop=True)
                    last.then_inc(m["sum_full"], 1)

                for u in range(NU + 2):
                    if u < NU:
                        scores(u)
                    if u >= 2:
                        values(u - 2)
                    for f in slot_fills.get(u, []):
                        background(f, b)
                    if u % PC == 0 and u > 0:
                        sums(u // PC - 1)
                    if more:
                        for f in next_fills.get(u, []):
                            background(f, b + 1)
                pe.wait_ge(m["exp_ready"], UP + b * NU + NU)
                for ks in (range(XP - 1), range(XP - 1, XP)):
                    if more and ks[-1] == XP - 1:
                        background(first_fills[12], b + 1)
                    pe.wait_ge(m["oT_ready"], UP + b * XP + ks[-1] + 1)
                    for i in range(TB):
                        for k in ks:
                            last = nc.tensor.matmul(p_s[:, i // 2, i % 2, 0:D], oT[:, k, i * P:(i + 1) * P], wo[:, k, :],
                                                    start=(k == 0), stop=(k == XP - 1))
                        if ks[-1] == XP - 1:
                            last.then_inc(m["y_full"], 1)
                if more:
                    background(first_fills[13], b + 1)

            for f in first_fills:
                background(f, 0)
            with pe.Fori(0, B - 1) as b:
                batch(b, True)
            batch(B - 1, False)

        @block.scalar
        def _(act):
            act.wait_ge(m["c_loaded"], C_LOADS)

            def evacuate(f, b):
                if not by_act(f):
                    return
                n = no[f]
                act.wait_ge(m["bg_full"], UP + b * NF + n + 1)
                src = p_bg[:, n % 2, :]
                if f[0] == "T":
                    i = f[1]
                    if i < 4:
                        k, t = divmod(4 * i, CT)
                        out, s = cT[:, k, t * P:t * P + S], 0
                    else:
                        k, out, s = i - 4, lT[:, i - 4, :], 1
                        act.wait_ge(m["rot_ready"], UP + b * ROPES - 2)
                        act.wait_ge(m["av_done"], UP + b * NU - PC)
                    ins = nc.scalar.activation(out, src, ACT.Identity, bias=b_in[:, s, k:k + 1], scale=g_in[:, s, k:k + 1])
                elif f[0] == "KV":
                    _, p, i = f
                    act.wait_ge(m["rot_ready"], UP + b * ROPES + 2 * (p - 1))
                    act.wait_ge(m["av_done"], UP + b * NU + (p - 1) * PC)
                    ins = nc.scalar.activation(kv[:, p % 2, 2 * i:2 * i + 2, :], src.rearrange("p (t n) -> p t n", t=2), ACT.Copy)
                elif f[0] == "Q":
                    h = f[1]
                    act.wait_ge(m["s_full"], UP + b * NU + (h // 2 - 1) * PC)
                    ins = nc.scalar.activation(qT[:, h // 2 % 2, h % 2, 0, :], src, ACT.Copy)
                    ins.then_inc(m["bg_act"], 1)
                    return
                else:
                    _, h, q = f
                    act.wait_ge(m["s_full"], UP + b * NU + (h // 2 - 1) * PC + (q + 1) * (PC // 2))
                    ins = nc.scalar.activation(kT[:, h % 2, q * S:(q + 1) * S], src, ACT.Copy)
                ins.then_inc(m["bg_act"], 1)

            def k_high(r, b):
                p, q = divmod(r, 2)
                act.wait_ge(m["kr_ready"], UP + b * ROPES + r + 1)
                act.wait_ge(m["bg_full"], UP + b * NF + (no[("KT", 2 * p - 1, q)] + 1 if p > 0 else FIRST_T))
                t = slice(4 * q, 4 * q + 4)
                nc.scalar.activation(stk[:, t, :, 0:XD].bitcast(F32R), t1[:, :, :, :], ACT.Copy).then_inc(m["khi_ready"], 1)

            def context_high(b):
                act.wait_ge(m["bg_act"], UP + b * NA + act_by[3])
                act.wait_ge(m["bg_dve"], UP + b * NV + dve_by[3])
                nc.scalar.activation(cT_hi[:, :, :], cT, ACT.Copy).then_inc(m["c_high"], 1)

            def pair_out(k, b):
                act.wait_ge(m["av_done"], UP + b * NU + (k + 1) * PC)
                if k == 0:
                    act.wait_ge(m["y_full"], UP + b * TB)
                nc.scalar.activation(oT[:, k, :], p_o[:, :], ACT.Copy).then_inc(m["o_out"], 1)

            def batch(b, more):
                for u in range(NU + 2):
                    if u < NU:
                        p, c = divmod(u - 4, PC)
                        act.wait_ge(m["s_full"], UP + b * NU + u + 1)
                        act.wait_ge(m["av_done"], UP + b * NU + u - 3)
                        act.wait_ge(m["added"], UP + (b * XP + p) * (PC - 1) + max(c, 1))
                        nc.scalar.activation(ex[:, u % 4, :, :], p_s[:, u % 2, :, :], ACT.Exp, scale=XD ** -0.5).then_inc(m["exp_ready"], 1)
                    if u % PC == 1 and u > PC:
                        pair_out(u // PC - 1, b)
                    for f in slot_fills.get(u, []):
                        evacuate(f, b)
                    if more:
                        for f in next_fills.get(u, []):
                            evacuate(f, b + 1)
                        if u == LAST + 3:
                            context_high(b + 1)
                    p, v = divmod(u, PC)
                    if p + 1 < XP and v in K_HIGH_AT:
                        k_high(2 * (p + 1) + K_HIGH_AT.index(v), b)
                if more:
                    k_high(0, b + 1)
                    k_high(1, b + 1)
                    for f in first_fills[12:14]:
                        evacuate(f, b + 1)

            for f in first_fills[0:6]:
                evacuate(f, 0)
            context_high(0)
            for f in first_fills[6:12]:
                evacuate(f, 0)
            k_high(0, 0)
            k_high(1, 0)
            for f in first_fills[12:14]:
                evacuate(f, 0)
            with act.Fori(0, B - 1) as b:
                batch(b, True)
            batch(B - 1, False)

        @block.vector
        def _(dve):
            ch = Chain(dve, m["dve_steps"])
            LO, HI = float(np.exp(np.float32(-CLIP))), float(np.exp(np.float32(CLIP)))

            def evacuate(f, b):
                if not by_dve(f):
                    return
                n = no[f]
                dve.wait_ge(m["bg_full"], UP + b * NF + n + 1)
                src = p_bg[:, n % 2, :]
                if f[0] == "T":
                    i = f[1]
                    if i < 4:
                        k, t = divmod(4 * i, CT)
                        out, s = cT[:, k, t * P:t * P + S], 0
                    else:
                        k, out, s = i - 4, lT[:, i - 4, :], 1
                        dve.wait_ge(m["av_done"], UP + b * NU - PC)
                    ins = nc.vector.tensor_scalar(out, src, g_in[:, s, k:k + 1], b_in[:, s, k:k + 1], ALU.mult, ALU.add)
                else:
                    h = f[1]
                    dve.wait_ge(m["bg_act"], UP + b * NA + act_by[n])
                    ins = nc.vector.tensor_tensor(qT[:, h // 2 % 2, h % 2, 1, :], src, as32(qT[:, h // 2 % 2, h % 2, 0, :]), ALU.subtract)
                ins.then_inc(m["bg_dve"], 1)

            def rotate(r, b):
                p, q = divmod(r, 2)
                dve.wait_ge(m["bg_act"], UP + b * NA + act_by[no[("KV", p, 2 * q + 1)]])
                dve.wait_ge(m["stk_ready"], UP + b * ROPES + r)
                t = slice(4 * q, 4 * q + 4)
                k4 = kv[:, p % 2, t, 0:P].rearrange("p t (h d) -> p t h d", d=XD)
                nc.vector.tensor_tensor(t1[:, :, :, :], k4, c2[:, t, :].unsqueeze(2).broadcast_to([P, 4, 2, XD]), ALU.mult)
                nc.vector.tensor_tensor(t2[:, :, :, :], k4, s2[:, t, :].unsqueeze(2).broadcast_to([P, 4, 2, XD]), ALU.mult)\
                    .then_inc(m["rot_ready"], 1)

            def recip(k, j, b):
                cols = slice(j * (S // 2), (j + 1) * (S // 2))
                dve.wait_ge(m["sum_full"], UP + b * XP + k + 1)
                dve.wait_ge(m["oT_ready"], UP + b * XP + k)
                nc.vector.reciprocal(rcp[:, cols], p_sum[:, cols]).then_inc(m["sum_used"], 1)

            def divide(k, b):
                dve.wait_ge(m["sum_used"], UP + b * 2 * XP + 2 * k + 2)
                dve.wait_ge(m["o_out"], UP + b * XP + k + 1)
                nc.vector.tensor_tensor(oT[:, k, :], oT[:, k, :], rcp[:, :], ALU.mult).then_inc(m["oT_ready"], 1)

            def latents(b):
                return [flat(tile_of(X, b * TB + i)) for i in range(TB)]

            def stats(n, b, first=False):
                nc.vector.memset(tmp[:, 0:1], 0.0)
                if n == 0 and not first:
                    dve.wait_ge(m["cx_loaded"], b * 16)
                for i in range(4 * n, 4 * n + 4):
                    last = nc.vector.bn_stats(st[:, i, :], cx[:, i, :] if i < CT else latents(b)[i - CT])
                ch.step(last)

            def stats_done():
                n = CT + TB
                nc.vector.memset(tmp[:, 0:1], 0.0)
                for i in range(n):
                    last = nc.vector.bn_aggr(mv[:, i, :], st[:, i, :])
                ch.step(last)
                ch.step(nc.vector.tensor_scalar_add(mv[:, 0:n, 1], mv[:, 0:n, 1], 1e-5))
                rsqrt_guess(nc, ch, rstd[:, 0:n], mv[:, 0:n, 1], tmp[:, 0:n])

            def stats_root(steps):
                n = CT + TB
                rsqrt_newton(nc, ch, rstd[:, 0:n], mv[:, 0:n, 1], tmp[:, 0:n], steps)

            def normalise(tiles, b):
                for i in tiles:
                    x = cx[:, i, :] if i < CT else latents(b)[i - CT]
                    out = x if i < CT else ln[:, i - CT, :]
                    last = nc.vector.tensor_scalar(out, x, mv[:, i, 0:1], rstd[:, i:i + 1], ALU.subtract, ALU.mult)
                return last

            def split_high(b):
                dve.wait_ge(m["bg_act"], UP + b * NA + act_by[5])
                dve.wait_ge(m["bg_dve"], UP + b * NV + dve_by[5])
                dve.wait_ge(m["bg_full"], UP + b * NF + 6)
                ch.step(nc.vector.tensor_copy(lT_hi[:, :, :], lT))

            def split_low(b):
                nc.vector.tensor_tensor(lT_lo[:, :, :], lT, as32(lT_hi[:, :, :]), ALU.subtract).then_inc(m["cx_used"], 1)
                dve.wait_ge(m["c_high"], UP + b + 1)
                nc.vector.tensor_tensor(cT_lo[:, :, :], cT, as32(cT_hi[:, :, :]), ALU.subtract).then_inc(m["xs_ready"], 1)

            STEPS = 3 + 2 + RSQRT_STEPS + 1

            def add_bias(t0, t1):
                ch.step(nc.vector.tensor_tensor(X[:, t0:t1, :], X[:, t0:t1, :], bo[:, :].unsqueeze(1).broadcast_to([P, t1 - t0, D]), ALU.add))

            def out_stats(t0, t1):
                layer_norm_stats(nc, ch, [X[:, t, :] for t in range(t0, t1)], st, mv, rstd, tmp, 1e-5)

            def out_norm(t0, t1):
                for t in range(t0, t1):
                    last = nc.vector.tensor_scalar(X[:, t, :], X[:, t, :], mv[:, t - t0, 0:1], rstd[:, t - t0:t - t0 + 1], ALU.subtract, ALU.mult)
                ch.step(last)

            def batch(b, more):
                DONE = NT - TB
                for u in range(NU + 2):
                    p, c = divmod(u, PC)
                    if u < NU:
                        dve.wait_ge(m["exp_ready"], UP + b * NU + u + 1)
                        e = ex[:, u % 4, :, :]
                        nc.vector.tensor_scalar(e, e, LO, HI, ALU.max, ALU.min).then_inc(m["clipped"], 1)
                        dve.wait_ge(m["clipped"], UP + b * NU + u + 1)
                        if c >= 1:
                            if c == 1:
                                dve.wait_ge(m["sum_full"], UP + b * XP + p)
                                first = ex[:, (u - 1) % 4, :, :]
                            else:
                                dve.wait_ge(m["added"], UP + (b * XP + p) * (PC - 1) + c - 1)
                                first = acc[:, :, :]
                            nc.vector.tensor_tensor(acc[:, :, :], first, e, ALU.add).then_inc(m["added"], 1)
                    for f in slot_fills.get(u, []):
                        evacuate(f, b)
                    p, v = divmod(u, PC)
                    if v in (1, 2) and 1 <= p < XP:
                        recip(p - 1, v - 1, b)
                    if v == 3 and 1 <= p < XP:
                        divide(p - 1, b)
                    if p + 1 < XP and v in ROTATE_AT:
                        rotate(2 * (p + 1) + ROTATE_AT.index(v), b)
                    if more:
                        if LAST - 8 <= u < LAST - 5:
                            stats(u - LAST + 8, b + 1)
                        if u == LAST - 5:
                            stats_done()
                        if LAST - 4 <= u < LAST - 1:
                            stats_root(2 if u == LAST - 4 else 1)
                        if u in (LAST - 2, LAST - 1):
                            half = (u - LAST + 2) * CT // 2
                            normalise(range(half, half + CT // 2), b + 1)
                        if u == LAST:
                            dve.wait_ge(m["stk_ready"], UP + (b + 1) * ROPES)
                            normalise(range(CT, CT + TB), b + 1).then_inc(m["normed"], 1)
                        for f in next_fills.get(u, []):
                            evacuate(f, b + 1)
                        if u == LAST + 3:
                            split_high(b + 1)
                        if u == LAST + 4:
                            split_low(b + 1)
                        if u == LAST + 9:
                            rotate(0, b + 1)
                    else:
                        if u == LAST + 1:
                            add_bias(0, DONE)
                        if u == LAST + 3:
                            out_stats(0, DONE)
                        if u == LAST + 5:
                            out_norm(0, DONE)
                recip(XP - 1, 0, b)
                recip(XP - 1, 1, b)
                divide(XP - 1, b)
                if more:
                    rotate(1, b + 1)
                    for f in first_fills[12:14]:
                        evacuate(f, b + 1)
                for i, x in enumerate(latents(b)):
                    dve.wait_ge(m["y_full"], UP + b * TB + i + 1)
                    last = nc.vector.tensor_tensor(x, p_s[:, i // 2, i % 2, 0:D], x, ALU.add)
                last.then_inc(m["y_added"], 1)
                dve.wait_ge(m["y_added"], UP + b + 1)

            ch.start(0)
            for n in range(3):
                stats(n, 0, first=True)
            stats_done()
            stats_root(4)
            normalise(range(CT + TB), 0).then_inc(m["normed"], 1)
            dve.wait_ge(m["c_loaded"], C_LOADS)
            for f in first_fills[0:6]:
                evacuate(f, 0)
            split_high(0)
            split_low(0)
            ch.step(nc.vector.tensor_scalar(s2[:, :, 32:64], s2[:, :, 32:64], -1.0, None, ALU.mult))
            rotate(0, 0)
            rotate(1, 0)
            for f in first_fills[10:14]:
                evacuate(f, 0)
            assert ch.n == STEPS + 1, (ch.n, STEPS)
            with dve.Fori(0, B - 1) as b:
                ch.start(1 + (b + 1) * STEPS)
                batch(b, True)
                assert ch.n == STEPS, (ch.n, STEPS)
            ch.start(1 + B * STEPS)
            batch(B - 1, False)
            add_bias(NT - TB, NT)
            out_stats(NT - TB, NT)
            out_norm(NT - TB, NT)


LH, LD = 16, 16
LAT = 128
LP = LH // 2
LG = LH // 4
MASKED = -1e30
KEPT = TB * (TB + 1) // 2 * P
FIRST = [i * (i + 1) // 2 * P for i in range(TB)]
NB_P = 4
LAG = NB_P - 1
NB_S = 5


LA_SEMS = ("w_high", "w_split", "u_split", "dve_steps", "pool_steps", "xn_ready", "xs_ready", "tp_full", "tp_free_act", "tp_free_dve",
           "cs_ready", "proj_full", "proj_out", "v_ready", "stacked", "s_full", "max_ready", "exp_ready", "inverted",
           "normed_pool", "normed_dve", "av_done", "o_free", "y_full", "y_added")
LA_DMA_SEMS = ("loaded", "x2_stored")


def latent_attention(nc, sems, X, ident, x2_dram, g_dram, w_q, w_dkv, w_uk, w_uv, w_o):
    with ExitStack() as ctx:
        sc = Scope(nc, ctx, "la", sems)
        w_hi = sc.sb("w_hi", [P, KD, D + LAT], F32R)
        w_lo = sc.sb("w_lo", [P, KD, D + LAT], F32R)
        u_hi = sc.sb("u_hi", [P, 2 * D], F32R)
        u_lo = sc.sb("u_lo", [P, 2 * D], F32R)
        wo = sc.sb("wo", [P, LG, D])
        g_in = sc.sb("g_in", [P, KD])
        st = sc.sb("st", [P, NT, 6])
        mv = sc.sb("mv", [P, NT, 2])
        rstd = sc.sb("rstd", [P, NT])
        tmp = sc.sb("tmp", [P, NT])
        xn = sc.sb("xn", [P, TB, D])
        xT = sc.sb("xT", [P, KD, S])
        xh = sc.sb("xh", [P, KD, S], F32R)
        xl = sc.sb("xl", [P, KD, S], F32R)
        cT = xT[:, 0, :]
        ch_ = sc.sb("ch", [P, S], F32R)
        cl_ = sc.sb("cl", [P, S], F32R)
        q = sc.sb("q", [P, TB, D])
        k = sc.sb("k", [P, TB, D])
        v_next = xn
        v = sc.sb("v", [P, TB, LH, 32])
        big = sc.sb("big", [P, 2 * TB * LP * P])
        kst = big[:, 0:TB * LP * P].rearrange("p (i a n) -> p i a n", i=TB, a=LP)
        qst = big[:, TB * LP * P:2 * TB * LP * P].rearrange("p (i a n) -> p i a n", i=TB, a=LP)
        kT = sc.sb("kT", [P, LP, S], F32R)
        qT = sc.sb("qT", [P, LH, S], F32R)
        nmx = sc.sb("nmx", [P, LH, TB])
        rs = sc.sb("rs", [P, LH, TB])
        ri = sc.sb("ri", [P, LH, TB])
        prob = sc.sb("prob", [P, NB_P, KEPT])
        pT0 = sc.sb("pT0", [P, 4, 3, S])
        w_st = flat(pT0[:, 0, :, :])[:, 0:KD * (D + LAT)].rearrange("p (k n) -> p k n", k=KD)
        u_st = pT0[:, 1, 0, :]
        pT = [big[:, 0:4 * 3 * S].rearrange("p (h t n) -> p h t n", h=4, t=3), pT0[:, :, :, :]]
        oT = sc.sb("oT", [P, LG, S])
        ident_b = sc.sb("ident_b", [P, P], BF16)
        mask_b = sc.sb("mask_b", [P, P], BF16)
        p_tp = sc.ps("p_tp", [P, 2, S])
        p_s = sc.ps("p_s", [P, NB_S, S])
        p_o = sc.ps("p_o", [P, S])

        m = {n: sc.sem(n) for n in LA_SEMS} | {n: sc.dma_sem(n) for n in LA_DMA_SEMS}

        BANKS = [[(3, 0)], [(2, P), (0, 0)], [(1, 0)]]
        PROJ = [("C", 0), ("Q", 0), ("Q", 1)] + [("KV", i) for i in range(TB)]
        NPJ = len(PROJ)
        proj_at = dict(zip(PROJ, (3, 5, 6, 7, 9, 11, 13)))
        T_AT, SPLIT_AT = 1, 2

        def bank_users(more):
            users = []
            for s in range(LH):
                users += [("S", s, n) for n in range(3)]
                users += [f for f in PROJ if more and proj_at[f] == s]
            return users

        USERS = {more: bank_users(more) for more in (False, True)}
        BANK = {more: {f: i % NB_S for i, f in enumerate(USERS[more])} for more in (False, True)}
        BANK["first"] = {f: i % NB_S for i, f in enumerate(PROJ)}
        assert len(USERS[True]) % NB_S == 0

        turned_rows = [("T", kk) for kk in range(KD)]
        turned_stacks = [("ST", a) for a in range(2 * LP)]

        def fills(more):
            items = []
            for s in range(LH + LAG):
                if s >= LAG:
                    items += [("P", s - LAG, n) for n in range(3)]
                if more and s == T_AT:
                    items += turned_rows
            return Fills(items + (turned_stacks if more else []))

        first, steady, final = Fills(turned_rows + turned_stacks), fills(True), fills(False)

        def counts(b, more):
            p = steady if more else final
            return p, first.count + b * steady.count, first.act[-1] + b * steady.act[-1], first.dve[-1] + b * steady.dve[-1]

        START = (first, 0, 0, 0)
        W_LOADS = 16 * 5
        LOADS = W_LOADS + 16 * 4
        TURN = {0: (0, 0), 1: (1, P), 3: (1, 0), 2: (2, 2 * P)}

        block = ctx.enter_context(nc.Block())

        @block.sync
        def _(sp):
            sp.dma_start(w_st[:, :, 0:D], w_q.rearrange("(k p) n -> p k n", p=P)).then_inc(m["loaded"], 16)
            sp.dma_start(w_st[:, :, D:D + LAT], w_dkv.rearrange("(k p) n -> p k n", p=P)).then_inc(m["loaded"], 16)
            sp.dma_start(u_st[:, 0:D], w_uk).then_inc(m["loaded"], 16)
            sp.dma_start(u_st[:, D:2 * D], w_uv).then_inc(m["loaded"], 16)
            with nc.allow_non_contiguous_dma("small vector"):
                sp.dma_start(g_in[:, :], g_dram.rearrange("(k p) -> p k", p=P)).then_inc(m["loaded"], 16)
            sp.dma_start(x2_dram, X[:, :, :]).then_inc(m["x2_stored"], 16)
            sp.wait_ge(m["pool_steps"], UP + 1)
            sp.wait_ge(m["loaded"], W_LOADS)
            rows = w_o.rearrange("(g a p) n -> a p g n", a=4, p=LD)
            for a in range(4):
                sp.dma_start(wo[32 * a:32 * a + LD, :, :], rows[a]).then_inc(m["loaded"], 16)

        @block.gpsimd
        def _(pool):
            nc.gpsimd.memset(wo[:, :, :], 0.0).then_inc(m["pool_steps"], 1)
            pool.wait_ge(m["w_high"], UP + 1)
            nc.gpsimd.tensor_tensor(u_lo[:, :], u_st, as32(u_hi[:, :]), ALU.subtract).then_inc(m["u_split"], 1)
            nc.gpsimd.memset(v[:, :, :, :], 0.0).then_inc(m["pool_steps"], 1)
            nc.gpsimd.memset(as32(qT[:, :, :]), 0.0).then_inc(m["pool_steps"], 1)
            nc.gpsimd.memset(mask_b[:, :], 0.0).then_inc(m["pool_steps"], 1)
            nc.gpsimd.memset(ident_b[:, :], 0.0).then_inc(m["pool_steps"], 1)
            pool.wait_ge(m["pool_steps"], UP + 5)
            nc.gpsimd.affine_select(out=mask_b[:, :], in_=mask_b[:, :], compare_op=ALU.is_ge, fill=MASKED, base=0,
                                    pattern=[[-1, P]], channel_multiplier=1).then_inc(m["pool_steps"], 1)
            nc.gpsimd.affine_select(out=ident_b[:, :], in_=ident_b[:, :], compare_op=ALU.not_equal, fill=1.0, base=0,
                                    pattern=[[-1, P]], channel_multiplier=1).then_inc(m["pool_steps"], 1)
            with pool.Fori(0, B) as b:
                for h in range(LH):
                    pool.wait_ge(m["exp_ready"], UP + b * 3 * LH + 3 * h + 3)
                    pool.wait_ge(m["inverted"], UP + b * LH + h + 1)
                    for i in range(TB - 2, TB):
                        pr = prob[:, h % NB_P, FIRST[i]:FIRST[i] + (i + 1) * P]
                        last = nc.gpsimd.tensor_tensor(pr, pr, ri[:, h, i:i + 1].broadcast_to([P, (i + 1) * P]), ALU.mult)
                    last.then_inc(m["normed_pool"], 1)

        @block.tensor
        def _(pe):
            def fill(c, f):
                plan, _, act0, dve0 = c
                n = plan.no[f]
                pe.wait_ge(m["tp_free_act"], UP + act0 + plan.act[max(n - 1, 0)])
                pe.wait_ge(m["tp_free_dve"], UP + dve0 + plan.dve[max(n - 1, 0)])
                return p_tp[:, n % 2, :]

            def emptied(c, f):
                plan, _, act0, dve0 = c
                n = plan.no[f]
                pe.wait_ge(m["tp_free_act"], UP + act0 + plan.act[n + 1])
                pe.wait_ge(m["tp_free_dve"], UP + dve0 + plan.dve[n + 1])

            def turn_rows(c, f, b):
                if f[1] == 0:
                    pe.wait_ge(m["xn_ready"], UP + b + 1)
                bank = fill(c, f)
                for i in range(TB):
                    last = nc.tensor.transpose(bank[:, i * P:(i + 1) * P], xn[:, i, f[1] * P:(f[1] + 1) * P], ident[:, :])
                last.then_inc(m["tp_full"], 1)

            def turn_stack(c, f, b):
                if f[1] % LP == 0:
                    pe.wait_ge(m["stacked"], UP + 2 * b + f[1] // LP + 1)
                bank = fill(c, f)
                src = kst if f[1] < LP else qst
                for i in range(TB):
                    last = nc.tensor.transpose(bank[:, i * P:(i + 1) * P], src[:, i, f[1] % LP, :], ident[:, :])
                last.then_inc(m["tp_full"], 1)

            def project(f, b, bank):
                out = p_s[:, bank, :]
                steps = [(x, w, kk) for x, w in ((xh, w_hi), (xh, w_lo), (xl, w_hi)) for kk in range(KD)]
                if f[0] == "C":
                    pe.wait_ge(m["xs_ready"], UP + b + 1)
                    for n, (x, w, kk) in enumerate(steps):
                        last = nc.tensor.matmul(out, w[:, kk, D:D + LAT], x[:, kk, :], start=(n == 0), stop=(n == len(steps) - 1))
                elif f[0] == "Q":
                    for j in range(2):
                        i = 2 * f[1] + j
                        for n, (x, w, kk) in enumerate(steps):
                            last = nc.tensor.matmul(out[:, j * D:(j + 1) * D], x[:, kk, i * P:(i + 1) * P], w[:, kk, 0:D],
                                                    start=(n == 0), stop=(n == len(steps) - 1))
                else:
                    if f[1] == 0:
                        pe.wait_ge(m["cs_ready"], UP + b + 1)
                    i = f[1]
                    for n, (x, w) in enumerate(((ch_, u_hi), (ch_, u_lo), (cl_, u_hi))):
                        last = nc.tensor.matmul(out, x[:, i * P:(i + 1) * P], w[:, :], start=(n == 0), stop=(n == 2))
                last.then_inc(m["proj_full"], 1)

            def attention(b, more):
                c = counts(b, more)
                users = USERS[more]

                def take(f):
                    n = users.index(f)
                    if n >= NB_S:
                        before = users[n - NB_S]
                        if before[0] == "S":
                            pe.wait_ge(m["exp_ready"], UP + b * 3 * LH + 3 * before[1] + before[2] + 1)
                        else:
                            pe.wait_ge(m["proj_out"], UP + (b + 1) * NPJ + PROJ.index(before) + 1)
                    elif n == 0:
                        pe.wait_ge(m["y_added"], UP + b)
                    return BANK[more][f]

                def scores(h, n):
                    bank = take(("S", h, n))
                    for i, c0 in BANKS[n]:
                        nk = (i + 1) * P
                        nc.tensor.matmul(p_s[:, bank, c0:c0 + nk], qT[:, h, i * P:(i + 1) * P], kT[:, h // 2, 0:nk], start=True, stop=False)
                        last = nc.tensor.matmul(p_s[:, bank, c0 + nk - P:c0 + nk], ident_b[:, :], mask_b[:, :], start=False, stop=True)
                    last.then_inc(m["s_full"], 1)

                def turn(h, n):
                    pe.wait_ge(m["normed_pool"], UP + b * LH + h + 1)
                    pe.wait_ge(m["normed_dve"], UP + b * LH + h + 1)
                    bank = fill(c, ("P", h, n))
                    for j, (nn, c0) in TURN.items():
                        if nn == n:
                            for i in range(j, TB):
                                col = c0 + (i - j) * P
                                last = nc.tensor.transpose(bank[:, col:col + P], prob[:, h % NB_P, FIRST[i] + j * P:FIRST[i] + (j + 1) * P], ident[:, :])
                    last.then_inc(m["tp_full"], 1)

                def values(g, j):
                    if j == 0:
                        emptied(c, ("P", 4 * g + 3, 2))
                        pe.wait_ge(m["o_free"], UP + b * LG + g)
                        pe.wait_ge(m["v_ready"], UP + b + 1)
                    n, c0 = TURN[j]
                    w = (TB - j) * P
                    for a in range(4):
                        last = nc.tensor.matmul(p_o[32 * a:32 * a + 32, j * P:S], v[:, j, 4 * g + a, :], pT[g % 2][:, a, n, c0:c0 + w],
                                                start=(j == 0), stop=(j == TB - 1))
                    if j == TB - 1:
                        last.then_inc(m["av_done"], 1)

                pe.wait_ge(m["pool_steps"], UP + 7)
                for s in range(LH + LAG):
                    for n in range(3):
                        if s < LH:
                            scores(s, n)
                        if s >= LAG:
                            turn(s - LAG, n)
                    if more:
                        if s == T_AT:
                            for f in turned_rows:
                                turn_rows(c, f, b + 1)
                        for f in PROJ:
                            if proj_at[f] == s:
                                project(f, b + 1, take(f))
                    if s >= LAG + 4:
                        values((s - LAG) // 4 - 1, (s - LAG) % 4)
                for j in range(TB):
                    values(LG - 1, j)
                pe.wait_ge(m["o_free"], UP + (b + 1) * LG)
                pe.wait_ge(m["exp_ready"], UP + (b + 1) * 3 * LH)
                pe.wait_ge(m["loaded"], LOADS)
                for i in range(TB):
                    for g in range(LG):
                        last = nc.tensor.matmul(p_s[:, i // 2, (i % 2) * D:(i % 2 + 1) * D], oT[:, g, i * P:(i + 1) * P], wo[:, g, :],
                                                start=(g == 0), stop=(g == LG - 1))
                    if i == TB - 1:
                        last.then_inc(m["y_full"], 1)
                    if more:
                        for f in turned_stacks[i * len(turned_stacks) // TB:(i + 1) * len(turned_stacks) // TB]:
                            turn_stack(c, f, b + 1)
                if more:
                    emptied(c, turned_stacks[-1])

            for f in turned_rows:
                turn_rows(START, f, 0)
            pe.wait_ge(m["w_split"], UP + 1)
            for n, f in enumerate(PROJ):
                if f == ("KV", 0):
                    pe.wait_ge(m["u_split"], UP + 1)
                if n >= NB_S:
                    pe.wait_ge(m["proj_out"], UP + n - NB_S + 1)
                project(f, 0, BANK["first"][f])
            for f in turned_stacks:
                turn_stack(START, f, 0)
            emptied(START, turned_stacks[-1])
            with pe.Fori(0, B - 1) as b:
                attention(b, True)
            attention(B - 1, False)

        @block.scalar
        def _(act):
            def stack_out(c, f):
                plan, fills0, _, _ = c
                if plan.by_act(f):
                    act.wait_ge(m["tp_full"], UP + fills0 + plan.no[f] + 1)
                    if f[1] < LP:
                        last = nc.scalar.activation(kT[:, f[1], :], p_tp[:, 0, :], ACT.Copy)
                    else:
                        h = 2 * (f[1] - LP)
                        nc.scalar.activation(qT[0:64, h, :], p_tp[0:64, 0, :], ACT.Copy)
                        last = nc.scalar.activation(qT[64:P, h + 1, :], p_tp[64:P, 0, :], ACT.Copy)
                    last.then_inc(m["tp_free_act"], 1)

            def rows_out(c, b):
                plan, fills0, _, _ = c
                act.wait_ge(m["tp_full"], UP + fills0 + plan.no[("T", 0)] + 1)
                nc.scalar.activation(xT[:, 0, :], p_tp[:, 0, :], ACT.Identity, scale=g_in[:, 0:1]).then_inc(m["tp_free_act"], 1)

            def projected(f, b, bank):
                act.wait_ge(m["proj_full"], UP + b * NPJ + PROJ.index(f) + 1)
                src = p_s[:, bank, :]
                if f[0] == "C":
                    ins = nc.scalar.activation(cT, src, ACT.Copy)
                elif f[0] == "Q":
                    act.wait_ge(m["stacked"], UP + 2 * b)
                    ins = nc.scalar.activation(q[:, 2 * f[1]:2 * f[1] + 2, :], src.rearrange("p (a d) -> p a d", a=2), ACT.Copy, scale=LD ** -0.5)
                else:
                    act.wait_ge(m["v_ready"], UP + b)
                    nc.scalar.activation(k[:, f[1], :], src[:, 0:D], ACT.Copy)
                    ins = nc.scalar.activation(v_next[:, f[1], :], src[:, D:2 * D], ACT.Copy)
                ins.then_inc(m["proj_out"], 1)

            def attention(b, more):
                c = counts(b, more)
                plan, fills0, _, _ = c

                def turned(h, n):
                    if plan.by_act(("P", h, n)):
                        act.wait_ge(m["tp_full"], UP + fills0 + plan.no[("P", h, n)] + 1)
                        act.wait_ge(m["av_done"], UP + b * LG + h // 4 - 1)
                        c0 = 2 * P if n == 2 else 0
                        nc.scalar.activation(pT[h // 4 % 2][:, h % 4, n, c0:S], p_tp[:, 0, c0:S], ACT.Copy).then_inc(m["tp_free_act"], 1)

                for s in range(LH + LAG):
                    if s < LH and s >= NB_P:
                        act.wait_ge(m["tp_full"], UP + fills0 + plan.no[("P", s - NB_P, 2)] + 1)
                    for n, tiles in enumerate(BANKS):
                        if s < LH:
                            act.wait_ge(m["max_ready"], UP + b * 3 * LH + 3 * s + n + 1)
                            for i, c0 in tiles:
                                nk = (i + 1) * P
                                last = nc.scalar.activation(prob[:, s % NB_P, FIRST[i]:FIRST[i] + nk], p_s[:, BANK[more][("S", s, n)], c0:c0 + nk],
                                                            ACT.Exp, bias=nmx[:, s, i:i + 1], accum_out=rs[:, s, i:i + 1])
                            last.then_inc(m["exp_ready"], 1)
                        if s >= LAG:
                            turned(s - LAG, n)
                    if s == 0:
                        act.wait_ge(m["proj_out"], UP + (b + 1) * NPJ)
                        nc.scalar.activation(v[:, :, :, 0:LD], v_next[:, :, :].rearrange("p i (h d) -> p i h d", d=LD), ACT.Copy)\
                            .then_inc(m["v_ready"], 1)
                    if more:
                        if s == T_AT:
                            rows_out(c, b + 1)
                        for f in PROJ:
                            if proj_at[f] == s:
                                projected(f, b + 1, BANK[True][f])
                    if s >= LAG + 8 and (s - LAG) % 4 == 0:
                        g = (s - LAG) // 4 - 2
                        act.wait_ge(m["av_done"], UP + b * LG + g + 1)
                        nc.scalar.activation(oT[:, g, :], p_o[:, :], ACT.Copy).then_inc(m["o_free"], 1)
                for g in range(LG - 2, LG):
                    act.wait_ge(m["av_done"], UP + b * LG + g + 1)
                    nc.scalar.activation(oT[:, g, :], p_o[:, :], ACT.Copy).then_inc(m["o_free"], 1)
                if more:
                    for f in turned_stacks:
                        stack_out(c, f)

            act.wait_ge(m["loaded"], W_LOADS)
            nc.scalar.activation(w_hi[:, :, :], w_st, ACT.Copy)
            nc.scalar.activation(u_hi[:, :], u_st, ACT.Copy).then_inc(m["w_high"], 1)
            rows_out(START, 0)
            for f in PROJ:
                projected(f, 0, BANK["first"][f])
            act.wait_ge(m["pool_steps"], UP + 7)
            for f in turned_stacks:
                stack_out(START, f)
            with act.Fori(0, B - 1) as b:
                attention(b, True)
            attention(B - 1, False)

        @block.vector
        def _(dve):
            ch = Chain(dve, m["dve_steps"])

            def rms(t0, t1):
                n = t1 - t0
                row_stats(nc, ch, [X[:, t, :] for t in range(t0, t1)], st, mv, tmp)
                ch.step(nc.vector.tensor_tensor(tmp[:, 0:n], mv[:, 0:n, 0], mv[:, 0:n, 0], ALU.mult))
                ch.step(nc.vector.scalar_tensor_tensor(mv[:, 0:n, 1], mv[:, 0:n, 1], 1e-6, tmp[:, 0:n], ALU.add, ALU.add))
                newton_rsqrt(nc, ch, rstd[:, t0:t1], mv[:, 0:n, 1], tmp[:, 0:n], None)

            def rows(b):
                dve.wait_ge(m["v_ready"], UP + b)
                for i in range(TB):
                    last = nc.vector.tensor_scalar(xn[:, i, :], flat(tile_of(X, b * TB + i)), rstd[:, bass.ds(b * TB + i, 1)], None, ALU.mult)
                last.then_inc(m["xn_ready"], 1)

            def rows_out(c):
                plan, fills0, _, _ = c
                dve.wait_ge(m["tp_full"], UP + fills0 + plan.no[("T", 1)] + 1)
                nc.vector.tensor_scalar(xT[:, 1, :], p_tp[:, 1, :], g_in[:, 1:2], None, ALU.mult).then_inc(m["tp_free_dve"], 1)

            def split_rows(c):
                plan, _, act0, dve0 = c
                n = plan.no[("T", KD - 1)] + 1
                dve.wait_ge(m["tp_free_act"], UP + act0 + plan.act[n])
                dve.wait_ge(m["tp_free_dve"], UP + dve0 + plan.dve[n])
                ch.step(nc.vector.tensor_copy(xh[:, :, :], xT[:, :, :]))
                nc.vector.tensor_tensor(xl[:, :, :], xT[:, :, :], as32(xh[:, :, :]), ALU.subtract).then_inc(m["xs_ready"], 1)

            def split_latents(b):
                dve.wait_ge(m["proj_out"], UP + b * NPJ + 1)
                ch.step(nc.vector.tensor_copy(ch_[:, :], cT))
                nc.vector.tensor_tensor(cl_[:, :], cT, as32(ch_[:, :]), ALU.subtract).then_inc(m["cs_ready"], 1)

            def stack_out(c, f):
                plan, fills0, _, _ = c
                if not plan.by_act(f):
                    dve.wait_ge(m["tp_full"], UP + fills0 + plan.no[f] + 1)
                    if f[1] < LP:
                        last = nc.vector.tensor_copy(kT[:, f[1], :], p_tp[:, 1, :])
                    else:
                        h = 2 * (f[1] - LP)
                        nc.vector.tensor_copy(qT[0:64, h, :], p_tp[0:64, 1, :])
                        last = nc.vector.tensor_copy(qT[64:P, h + 1, :], p_tp[64:P, 1, :])
                    last.then_inc(m["tp_free_dve"], 1)

            def stack(c, b):
                dve.wait_ge(m["proj_out"], UP + (b + 1) * NPJ)
                dve.wait_ge(m["av_done"], UP + b * LG - 1)
                for src, dst, first_high, second_high, lows in ((k, kst, 0, 1, (2, 3)), (q, qst, 0, 2, (1, 3))):
                    parts = dst.rearrange("p i a (e r d) -> p (i a e) r d", e=2, r=4)
                    whole = src[:, :, :].rearrange("p i (h d) -> p (i h) d", d=LD)
                    ch.step(nc.vector.tensor_copy(parts[:, :, first_high, :].bitcast(F32R), whole))
                    nc.vector.tensor_copy(parts[:, :, second_high, :], parts[:, :, first_high, :])
                    for r in lows:
                        last = nc.vector.tensor_tensor(parts[:, :, r, :], whole, parts[:, :, first_high, :], ALU.subtract)
                    last.then_inc(m["stacked"], 1)
                for f in turned_stacks:
                    stack_out(c, f)

            def attention(b, more):
                c = counts(b, more)
                plan, fills0, _, _ = c

                def norm(h):
                    dve.wait_ge(m["exp_ready"], UP + b * 3 * LH + 3 * h + 3)
                    nc.vector.reciprocal(ri[:, h, :], rs[:, h, :]).then_inc(m["inverted"], 1)
                    dve.wait_ge(m["inverted"], UP + b * LH + h + 1)
                    for i in range(TB - 2):
                        pr = prob[:, h % NB_P, FIRST[i]:FIRST[i] + (i + 1) * P]
                        last = nc.vector.tensor_scalar(pr, pr, ri[:, h, i:i + 1], None, ALU.mult)
                    last.then_inc(m["normed_dve"], 1)

                def turned(h, n):
                    if not plan.by_act(("P", h, n)):
                        dve.wait_ge(m["tp_full"], UP + fills0 + plan.no[("P", h, n)] + 1)
                        dve.wait_ge(m["av_done"], UP + b * LG + h // 4 - 1)
                        c0 = 2 * P if n == 2 else 0
                        nc.vector.tensor_copy(pT[h // 4 % 2][:, h % 4, n, c0:S], p_tp[:, 1, c0:S]).then_inc(m["tp_free_dve"], 1)

                for s in range(LH + LAG):
                    for n, tiles in enumerate(BANKS):
                        if s < LH:
                            dve.wait_ge(m["s_full"], UP + b * 3 * LH + 3 * s + n + 1)
                            for i, c0 in tiles:
                                nk = (i + 1) * P
                                last = nc.vector.tensor_reduce(nmx[:, s, i:i + 1], p_s[:, BANK[more][("S", s, n)], c0:c0 + nk], AX.X, ALU.max,
                                                               negate=True)
                            last.then_inc(m["max_ready"], 1)
                        if s >= LAG:
                            turned(s - LAG, n)
                    if 1 <= s <= LH:
                        norm(s - 1)
                    if more:
                        if s == T_AT:
                            rows(b + 1)
                            rows_out(c)
                        if s == SPLIT_AT:
                            split_rows(c)
                        if s == proj_at[("C", 0)] + 1:
                            split_latents(b + 1)
                if more:
                    stack(c, b + 1)
                dve.wait_ge(m["y_full"], UP + b + 1)
                dve.wait_ge(m["x2_stored"], 16)
                for i in range(TB):
                    x = flat(tile_of(X, b * TB + i))
                    last = nc.vector.tensor_tensor(x, p_s[:, i // 2, (i % 2) * D:(i % 2 + 1) * D], x, ALU.add)
                last.then_inc(m["y_added"], 1)
                dve.wait_ge(m["y_added"], UP + b + 1)

            ch.start(0)
            rms(0, TB)
            before = ch.n
            rows(0)
            dve.wait_ge(m["loaded"], W_LOADS)
            rows_out(START)
            split_rows(START)
            dve.wait_ge(m["w_high"], UP + 1)
            nc.vector.tensor_tensor(w_lo[:, :, :], w_st, as32(w_hi[:, :, :]), ALU.subtract).then_inc(m["w_split"], 1)
            start_extra = ch.n
            rms(TB, NT)
            start_extra = ch.n - start_extra
            split_latents(0)
            dve.wait_ge(m["pool_steps"], UP + 7)
            stack(START, 0)
            first_steps, loop_steps = ch.n, ch.n - before - start_extra
            with dve.Fori(0, B - 1) as b:
                ch.start(first_steps + b * loop_steps)
                attention(b, True)
                assert ch.n == loop_steps, (ch.n, loop_steps)
            attention(B - 1, False)


NE, EH = 8, 512
EC = EH // P
NB = NT // TB


ME_SEMS = ("dve_steps", "iota_ready", "xn_ready", "tp_full", "tp_free", "ts_ready", "lg_full", "diff_ready",
           "ediff_ready", "comb_ready", "x2_added", "combT_full", "combT_ready", "w_split", "h_full", "silu_ready", "h_ready",
           "y_full", "y_added", "final")
ME_DMA_SEMS = ("loaded", "comb_stored", "stored", "x2_loaded", "w_loaded")


def experts(nc, sems, X, ident, x2_dram, g_dram, gate_w, w1, w2, comb_dram, out):
    with ExitStack() as ctx:
        sc = Scope(nc, ctx, "me", sems)
        T = NT * P
        g_in = sc.sb("g_in", [P, KD])
        gate = sc.sb("gate", [P, KD, NE])
        st = sc.sb("st", [P, NT, 6])
        mv = sc.sb("mv", [P, NT, 2])
        rstd = sc.sb("rstd", [P, NT])
        tmp = sc.sb("tmp", [P, NT])
        t_hi = sc.sb("t_hi", [P, KD, T], F32R)
        t_lo = sc.sb("t_lo", [P, KD, T], F32R)
        lg = sc.sb("lg", [P, NT, NE])
        mx = sc.sb("mx", [P, NT, NE])
        ix = sc.sb("ix", [P, NT, NE], mybir.dt.uint32)
        top = sc.sb("top", [P, NT, 2])
        gt = sc.sb("gt", [P, 3, NT])
        num = sc.sb("num", [P, NE])
        oh = sc.sb("oh", [P, 2, NT, NE])
        comb = sc.sb("comb", [P, NT, NE])
        combT = sc.sb("combT", [P, P])
        w_st = sc.sb("w_st", [P, 2, KD * EH])
        w_hi = sc.sb("w_hi", [P, 2, 2, KD * EH], F32R)
        w_lo = sc.sb("w_lo", [P, 2, 2, KD * EH], F32R)
        cb = sc.sb("cb", [P, 2, T])
        sg = sc.sb("sg", [P, 2, S])
        h_hi = sc.sb("h_hi", [P, 2, EC, S], F32R)
        h_lo = sc.sb("h_lo", [P, 2, EC, S], F32R)
        xn = cb[:, :, :].rearrange("p a (t d) -> p (a t) d", d=D)
        tT0 = sc.sb("tT0", [P, KD, S])
        tT = [tT0, sg]
        x2 = sc.sb("x2", [P, NT, D])
        p_h = sc.ps("p_h", [P, 4, S])
        p_y = sc.ps("p_y", [P, 2, 2, S])

        m = {n: sc.sem(n) for n in ME_SEMS} | {n: sc.dma_sem(n) for n in ME_DMA_SEMS}
        w_loaded = m["w_loaded"]
        cb_loaded = [sc.dma_sem(f"cb_loaded{i}") for i in range(2)]
        NC = NB * EC

        block = ctx.enter_context(nc.Block())

        @block.sync
        def _(sp):
            with nc.allow_non_contiguous_dma("small vectors"):
                sp.dma_start(g_in[:, :], g_dram.rearrange("(k p) -> p k", p=P)).then_inc(m["loaded"], 16)
                sp.dma_start(gate[:, :, :], gate_w.rearrange("(k p) n -> p k n", p=P)).then_inc(m["loaded"], 16)
            sp.dma_start(x2[:, :, :], x2_dram).then_inc(m["x2_loaded"], 16)
            sp.wait_ge(m["combT_ready"], UP + 1)
            sp.dma_start(comb_dram.rearrange("e (t n) -> t e n", n=P), combT[:, :]).then_inc(m["comb_stored"], 16)
            sp.wait_ge(m["comb_stored"], 16)
            with sp.Fori(0, NE // 2) as ep:
                for j in range(2):
                    sp.wait_ge(m["h_ready"], UP + ep * 2 * NC - (1 - j) * NC)
                    sp.dma_start(cb[:, j, :], comb_dram[bass.ds(2 * ep + j, 1), :].broadcast_to([P, T])).then_inc(cb_loaded[j], 16)
            sp.wait_ge(m["final"], UP + 1)
            sp.dma_start(out.rearrange("b (i p) d -> p (b i) d", p=P), X[:, 0:NT, :]).then_inc(m["stored"], 16)
            sp.wait_ge(m["stored"], 16)

        @block.gpsimd
        def _(pool):
            nc.gpsimd.iota(num[:, :], [[1, NE]], base=0, channel_multiplier=0, allow_small_or_imprecise_dtypes=True).then_inc(m["iota_ready"], 1)
            with pool.Fori(0, NE) as e:
                pool.wait_ge(m["w_split"], UP + e)
                pool.dma_start(w_st[:, 0, :].rearrange("p (k n) -> p k n", k=KD),
                               w1[bass.ds(e, 1), :, :].rearrange("e (k p) n -> p (e k) n", p=P)).then_inc(w_loaded, 16)
                pool.dma_start(w_st[:, 1, :].rearrange("p (k n) -> p k n", k=EC),
                               w2[bass.ds(e, 1), :, :].rearrange("e (k p) n -> p (e k) n", p=P)).then_inc(w_loaded, 16)

        @block.tensor
        def _(pe):
            pe.wait_ge(m["loaded"], 32)
            def turn(nb):
                pe.wait_ge(m["xn_ready"], UP + nb + 1)
                for k in range(KD):
                    if nb > 1:
                        pe.wait_ge(m["tp_free"], UP + KD * (nb - 2) + k + 1)
                    for i in range(TB):
                        last = nc.tensor.transpose(p_y[:, nb % 2, k, i * P:(i + 1) * P], xn[:, nb * TB + i, k * P:(k + 1) * P], ident[:, :])
                    last.then_inc(m["tp_full"], 1)

            def logits(nb):
                pe.wait_ge(m["tp_free"], UP + KD * (nb + 1))
                for i in range(TB):
                    t = nb * TB + i
                    for k in range(KD):
                        last = nc.tensor.matmul(p_h[:, 2, t * NE:(t + 1) * NE], tT[nb % 2][:, k, i * P:(i + 1) * P], gate[:, k, :],
                                                start=(k == 0), stop=(k == KD - 1))
                last.then_inc(m["lg_full"], 1)

            turn(0)
            for nb in range(NB):
                if nb + 1 < NB:
                    turn(nb + 1)
                logits(nb)
            pe.wait_ge(m["comb_ready"], UP + 1)
            nc.tensor.transpose(p_h[:, 3, 0:P], comb[:, :, :].rearrange("p t e -> p (t e)"), ident[:, :]).then_inc(m["combT_full"], 1)
            pe.wait_ge(m["combT_ready"], UP + 1)
            pe.wait_ge(m["ts_ready"], UP + NB)

            def weights(j):
                return [w[:, j, 0, :].rearrange("p (k n) -> p k n", k=KD) for w in (w_hi, w_lo)], \
                       [w[:, j, 1, :].rearrange("p (k n) -> p k n", k=EC) for w in (w_hi, w_lo)]

            def hidden(ep, j, nb, c):
                (w1h, w1l), _ = weights(j)
                r = nb * EC + c
                pe.wait_ge(m["silu_ready"], UP + ep * 2 * NC + j * NC + r - 3)
                steps = [(w, x, k) for w, x in ((w1h, t_hi), (w1l, t_hi), (w1h, t_lo)) for k in range(KD)]
                for n, (w, x, k) in enumerate(steps):
                    last = nc.tensor.matmul(p_h[:, r % 4, :], w[:, k, c * P:(c + 1) * P], x[:, k, nb * S:(nb + 1) * S],
                                            start=(n == 0), stop=(n == len(steps) - 1))
                last.then_inc(m["h_full"], 1)

            def back(ep, j, nb):
                _, (w2h, w2l) = weights(j)
                blocks = ep * 2 * NB + j * NB + nb
                pe.wait_ge(m["h_ready"], UP + blocks * EC + EC)
                pe.wait_ge(m["y_added"], UP + blocks - 1)
                for i in range(TB):
                    steps = [(x, w, c) for c in range(EC) for x, w in ((h_hi, w2h), (h_hi, w2l), (h_lo, w2h))]
                    for n, (x, w, c) in enumerate(steps):
                        last = nc.tensor.matmul(p_y[:, nb % 2, i // 2, (i % 2) * D:(i % 2 + 1) * D], x[:, nb % 2, c, i * P:(i + 1) * P],
                                                w[:, c, :], start=(n == 0), stop=(n == len(steps) - 1))
                last.then_inc(m["y_full"], 1)

            def pair(ep, first):
                for n in range(2 * NB):
                    j, nb = divmod(n, NB)
                    if nb == 0:
                        pe.wait_ge(m["w_split"], UP + 2 * ep + j + 1)
                    for c in range(EC):
                        hidden(ep, j, nb, c)
                    if n > 0:
                        back(ep, *divmod(n - 1, NB))
                    elif not first:
                        back(ep - 1, 1, NB - 1)

            pair(0, True)
            with pe.Fori(1, NE // 2) as ep:
                pair(ep, False)
            back(NE // 2 - 1, 1, NB - 1)

        @block.scalar
        def _(act):
            act.wait_ge(m["loaded"], 32)
            for nb in range(NB):
                if nb > 1:
                    act.wait_ge(m["lg_full"], UP + nb - 1)
                    act.wait_ge(m["ts_ready"], UP + nb - 1)
                for k in range(KD):
                    act.wait_ge(m["tp_full"], UP + KD * nb + k + 1)
                    nc.scalar.activation(tT[nb % 2][:, k, :], p_y[:, nb % 2, k, :], ACT.Identity, scale=g_in[:, k:k + 1]).then_inc(m["tp_free"], 1)
            act.wait_ge(m["diff_ready"], UP + 1)
            nc.scalar.activation(gt[:, 2, :], gt[:, 1, :], ACT.Exp).then_inc(m["ediff_ready"], 1)
            act.wait_ge(m["combT_full"], UP + 1)
            nc.scalar.activation(combT[:, :], p_h[:, 3, 0:P], ACT.Copy).then_inc(m["combT_ready"], 1)
            with act.Fori(0, NE // 2) as ep:
                for r in range(2 * NC):
                    act.wait_ge(m["h_full"], UP + ep * 2 * NC + r + 1)
                    act.wait_ge(m["h_ready"], UP + ep * 2 * NC + r - 1)
                    nc.scalar.activation(sg[:, r % 2, :], p_h[:, r % 4, :], ACT.Silu).then_inc(m["silu_ready"], 1)

        @block.vector
        def _(dve):
            ch = Chain(dve, m["dve_steps"])
            xs = [X[:, t, :] for t in range(NT)]
            row_stats(nc, ch, xs, st, mv, tmp)
            ch.step(nc.vector.tensor_tensor(tmp[:, :], mv[:, :, 0], mv[:, :, 0], ALU.mult))
            ch.step(nc.vector.scalar_tensor_tensor(mv[:, :, 1], mv[:, :, 1], 1e-6, tmp[:, :], ALU.add, ALU.add))
            newton_rsqrt(nc, ch, rstd[:, :], mv[:, :, 1], tmp[:, :], None)
            for t in range(NT):
                last = nc.vector.tensor_scalar(xn[:, t, :], xs[t], rstd[:, t:t + 1], None, ALU.mult)
                if t % TB == TB - 1:
                    last.then_inc(m["xn_ready"], 1)
            for nb in range(NB):
                dve.wait_ge(m["tp_free"], UP + KD * (nb + 1))
                c = slice(nb * S, (nb + 1) * S)
                ch.step(nc.vector.tensor_copy(t_hi[:, :, c], tT[nb % 2][:, :, :]))
                nc.vector.tensor_tensor(t_lo[:, :, c], tT[nb % 2][:, :, :], as32(t_hi[:, :, c]), ALU.subtract).then_inc(m["ts_ready"], 1)
            dve.wait_ge(m["x2_loaded"], 16)
            dve.wait_ge(m["iota_ready"], UP + 1)
            dve.wait_ge(m["lg_full"], UP + NB)
            ch.step(nc.vector.tensor_copy(lg[:, :, :], p_h[:, 2, 0:NT * NE].rearrange("p (t e) -> p t e", e=NE)))
            for t in range(NT):
                last = nc.vector.max(mx[:, t, :], lg[:, t, :])
            ch.step(last)
            for t in range(NT):
                last = nc.vector.max_index(ix[:, t, :], mx[:, t, :], lg[:, t, :])
            nc.vector.tensor_tensor(gt[:, 1, :], mx[:, :, 1], mx[:, :, 0], ALU.subtract).then_inc(m["diff_ready"], 1)
            ch.step(nc.vector.memset(tmp[:, :], 0.0))
            ch.step(nc.vector.tensor_copy(top[:, :, :], ix[:, :, 0:2]))
            dve.wait_ge(m["ediff_ready"], UP + 1)
            ch.step(nc.vector.tensor_scalar_add(tmp[:, :], gt[:, 2, :], 1.0))
            ch.step(nc.vector.reciprocal(gt[:, 0, :], tmp[:, :]))
            nc.vector.tensor_tensor(gt[:, 1, :], gt[:, 2, :], gt[:, 0, :], ALU.mult)
            for j in range(2):
                last = nc.vector.tensor_tensor(oh[:, j, :, :], num[:, :].unsqueeze(1).broadcast_to([P, NT, NE]),
                                               top[:, :, j:j + 1].broadcast_to([P, NT, NE]), ALU.is_equal)
            ch.step(last)
            for j in range(2):
                last = nc.vector.tensor_tensor(oh[:, j, :, :], oh[:, j, :, :], gt[:, j, :].unsqueeze(2).broadcast_to([P, NT, NE]), ALU.mult)
            ch.step(last)
            nc.vector.tensor_tensor(comb[:, :, :], oh[:, 0, :, :], oh[:, 1, :, :], ALU.add).then_inc(m["comb_ready"], 1)
            def split_weights(e, ep, j):
                dve.wait_ge(w_loaded, 32 * (e + 1))
                dve.wait_ge(m["y_full"], UP + ep * 2 * NB - (1 - j) * NB)
                ch.step(nc.vector.tensor_copy(w_hi[:, j, :, :], w_st[:, :, :]))
                nc.vector.tensor_tensor(w_lo[:, j, :, :], w_st[:, :, :], as32(w_hi[:, j, :, :]), ALU.subtract).then_inc(m["w_split"], 1)

            def add(ep, j, nb):
                dve.wait_ge(m["y_full"], UP + ep * 2 * NB + j * NB + nb + 1)
                xb = X[:, nb * TB:(nb + 1) * TB, :]
                nc.vector.tensor_tensor(xb, p_y[:, nb % 2, :, :].rearrange("p a (c d) -> p (a c) d", d=D), xb, ALU.add).then_inc(m["y_added"], 1)

            def pair(ep, first, more):
                for j in range(2):
                    dve.wait_ge(cb_loaded[j], 16 * ep + 16)
                    for nb in range(NB):
                        for c in range(EC):
                            r = j * NC + nb * EC + c
                            dve.wait_ge(m["silu_ready"], UP + ep * 2 * NC + r + 1)
                            s = sg[:, r % 2, :]
                            ch.step(nc.vector.tensor_tensor(s, s, cb[:, j, nb * S:(nb + 1) * S], ALU.mult))
                            dve.wait_ge(m["y_full"], UP + ep * 2 * NB + j * NB + nb - 1)
                            ch.step(nc.vector.tensor_copy(h_hi[:, nb % 2, c, :], s))
                            nc.vector.tensor_tensor(h_lo[:, nb % 2, c, :], s, as32(h_hi[:, nb % 2, c, :]), ALU.subtract).then_inc(m["h_ready"], 1)
                            dve.wait_ge(m["h_ready"], UP + ep * 2 * NC + r + 1)
                        if nb > 0:
                            add(ep, j, nb - 1)
                        elif j > 0:
                            add(ep, j - 1, NB - 1)
                        elif not first:
                            add(ep - 1, 1, NB - 1)
                        if nb == 1 and (j == 0 or more):
                            split_weights(2 * ep + j + 1, ep + j, 1 - j)

            split_weights(0, 0, 0)
            nc.vector.tensor_tensor(X[:, :, :], X[:, :, :], x2[:, :, :], ALU.add).then_inc(m["x2_added"], 1)
            dve.wait_ge(m["x2_added"], UP + 1)
            START = ch.n
            pair(0, True, True)
            STEPS = ch.n - START
            with dve.Fori(1, NE // 2 - 1) as ep:
                ch.start(START + ep * STEPS)
                pair(ep, False, True)
                assert ch.n == STEPS, (ch.n, STEPS)
            ch.start(START + (NE // 2 - 1) * STEPS)
            pair(NE // 2 - 1, False, False)
            add(NE // 2 - 1, 1, NB - 1)
            dve.wait_ge(m["y_added"], UP + NE * NB)
            layer_norm_stats(nc, ch, xs, st, mv, rstd, tmp, 1e-5)
            for t in range(NT):
                last = nc.vector.tensor_scalar(xs[t], xs[t], mv[:, t, 0:1], rstd[:, t:t + 1], ALU.subtract, ALU.mult)
            last.then_inc(m["final"], 1)


def program(nc, x, w, out, until=9):
    with ExitStack() as ctx:
        X = ctx.enter_context(nc.sbuf_tensor("X", [P, NT, D], F32))
        ident = ctx.enter_context(nc.sbuf_tensor("ident", [P, P], F32))
        id_ready = ctx.enter_context(nc.semaphore("id_ready"))
        stored = ctx.enter_context(nc.semaphore("stored"))
        sems = Semaphores(nc, ctx, [f"{tag}_{n}" for tag, names in (("sa", SA_SEMS), ("xa", XA_SEMS), ("la", LA_SEMS), ("me", ME_SEMS))
                                    for n in names])
        with nc.Block() as block:
            @block.sync
            def _(sp):
                sems.raise_all(sp)

            @block.gpsimd
            def _(pool):
                nc.gpsimd.memset(ident[:, :], 0.0).then_inc(id_ready, 1)
                pool.wait_ge(id_ready, 1)
                nc.gpsimd.affine_select(out=ident[:, :], in_=ident[:, :], compare_op=ALU.not_equal, fill=1.0, base=0,
                                        pattern=[[-1, P]], channel_multiplier=1).then_inc(id_ready, 1)
        shared = ctx.enter_context(ExitStack())
        weights = CrossWeights(nc, shared, sems)
        self_attention(nc, sems, X, ident, weights, w["ctx_1024"], w["L0_xattn_Wkv"], w["L0_xattn_Wq"], x, w["L0_attn_ln_gamma"], w["L0_attn_ln_beta"], w["L0_attn_q_gamma"], w["L0_attn_k_gamma"],
                       w["L0_attn_w_q"], w["L0_attn_w_k"], w["L0_attn_w_v"], w["L0_attn_w_o"], w["L0_attn_b_o"])
        if until >= 2:
            cross_attention(nc, sems, X, ident, weights, w["ctx_1024"], w["L0_xattn_cos"], w["L0_xattn_sin"], w["L0_xattn_ln_lat_g"], w["L0_xattn_ln_lat_b"],
                            w["L0_xattn_ln_ctx_g"], w["L0_xattn_ln_ctx_b"], w["L0_xattn_Wo"],
                            w["L0_xattn_bo"])
        shared.close()
        if until >= 3:
            x2_dram = nc.dram_tensor("x2", [P, NT, D], F32).ap()
            latent_attention(nc, sems, X, ident, x2_dram, w["L0_ffn_g1"], w["L0_ffn_Wq"], w["L0_ffn_Wdkv"], w["L0_ffn_Wuk"], w["L0_ffn_Wuv"], w["L0_ffn_Wo"])
        if until >= 4:
            comb_dram = nc.dram_tensor("comb", [NE, NT * P], F32).ap()
            experts(nc, sems, X, ident, x2_dram, w["L0_ffn_g2"], w["L0_ffn_gate_w"], w["L0_ffn_w1"], w["L0_ffn_w2"], comb_dram, out)
            return
        with nc.Block() as block:
            @block.sync
            def _(sp):
                sp.dma_start(out.rearrange("b (i p) d -> p (b i) d", p=P), X[:, 0:NT, :]).then_inc(stored, 16)
                sp.wait_ge(stored, 16)


_TRANSPOSED = ("L0_attn_w_q", "L0_attn_w_k", "L0_attn_w_v", "L0_attn_w_o")


def kernel(**inputs):
    import numpy as _np
    import concourse.bacc as _bacc
    from concourse import mybir as _mybir
    from concourse.bass_utils import run_bass_kernel_spmd as _run

    nc = _bacc.Bacc("TRN2", target_bir_lowering=False, num_devices=1)
    arrays, aps = {}, {}
    for name, a in inputs.items():
        a = _np.asarray(a)
        a = _np.ascontiguousarray(a.T if name in _TRANSPOSED else a)
        arrays[f"in_{name}"] = a
        aps[name] = nc.dram_tensor(f"in_{name}", a.shape, _mybir.dt.from_np(a.dtype), kind="ExternalInput").ap()
    out = nc.dram_tensor("out_x", (B, S, D), _mybir.dt.float32, kind="ExternalOutput").ap()
    program(nc, aps["x"], aps, out)
    r = _run(nc, [arrays], core_ids=[0])
    return r.results[0]["out_x"]
```
